# Optimizing a Trainium2 kernel written in Bass

```python
import numpy as np
import jax
import jax.numpy as jnp

def _softmax(x, axis=-1):
    return jax.nn.softmax(x, axis=axis)

def _gelu(x):
    return jax.nn.gelu(x, approximate=True)

def _silu(x):
    return jax.nn.silu(x)

def _sigmoid(x):
    return jax.nn.sigmoid(x)

def _layernorm(x, axis=-1, eps=1e-05):
    m = jnp.mean(x, axis=axis, keepdims=True)
    v = jnp.var(x, axis=axis, keepdims=True)
    return (x - m) / jnp.sqrt(v + eps)

def _scatter_add(tgt, idx, src, axis=0):
    return tgt.at[idx].add(src)

def _segment_sum(src, seg, n):
    return jax.ops.segment_sum(src, seg, n)
kernel_name = 'mk_gnn_ffn_d1_gnn_r8_0ea2b2'

def setup_inputs(seed: int=0):
    np.random.seed(seed)
    _w = jnp.asarray

    def _rec_inputs():
        import jax
        import jax.numpy as jnp
        _gk = jax.random.key(seed)
        x = -8.776e-05 + 1 * jax.random.normal(jax.random.fold_in(_gk, 1), (1250, 512), jnp.float32)
        src = jax.random.randint(jax.random.fold_in(_gk, 2), (20000,), 0, 1250, jnp.int32)
        dst = jax.random.randint(jax.random.fold_in(_gk, 3), (20000,), 0, 1250, jnp.int32)
        _o = jnp.argsort(dst, stable=True)
        src = src[_o]
        dst = dst[_o]
        edge_attr_128 = 0.000283511 + 1.00007 * jax.random.normal(jax.random.fold_in(_gk, 11), (20000, 128), jnp.float32)
        return (x, src, dst, edge_attr_128)
    x, src, dst, edge_attr_128 = _rec_inputs()

    def _L0_gnn_setup():
        import jax, jax.numpy as jnp
        import numpy as np
        N, E = (1250, 18750)
        HD, ED = (512, 128)
        BN_EPS = 1e-05
        key = jax.random.key(seed)
        ks = jax.random.split(key, 16)
        s = 0.02
        return {'h': jax.random.normal(ks[0], (N, HD), jnp.float32), 'edge_index': jax.random.randint(ks[1], (2, E), 0, N, jnp.int32), 'edge_attr': jax.random.normal(ks[2], (E, ED), jnp.float32), 'W1': jax.random.normal(ks[3], (HD, HD + ED), jnp.float32) * s, 'b1': jnp.zeros((HD,), jnp.float32), 'W2': jax.random.normal(ks[4], (HD, HD), jnp.float32) * s, 'b2': jnp.zeros((HD,), jnp.float32), 'W_ih': jax.random.normal(ks[5], (3 * HD, HD), jnp.float32) * s, 'W_hh': jax.random.normal(ks[6], (3 * HD, HD), jnp.float32) * s, 'b_ih': jnp.zeros((3 * HD,), jnp.float32), 'b_hh': jnp.zeros((3 * HD,), jnp.float32), 'gamma': jnp.ones((HD,), jnp.float32), 'beta': jnp.zeros((HD,), jnp.float32), 'run_mean': jnp.zeros((HD,), jnp.float32), 'run_var': jnp.ones((HD,), jnp.float32)}
    _L0_gnn_all = _L0_gnn_setup()
    _L0_gnn_in = {k: v for k, v in _L0_gnn_all.items() if k in ('W1', 'b1', 'W2', 'b2', 'W_ih', 'W_hh', 'b_ih', 'b_hh', 'gamma', 'beta', 'run_mean', 'run_var')}
    del _L0_gnn_all

    def _L0_ffn_setup():
        import jax, jax.numpy as jnp
        import numpy as np
        D = 512
        H = 8
        K = 4
        HD = D // H

        def _ln(x, w, b, eps=1e-05):
            m = x.mean(-1, keepdims=True)
            v = ((x - m) ** 2).mean(-1, keepdims=True)
            return (x - m) / jnp.sqrt(v + eps) * w + b

        def _spatial_experts(xn, idx, in_w, in_b, out_w, out_b):
            W = in_w[idx]
            qkv = jnp.einsum('btd,bed->bte', xn, W) + in_b[idx][:, None, :]
            q, k, v = jnp.split(qkv, 3, axis=-1)
            B, T, _ = xn.shape
            q = q.reshape(B, T, H, HD) * HD ** (-0.5)
            k = k.reshape(B, T, H, HD)
            v = v.reshape(B, T, H, HD)
            att = jax.nn.softmax(jnp.einsum('bthd,bshd->bhts', q, k), axis=-1)
            o = jnp.einsum('bhts,bshd->bthd', att, v).reshape(B, T, D)
            return jnp.einsum('btd,bod->bto', o, out_w[idx]) + out_b[idx][:, None, :]

        def _temporal_experts(xt, idx, qw, qb, kw, kb, vw, vb, pw, pb):
            B, T, _ = xt.shape
            q = (jnp.einsum('btd,bod->bto', xt, qw[idx]) + qb[idx][:, None, :]).reshape(B, T, H, HD)
            k = (jnp.einsum('btd,bod->bto', xt, kw[idx]) + kb[idx][:, None, :]).reshape(B, T, H, HD)
            v = (jnp.einsum('btd,bod->bto', xt, vw[idx]) + vb[idx][:, None, :]).reshape(B, T, H, HD)
            logits = jnp.einsum('bthd,bshd->bhts', q, k) * HD ** (-0.5)
            causal = jnp.tril(jnp.ones((T, T), dtype=bool))
            logits = jnp.where(causal, logits, -jnp.inf)
            att = jax.nn.softmax(logits, axis=-1)
            o = jnp.einsum('bhts,bshd->bthd', att, v).reshape(B, T, D)
            o = jnp.einsum('btd,bod->bto', o, pw[idx]) + pb[idx][:, None, :]
            return xt + o

        def _cross_mha(q_in, kv_in, in_w, in_b, out_w, out_b):
            B, T, _ = q_in.shape
            S = kv_in.shape[1]
            Wq, Wk, Wv = (in_w[:D], in_w[D:2 * D], in_w[2 * D:])
            bq, bk, bv = (in_b[:D], in_b[D:2 * D], in_b[2 * D:])
            q = (q_in @ Wq.T + bq).reshape(B, T, H, HD) * HD ** (-0.5)
            k = (kv_in @ Wk.T + bk).reshape(B, S, H, HD)
            v = (kv_in @ Wv.T + bv).reshape(B, S, H, HD)
            att = jax.nn.softmax(jnp.einsum('bthd,bshd->bhts', q, k), axis=-1)
            o = jnp.einsum('bhts,bshd->bthd', att, v).reshape(B, T, D)
            return o @ out_w.T + out_b
        key = jax.random.key(seed)
        ks = iter(jax.random.split(key, 40))
        B, T = (256, 64)
        p = lambda *shape: jax.random.normal(next(ks), shape, dtype=jnp.float32) * 0.02
        inp = {'x': jax.random.normal(next(ks), (B, T, D), dtype=jnp.float32), 'router_w1': p(128, D), 'router_b1': jnp.zeros((128,), jnp.float32), 'router_w2': p(2 * K, 128), 'router_b2': jnp.zeros((2 * K,), jnp.float32), 'norm_s_w': jnp.ones((D,), jnp.float32), 'norm_s_b': jnp.zeros((D,), jnp.float32), 'norm_t_w': jnp.ones((D,), jnp.float32), 'norm_t_b': jnp.zeros((D,), jnp.float32), 'sp_in_w': p(K, 3 * D, D), 'sp_in_b': jnp.zeros((K, 3 * D), jnp.float32), 'sp_out_w': p(K, D, D), 'sp_out_b': jnp.zeros((K, D), jnp.float32), 'tq_w': p(K, D, D), 'tq_b': jnp.zeros((K, D), jnp.float32), 'tk_w': p(K, D, D), 'tk_b': jnp.zeros((K, D), jnp.float32), 'tv_w': p(K, D, D), 'tv_b': jnp.zeros((K, D), jnp.float32), 'tp_w': p(K, D, D), 'tp_b': jnp.zeros((K, D), jnp.float32), 'cross_in_w': p(3 * D, D), 'cross_in_b': jnp.zeros((3 * D,), jnp.float32), 'cross_out_w': p(D, D), 'cross_out_b': jnp.zeros((D,), jnp.float32), 'norm_mlp_w': jnp.ones((D,), jnp.float32), 'norm_mlp_b': jnp.zeros((D,), jnp.float32), 'mlp_w1': p(4 * D, D), 'mlp_b1': jnp.zeros((4 * D,), jnp.float32), 'mlp_w2': p(D, 4 * D), 'mlp_b2': jnp.zeros((D,), jnp.float32)}
        return inp
    _L0_ffn_all = _L0_ffn_setup()
    _L0_ffn_in = {k: v for k, v in _L0_ffn_all.items() if k in ('router_w1', 'router_b1', 'router_w2', 'router_b2', 'norm_s_w', 'norm_s_b', 'norm_t_w', 'norm_t_b', 'sp_in_w', 'sp_in_b', 'sp_out_w', 'sp_out_b', 'tq_w', 'tq_b', 'tk_w', 'tk_b', 'tv_w', 'tv_b', 'tp_w', 'tp_b', 'cross_in_w', 'cross_in_b', 'cross_out_w', 'cross_out_b', 'norm_mlp_w', 'norm_mlp_b', 'mlp_w1', 'mlp_b1', 'mlp_w2', 'mlp_b2')}
    del _L0_ffn_all
    return {'x': x, 'src': src, 'dst': dst, 'edge_attr_128': edge_attr_128, 'L0_gnn_W1': _L0_gnn_in['W1'], 'L0_gnn_b1': _L0_gnn_in['b1'], 'L0_gnn_W2': _L0_gnn_in['W2'], 'L0_gnn_b2': _L0_gnn_in['b2'], 'L0_gnn_W_ih': _L0_gnn_in['W_ih'], 'L0_gnn_W_hh': _L0_gnn_in['W_hh'], 'L0_gnn_b_ih': _L0_gnn_in['b_ih'], 'L0_gnn_b_hh': _L0_gnn_in['b_hh'], 'L0_gnn_gamma': _L0_gnn_in['gamma'], 'L0_gnn_beta': _L0_gnn_in['beta'], 'L0_gnn_run_mean': _L0_gnn_in['run_mean'], 'L0_gnn_run_var': _L0_gnn_in['run_var'], 'L0_ffn_router_w1': _L0_ffn_in['router_w1'], 'L0_ffn_router_b1': _L0_ffn_in['router_b1'], 'L0_ffn_router_w2': _L0_ffn_in['router_w2'], 'L0_ffn_router_b2': _L0_ffn_in['router_b2'], 'L0_ffn_norm_s_w': _L0_ffn_in['norm_s_w'], 'L0_ffn_norm_s_b': _L0_ffn_in['norm_s_b'], 'L0_ffn_norm_t_w': _L0_ffn_in['norm_t_w'], 'L0_ffn_norm_t_b': _L0_ffn_in['norm_t_b'], 'L0_ffn_sp_in_w': _L0_ffn_in['sp_in_w'], 'L0_ffn_sp_in_b': _L0_ffn_in['sp_in_b'], 'L0_ffn_sp_out_w': _L0_ffn_in['sp_out_w'], 'L0_ffn_sp_out_b': _L0_ffn_in['sp_out_b'], 'L0_ffn_tq_w': _L0_ffn_in['tq_w'], 'L0_ffn_tq_b': _L0_ffn_in['tq_b'], 'L0_ffn_tk_w': _L0_ffn_in['tk_w'], 'L0_ffn_tk_b': _L0_ffn_in['tk_b'], 'L0_ffn_tv_w': _L0_ffn_in['tv_w'], 'L0_ffn_tv_b': _L0_ffn_in['tv_b'], 'L0_ffn_tp_w': _L0_ffn_in['tp_w'], 'L0_ffn_tp_b': _L0_ffn_in['tp_b'], 'L0_ffn_cross_in_w': _L0_ffn_in['cross_in_w'], 'L0_ffn_cross_in_b': _L0_ffn_in['cross_in_b'], 'L0_ffn_cross_out_w': _L0_ffn_in['cross_out_w'], 'L0_ffn_cross_out_b': _L0_ffn_in['cross_out_b'], 'L0_ffn_norm_mlp_w': _L0_ffn_in['norm_mlp_w'], 'L0_ffn_norm_mlp_b': _L0_ffn_in['norm_mlp_b'], 'L0_ffn_mlp_w1': _L0_ffn_in['mlp_w1'], 'L0_ffn_mlp_b1': _L0_ffn_in['mlp_b1'], 'L0_ffn_mlp_w2': _L0_ffn_in['mlp_w2'], 'L0_ffn_mlp_b2': _L0_ffn_in['mlp_b2']}

def reference(x, src, dst, edge_attr_128, L0_gnn_W1, L0_gnn_b1, L0_gnn_W2, L0_gnn_b2, L0_gnn_W_ih, L0_gnn_W_hh, L0_gnn_b_ih, L0_gnn_b_hh, L0_gnn_gamma, L0_gnn_beta, L0_gnn_run_mean, L0_gnn_run_var, L0_ffn_router_w1, L0_ffn_router_b1, L0_ffn_router_w2, L0_ffn_router_b2, L0_ffn_norm_s_w, L0_ffn_norm_s_b, L0_ffn_norm_t_w, L0_ffn_norm_t_b, L0_ffn_sp_in_w, L0_ffn_sp_in_b, L0_ffn_sp_out_w, L0_ffn_sp_out_b, L0_ffn_tq_w, L0_ffn_tq_b, L0_ffn_tk_w, L0_ffn_tk_b, L0_ffn_tv_w, L0_ffn_tv_b, L0_ffn_tp_w, L0_ffn_tp_b, L0_ffn_cross_in_w, L0_ffn_cross_in_b, L0_ffn_cross_out_w, L0_ffn_cross_out_b, L0_ffn_norm_mlp_w, L0_ffn_norm_mlp_b, L0_ffn_mlp_w1, L0_ffn_mlp_b1, L0_ffn_mlp_w2, L0_ffn_mlp_b2):
    import jax
    import jax.numpy as jnp

    def _L0_gnn_ref(h, edge_index, edge_attr, W1, b1, W2, b2, W_ih, W_hh, b_ih, b_hh, gamma, beta, run_mean, run_var):
        import jax, jax.numpy as jnp
        import numpy as np
        N, E = (1250, 18750)
        HD, ED = (512, 128)
        BN_EPS = 1e-05
        src, dst = (edge_index[0], edge_index[1])
        m_in = jnp.concatenate([h[src], edge_attr], axis=1)
        m = jax.nn.relu(m_in @ W1.T + b1) @ W2.T + b2
        agg = jax.ops.segment_sum(m, dst, num_segments=h.shape[0])
        gi = agg @ W_ih.T + b_ih
        gh = h @ W_hh.T + b_hh
        i_r, i_z, i_n = jnp.split(gi, 3, axis=1)
        h_r, h_z, h_n = jnp.split(gh, 3, axis=1)
        r = jax.nn.sigmoid(i_r + h_r)
        z = jax.nn.sigmoid(i_z + h_z)
        n = jnp.tanh(i_n + r * h_n)
        h_new = (1.0 - z) * n + z * h
        bn = gamma * (h_new - run_mean) * jax.lax.rsqrt(run_var + BN_EPS) + beta
        return h + bn

    def _L0_ffn_ref(x, router_w1, router_b1, router_w2, router_b2, norm_s_w, norm_s_b, norm_t_w, norm_t_b, sp_in_w, sp_in_b, sp_out_w, sp_out_b, tq_w, tq_b, tk_w, tk_b, tv_w, tv_b, tp_w, tp_b, cross_in_w, cross_in_b, cross_out_w, cross_out_b, norm_mlp_w, norm_mlp_b, mlp_w1, mlp_b1, mlp_w2, mlp_b2):
        import jax, jax.numpy as jnp
        import numpy as np
        D = 512
        H = 8
        K = 4
        HD = D // H

        def _ln(x, w, b, eps=1e-05):
            m = x.mean(-1, keepdims=True)
            v = ((x - m) ** 2).mean(-1, keepdims=True)
            return (x - m) / jnp.sqrt(v + eps) * w + b

        def _spatial_experts(xn, idx, in_w, in_b, out_w, out_b):
            W = in_w[idx]
            qkv = jnp.einsum('btd,bed->bte', xn, W) + in_b[idx][:, None, :]
            q, k, v = jnp.split(qkv, 3, axis=-1)
            B, T, _ = xn.shape
            q = q.reshape(B, T, H, HD) * HD ** (-0.5)
            k = k.reshape(B, T, H, HD)
            v = v.reshape(B, T, H, HD)
            att = jax.nn.softmax(jnp.einsum('bthd,bshd->bhts', q, k), axis=-1)
            o = jnp.einsum('bhts,bshd->bthd', att, v).reshape(B, T, D)
            return jnp.einsum('btd,bod->bto', o, out_w[idx]) + out_b[idx][:, None, :]

        def _temporal_experts(xt, idx, qw, qb, kw, kb, vw, vb, pw, pb):
            B, T, _ = xt.shape
            q = (jnp.einsum('btd,bod->bto', xt, qw[idx]) + qb[idx][:, None, :]).reshape(B, T, H, HD)
            k = (jnp.einsum('btd,bod->bto', xt, kw[idx]) + kb[idx][:, None, :]).reshape(B, T, H, HD)
            v = (jnp.einsum('btd,bod->bto', xt, vw[idx]) + vb[idx][:, None, :]).reshape(B, T, H, HD)
            logits = jnp.einsum('bthd,bshd->bhts', q, k) * HD ** (-0.5)
            causal = jnp.tril(jnp.ones((T, T), dtype=bool))
            logits = jnp.where(causal, logits, -jnp.inf)
            att = jax.nn.softmax(logits, axis=-1)
            o = jnp.einsum('bhts,bshd->bthd', att, v).reshape(B, T, D)
            o = jnp.einsum('btd,bod->bto', o, pw[idx]) + pb[idx][:, None, :]
            return xt + o

        def _cross_mha(q_in, kv_in, in_w, in_b, out_w, out_b):
            B, T, _ = q_in.shape
            S = kv_in.shape[1]
            Wq, Wk, Wv = (in_w[:D], in_w[D:2 * D], in_w[2 * D:])
            bq, bk, bv = (in_b[:D], in_b[D:2 * D], in_b[2 * D:])
            q = (q_in @ Wq.T + bq).reshape(B, T, H, HD) * HD ** (-0.5)
            k = (kv_in @ Wk.T + bk).reshape(B, S, H, HD)
            v = (kv_in @ Wv.T + bv).reshape(B, S, H, HD)
            att = jax.nn.softmax(jnp.einsum('bthd,bshd->bhts', q, k), axis=-1)
            o = jnp.einsum('bhts,bshd->bthd', att, v).reshape(B, T, D)
            return o @ out_w.T + out_b
        pooled = x.mean(axis=1)
        h = jax.nn.gelu(pooled @ router_w1.T + router_b1, approximate=False)
        route = jax.nn.softmax(h @ router_w2.T + router_b2, axis=-1)
        idx_s = jnp.argmax(route[:, :K], axis=-1)
        idx_t = jnp.argmax(route[:, K:], axis=-1)
        xn = _ln(x, norm_s_w, norm_s_b)
        spatial_out = _spatial_experts(xn, idx_s, sp_in_w, sp_in_b, sp_out_w, sp_out_b)
        xt = _ln(x, norm_t_w, norm_t_b)
        temporal_out = _temporal_experts(xt, idx_t, tq_w, tq_b, tk_w, tk_b, tv_w, tv_b, tp_w, tp_b)
        fused = _cross_mha(spatial_out, temporal_out, cross_in_w, cross_in_b, cross_out_w, cross_out_b)
        x = x + fused
        h2 = _ln(x, norm_mlp_w, norm_mlp_b)
        x = x + (jax.nn.gelu(h2 @ mlp_w1.T + mlp_b1, approximate=False) @ mlp_w2.T + mlp_b2)
        return x
    edge_index = jnp.stack([src, dst])
    x = x + _L0_gnn_ref(_layernorm(x, axis=-1), edge_index, edge_attr_128, L0_gnn_W1, L0_gnn_b1, L0_gnn_W2, L0_gnn_b2, L0_gnn_W_ih, L0_gnn_W_hh, L0_gnn_b_ih, L0_gnn_b_hh, L0_gnn_gamma, L0_gnn_beta, L0_gnn_run_mean, L0_gnn_run_var)
    x = x + _L0_ffn_ref(_layernorm(x, axis=-1)[None], L0_ffn_router_w1, L0_ffn_router_b1, L0_ffn_router_w2, L0_ffn_router_b2, L0_ffn_norm_s_w, L0_ffn_norm_s_b, L0_ffn_norm_t_w, L0_ffn_norm_t_b, L0_ffn_sp_in_w, L0_ffn_sp_in_b, L0_ffn_sp_out_w, L0_ffn_sp_out_b, L0_ffn_tq_w, L0_ffn_tq_b, L0_ffn_tk_w, L0_ffn_tk_b, L0_ffn_tv_w, L0_ffn_tv_b, L0_ffn_tp_w, L0_ffn_tp_b, L0_ffn_cross_in_w, L0_ffn_cross_in_b, L0_ffn_cross_out_w, L0_ffn_cross_out_b, L0_ffn_norm_mlp_w, L0_ffn_norm_mlp_b, L0_ffn_mlp_w1, L0_ffn_mlp_b1, L0_ffn_mlp_w2, L0_ffn_mlp_b2)[0]
    return x

_drawn_inputs = setup_inputs


def setup_inputs(seed=0):
    import zlib

    import numpy as np

    out = dict(_drawn_inputs(seed))
    spreads = {'L0_gnn_b1': (0.0, 0.1),
     'L0_gnn_b2': (0.0, 0.1),
     'L0_gnn_b_ih': (0.0, 0.435),
     'L0_gnn_b_hh': (0.0, 0.634),
     'L0_gnn_gamma': (1.0, 0.2),
     'L0_gnn_beta': (0.0, 0.1),
     'L0_gnn_run_mean': (0.0, 0.1),
     'L0_gnn_run_var': (1.0, 0.6),
     'L0_ffn_router_b1': (0.0, 0.1),
     'L0_ffn_router_b2': (0.0, 0.792),
     'L0_ffn_norm_s_w': (1.0, 0.6),
     'L0_ffn_norm_s_b': (0.0, 0.8),
     'L0_ffn_norm_t_w': (1.0, 0.6),
     'L0_ffn_norm_t_b': (0.0, 0.8),
     'L0_ffn_sp_in_b': (0.0, 0.8),
     'L0_ffn_sp_out_b': (0.0, 0.8),
     'L0_ffn_tq_b': (0.0, 0.8),
     'L0_ffn_tk_b': (0.0, 2.0),
     'L0_ffn_tv_b': (0.0, 0.8),
     'L0_ffn_tp_b': (0.0, 0.8),
     'L0_ffn_cross_in_b': (0.0, 0.613),
     'L0_ffn_cross_out_b': (0.0, 2.0),
     'L0_ffn_norm_mlp_w': (1.0, 0.6),
     'L0_ffn_norm_mlp_b': (0.0, 2.0),
     'L0_ffn_mlp_b1': (0.0, 2.0),
     'L0_ffn_mlp_b2': (0.0, 2.0)}
    factors = {'L0_ffn_router_w1': 8.0,
     'L0_ffn_router_w2': 8.0,
     'L0_ffn_sp_in_w': 8.0,
     'L0_ffn_sp_out_w': 8.0,
     'L0_ffn_tq_w': 8.0,
     'L0_ffn_tk_w': 8.0,
     'L0_ffn_tv_w': 8.0,
     'L0_ffn_tp_w': 8.0,
     'L0_ffn_cross_in_w': 4.84,
     'L0_ffn_cross_out_w': 3.156,
     'L0_ffn_mlp_w1': 8.0,
     'L0_ffn_mlp_w2': 7.428}
    for name, (base, spread) in spreads.items():
        noise = np.random.default_rng([zlib.crc32(name.encode()), seed]).standard_normal(out[name].shape)
        drawn = base * np.exp(spread * noise) if base else spread * noise
        out[name] = jnp.asarray(drawn.astype(out[name].dtype))
    for name, factor in factors.items():
        out[name] = (out[name] * factor).astype(out[name].dtype)
    return out
```

```python
from contextlib import ExitStack

import numpy as np
import concourse.bass as bass
from concourse import mybir

F32 = mybir.dt.float32
F16 = mybir.dt.float16
I32 = mybir.dt.int32
U32 = mybir.dt.uint32
ALU = mybir.AluOpType
ACT = mybir.ActivationFunctionType
AX = mybir.AxisListType

N = 1250
E = 20000
D = 512
ED = 128
P = 125
NT = N // P
ET = E // P
GE = 4
NG = ET // GE
GW = GE * P
KD = D // 128
H = 8
HD = D // H
FF = 4 * D
CH = [(0, 500), (500, 500), (1000, 250)]
NC = len(CH)
SG = 64.0
SF = 16.0
EPS = 1e-5
QK_SCALE = HD ** -0.5
PB = 2 * P
NB = N // PB
MASKED = -60000.0
MASK_GAIN = 2048.0
PAGE = 5160
EXPERTS = 4

VEC = {}
for _name, _n in [("b_ih", 12), ("b_hh", 12), ("gamma", 4), ("beta", 4), ("mean", 4), ("var", 4),
                  ("ns_w", 4), ("ns_b", 4), ("nt_w", 4), ("nt_b", 4), ("cq_b", 4), ("ck_b", 4),
                  ("nm_w", 4), ("nm_b", 4), ("m1_b", 16), ("rb1", 1)]:
    VEC[_name] = (sum(n for _, n in VEC.values()), _n)
NV = sum(n for _, n in VEC.values())
ROW = {"b1": 0, "b2": 1, "cv": 2, "cout": 3, "m2": 4}


def program(nc, a, out):
    ctx = ExitStack()
    with ctx:
        def sb(name, shape, dt):
            return ctx.enter_context(nc.sbuf_tensor(name, shape, dt))

        def sem(name):
            return ctx.enter_context(nc.semaphore(name))

        bank = [ctx.enter_context(nc.psum_tensor(f"bank{i}", [128, 512], F32)) for i in range(8)]

        pages = sb("pages", [128, 7 * PAGE], F32)
        page = [None] + [pages[:, i * PAGE:(i + 1) * PAGE] for i in range(7)]
        wide = [pages[:, 2 * s * PAGE:2 * s * PAGE + 8 * N].bitcast(F16).rearrange("p (k n) -> p k n", k=FF // 128)
                for s in range(2)]
        slots = sb("slots", [128, 4, 2, KD, D], F16)
        stage = sb("stage", [128, 4, D], F32)
        scratch = sb("scratch", [128, 2560], F32)
        t32 = scratch[:, 0:1536].rearrange("p (c n) -> p c n", c=NC)
        rowst = scratch[:, 1536:2560].rearrange("p (c n) -> p c n", c=2)
        prob32 = scratch[:, 0:1000].rearrange("p (c n) -> p c n", c=2)
        probh = scratch[:, 1000:1750].bitcast(F16).rearrange("p (c n) -> p c n", c=3)
        probl = scratch[:, 1750:2500].bitcast(F16).rearrange("p (c n) -> p c n", c=3)
        eah = scratch[:, 0:500].bitcast(F16).rearrange("p (c n) -> p c n", c=2)
        eal = scratch[:, 500:1000].bitcast(F16).rearrange("p (c n) -> p c n", c=2)
        ident = sb("ident", [128, 128], F32)
        gain16 = sb("gain16", [128, 128], F16)
        eights = sb("eights", [NT, P], F16)
        ones32 = sb("ones32", [P, 1], F32)
        ones16 = sb("ones16", [P, 1], F16)
        blockdiag = sb("blockdiag", [NT, NT, P], F16)
        turns = sb("turns", [128, 1250], F32)
        srcs = turns[0:P, 512:512 + ET].bitcast(I32)
        dstf = turns[0:P, 672:672 + ET]
        win = turns[0:1, 832:832 + 4 * NG].bitcast(I32)     
        rw1 = turns[:, 0:512].rearrange("p (k n) -> p k n", k=KD)
        shift = turns[0:NT, :].bitcast(F16).rearrange("p (a n) -> p a n", a=2)
        node_id = sb("node_id", [P, N], F16)
        idx_ring = sb("idx_ring", [P, 2, GE], I32)
        cnt = sb("cnt", [P, NT], F32)
        vec = sb("vec", [128, NV], F32)
        vsp = sb("vsp", [128, 12], F32)
        vtp = sb("vtp", [128, 12], F32)
        rowb = sb("rowb", [P, D], F32)
        stats = sb("stats", [P, NT, 6], F32)
        mv = sb("mv", [P, NT, 2], F32)
        rstd = sb("rstd", [P, NT], F32)
        bsum = sb("bsum", [128, 12], F32)
        bns = sb("bns", [128, 2, KD], F32)
        mxs = sb("mxs", [P, 2, NT, NB], F32)
        mx = sb("mx", [P, 2, NT], F32)
        rden = sb("rden", [P, 2], F32)
        olo = sb("olo", [P, 2, HD], F32)
        osum = sb("osum", [P, 2, HD], F32)
        rs = sb("rs", [128, 8], F32)
        rw2 = sb("rw2", [128, 2 * EXPERTS], F32)
        rb2 = sb("rb2", [1, 2 * EXPERTS], F32)
        lg = sb("lg", [1, 40], F32)
        choice = sb("choice", [1, 16], U32)

        def vcol(name, i=0, n=1):
            at = VEC[name][0] + i
            return vec[:, bass.ds(at, n)]

        def rows(p):
            return page[p][0:P, 0:NT * D].rearrange("p (t d) -> p t d", t=NT)

        def cols(p):
            return page[p][:, 0:KD * N].rearrange("p (k n) -> p k n", k=KD)

        def split(p):
            return page[p][:, 0:KD * N].bitcast(F16).rearrange("p (s k n) -> p s k n", s=2, k=KD)

        def heads(p):
            return page[p][:, 0:KD * N].bitcast(F16)

        def values(p):
            return page[p][0:P, 0:NT * H * 129 // 2].bitcast(F16).rearrange(
                "p (t h c) -> p t h c", t=NT, h=H)

        def value_cols(p):
            return page[p][0:P, 0:NT * H * 129 // 2].bitcast(F16)

        def hidden(s, m, i, n0, w):
            return pages[:, 2 * s * PAGE:2 * s * PAGE + 8 * N].bitcast(F16)[:, bass.ds((4 * m + i) * N + n0, w)]

        gath = page[6][0:P, 0:8 * D].rearrange("p (s d) -> p s d", s=8)
        eas = page[6][:, 8 * D:8 * D + 1000].rearrange("p (s n) -> p s n", s=2)
        relu = page[7][0:P, 0:8 * D].bitcast(F16).rearrange("p (s l d) -> p s l d", s=8, l=2)
        esum = page[7][0:P, 8 * D:10 * D].rearrange("p (s d) -> p s d", s=2)
        onehot = page[4][0:P, 0:5000].bitcast(F16).rearrange("p (s n) -> p s n", s=8)
        cntb = page[6][0:NT, 0:N]
        cnth = page[6][0:NT, N:2 * N].bitcast(F16).rearrange("p (l n) -> p l n", l=2)
        b2f = page[6][0:NT, 2 * N:2 * N + D]
        b2h = page[6][0:NT, 2 * N + D:2 * N + 2 * D].bitcast(F16).rearrange("p (l n) -> p l n", l=2)
        mask_s = node_id[:, 0:2 * PB].rearrange("p (a n) -> p a n", a=2)
        mask_t = node_id[:, 2 * PB:4 * PB].rearrange("p (a n) -> p a n", a=2)
        grp_i = page[7][0:NG, 0:GW].bitcast(I32)
        grp_f = page[7][0:NG, GW:2 * GW]
        gw = page[7][0:NG, 1000:1032]
        gwi = page[7][0:NG, 1040:1044].bitcast(I32)
        tri = page[7][0:NG, 1100:1100 + 2 * NG].rearrange("p (a n) -> p a n", a=2)
        dsts = page[7][0:P, 1200:1200 + ET].bitcast(I32)

        proj_d = nc.dram_tensor("proj_d", (N, D), F32, kind="Internal").ap()
        x1_d = nc.dram_tensor("x1_d", (P, NT * D), F32, kind="Internal").ap()
        xl_d = nc.dram_tensor("xl_d", (P, NT * D), F32, kind="Internal").ap()
        xt_d = nc.dram_tensor("xt_d", (128, KD * N), F32, kind="Internal").ap()
        win_d = nc.dram_tensor("win_d", (NG, 4), I32, kind="Internal").ap()

        in_ld = sem("in_ld")
        x_ld = sem("x_ld")
        pool_c = sem("pool_c")
        dve_c = sem("dve_c")
        link_s = sem("link_s")
        ln_var = sem("ln_var")
        ln_sd = sem("ln_sd")
        ln_out = sem("ln_out")
        f_mm = sem("f_mm")
        f_act = sem("f_act")
        f_lo = sem("f_lo")
        t_mm = sem("t_mm")
        t_ev = sem("t_ev")
        v_hi = sem("v_hi")
        v_lo = sem("v_lo")
        p_st = [sem(f"p_st{i}") for i in range(2)]
        w_ld = [sem(f"w_ld{i}") for i in range(4)]
        w_sc = sem("w_sc")
        w_hi = sem("w_hi")
        w_split = sem("w_split")
        win_s = sem("win_s")
        win_io = sem("win_io")
        ea_ld = [sem(f"ea_ld{i}") for i in range(2)]
        ea_hi = sem("ea_hi")
        ea_lo = sem("ea_lo")
        g_ix = sem("g_ix")
        g_ld = [sem(f"g_ld{i}") for i in range(8)]
        e_mm = sem("e_mm")
        e_sum = sem("e_sum")
        e_hi = sem("e_hi")
        e_lo = sem("e_lo")
        s_mm = sem("s_mm")
        s_add = sem("s_add")
        agg_done = sem("agg_done")
        c_s = sem("c_s")
        c_mt = sem("c_mt")
        n_hr = sem("n_hr")
        n_new = sem("n_new")
        rw_ld = sem("rw_ld")
        b2_ld = sem("b2_ld")
        r_mm = sem("r_mm")
        r_act = sem("r_act")
        r_ix = sem("r_ix")
        sp_io = sem("sp_io")
        to_sum = sem("to_sum")
        xs_done = sem("xs_done")
        back = sem("back")
        eb_ld = sem("eb_ld")
        row_ld = sem("row_ld")
        dup_q = sem("dup_q")
        dup_k = sem("dup_k")
        a_mm = sem("a_mm")
        a_mx = sem("a_mx")
        m_all = sem("m_all")
        m_t = sem("m_t")
        m_sh = sem("m_sh")
        s_sc = sem("s_sc")
        s_exp = sem("s_exp")
        s_plo = sem("s_plo")
        s_pv = sem("s_pv")
        o_ev = sem("o_ev")
        o_st = sem("o_st")
        y_st = sem("y_st")

        F_TILES, T_TILES, LOWS = {}, {}, {}
        g = l = t = 0
        for name, kind, tiles, low in [
                ("hT", "F", KD * NC, 1), ("P", "T", NT, 0), ("aggT", "F", KD * NC, 1), ("M", "F", KD * NC, 1),
                ("r", "F", KD * NC, 0), ("z", "F", KD * NC, 0), ("n", "F", KD * NC, 0), ("x1", "T", NT, 0),
                ("xn", "F", KD * NC, 1), ("xt", "F", KD * NC, 1),
                ("sq", "F", KD * NC, 1), ("sk", "F", KD * NC, 1), ("sv", "T", NT, 0),
                ("soT", "F", KD * NC, 1), ("so", "F", KD * NC, 1), ("cq", "F", KD * NC, 1),
                ("tq", "F", KD * NC, 1), ("tk", "F", KD * NC, 1), ("tv", "T", NT, 0),
                ("toT", "F", KD * NC, 1), ("to", "F", KD * NC, 1),
                ("ck", "F", KD * NC, 1), ("cv", "T", NT, 0),
                ("coT", "F", KD * NC, 1), ("co", "T", NT, 0), ("h2", "F", KD * NC, 1),
                ("up0", "F", KD * NC, 1), ("up1", "F", KD * NC, 1), ("up2", "F", KD * NC, 1),
                ("up3", "F", KD * NC, 1), ("down", "T", NT, 0)]:
            if kind == "F":
                F_TILES[name] = (g, g + tiles)
                LOWS[name] = (l, l + tiles * low)
                g, l = g + tiles, l + tiles * low
            else:
                T_TILES[name] = (t, t + tiles)
                t += tiles

        def since(u, units, ring):
            return ring if u >= ring else u + units - max(v for v in range(units) if v % ring == u)

        def f_read(name):
            return F_TILES[name][1] + NC

        def f_split(name):
            return LOWS[name][1] + NC

        def t_read(name):
            return T_TILES[name][1] + 2

        UNITS = [("w1a", "w1T", None, 0, 0, KD, SG, "P"), ("w1b", "w1T", None, D, 0, 1, SG, "aggT"),
                 ("w2", "w2T", None, 0, 0, KD, SG, "M")]
        for i, stg in enumerate(("r", "z", "n")):
            UNITS += [("ih" + stg, "wihT", None, 0, i * D, KD, SG, stg),
                      ("hh" + stg, "whhT", None, 0, i * D, KD, SG, stg)]
        UNITS += [("sq", "spinT", "s", 0, 0, KD, SF, "sq"), ("sk", "spinT", "s", 0, D, KD, SF, "sk"),
                  ("sv", "spinT", "s", 0, 2 * D, KD, SF, "sv"), ("so", "spoutT", "s", 0, 0, KD, SF, "so"),
                  ("cq", "cinT", None, 0, 0, KD, SF, "cq"),
                  ("tq", "tqT", "t", 0, 0, KD, SF, "tq"), ("tk", "tkT", "t", 0, 0, KD, SF, "tk"),
                  ("tv", "tvT", "t", 0, 0, KD, SF, "tv"), ("to", "tpT", "t", 0, 0, KD, SF, "to"),
                  ("ck", "cinT", None, 0, D, KD, SF, "ck"), ("cv", "cinT", None, 0, 2 * D, KD, SF, "cv"),
                  ("co", "coutT", None, 0, 0, KD, SF, "co")]
        UNITS += [(f"up{i}", "m1T", None, 0, i * D, KD, SF, f"up{i}") for i in range(4)]
        UNITS += [(f"down{i}", "m2T", None, i * D, 0, KD, SF, "down") for i in range(4)]
        UNIT = {u[0]: i for i, u in enumerate(UNITS)}
        SLOT = {u[0]: i % 4 for i, u in enumerate(UNITS)}
        CHUNKS = [(i, k) for i, u in enumerate(UNITS) for k in range(u[5])]
        SPLIT_AT = {}
        for n, (i, k) in enumerate(CHUNKS):
            SPLIT_AT[UNITS[i][0]] = n + 1
        FIRST_AFTER_EDGES = CHUNKS.index((2, 0))

        ATT = [dict(n="s", qh=1, ql=2, k=6, v=7, o=3, causal=False),
               dict(n="t", qh=3, ql=4, k=7, v=1, o=6, causal=True),
               dict(n="c", qh=5, ql=6, k=7, v=3, o=1, causal=False)]
        u0 = b0 = a0 = h0 = 0
        for at in ATT:
            at["units"] = [(c, p) for c in range(NB) for p in range(c + 1 if at["causal"] else NB)]
            at["u0"], at["b0"], at["a0"], at["h0"] = u0, b0, a0, h0
            nu = len(at["units"])
            at["early"] = [[2 * u, 2 * u + 1] if u < 5 else ([u + 5] if u + 5 < nu else []) for u in range(nu)]
            u0, b0, a0, h0 = u0 + nu * H, b0 + NB * H, a0 + nu * H, h0 + H
        ATT_END = [dict(u=x["u0"] + len(x["units"]) * H, b=x["b0"] + NB * H, h=x["h0"] + H) for x in ATT]

        block = ctx.enter_context(nc.Block())

        @block.sync
        def _(sp):
            for s, v in ((f_act, NC), (f_lo, NC), (t_ev, 2), (ea_lo, 2), (e_mm, GE), (e_sum, GE), (e_hi, 2),
                         (e_lo, 2), (a_mx, 2), (s_mm, NT), (s_add, NT), (s_exp, 2), (s_plo, 2), (s_pv, 3), (o_ev, 2)):
                sp.sem_inc(s, v)
            sp.dma_start(vec[:], a["vec"]).then_inc(in_ld, 16)
            sp.dma_start(srcs, a["src_pt"]).then_inc(in_ld, 16)
            sp.dma_start(dsts, a["dst_pt"]).then_inc(in_ld, 16)
            sp.dma_start(grp_i, a["dst_g"]).then_inc(in_ld, 16)
            sp.dma_start(rowb[:], a["rowv"][0:1, :].to_broadcast([P, D])).then_inc(row_ld, 16)

            def load_weights(first, last, pick):
                for n in range(first, last):
                    i, k = CHUNKS[n]
                    _, name, expert, r0, c0, _, _, _ = UNITS[i]
                    if n >= 4:
                        sp.wait_ge(w_split, n - 3)
                    src = a[name]
                    if expert:
                        src = src[bass.ds(pick[expert], 1), r0 + 128 * k:r0 + 128 * k + 128, c0:c0 + D]
                        src = src.rearrange("a p n -> (a p) n")
                    else:
                        src = src[r0 + 128 * k:r0 + 128 * k + 128, c0:c0 + D]
                    sp.dma_start(stage[:, n % 4, :], src).then_inc(w_ld[n % 4], 16)

            load_weights(0, FIRST_AFTER_EDGES, {})
            sp.wait_ge(win_s, 3)
            sp.dma_start(win_d, gwi).then_inc(win_io, 16)
            sp.wait_ge(win_io, 16)
            sp.dma_start(win, win_d.rearrange("(o g) c -> o (g c)", o=1)).then_inc(win_io, 16)
            for j in range(NT):
                sp.wait_ge(t_ev, T_TILES["P"][0] + j + 1 + 2)
                sp.dma_start(proj_d[j * P:(j + 1) * P, :], rowst[0:P, j % 2, :]).then_inc(p_st[j % 2], 16)
            sp.wait_ge(f_mm, F_TILES["hT"][1])
            with sp.Fori(0, NG // 2) as i:
                for s in range(2):
                    sp.wait_ge(ea_lo, 2 * i + s + 1)
                    sp.dma_start(eas[:, s, :], a["eaT"][:, bass.ds((2 * i + s) * GW, GW)]).then_inc(ea_ld[s], 16)
            split_s = CHUNKS.index((UNIT["sq"], 0))
            ihz_at = CHUNKS.index((UNIT["ihz"], 0))
            load_weights(FIRST_AFTER_EDGES, ihz_at, {})
            sp.wait_ge(agg_done, 1)
            sp.wait_ge(f_mm, F_TILES["aggT"][1])
            sp.dma_start(b2f, a["rowv"][ROW["b2"]:ROW["b2"] + 1, :].to_broadcast([NT, D])).then_inc(b2_ld, 16)
            sp.dma_start(rw1, a["rw1T"].rearrange("(k p) n -> p k n", p=128)).then_inc(rw_ld, 16)
            sp.dma_start(rw2[:], a["rw2T"]).then_inc(rw_ld, 16)
            sp.dma_start(rb2[:], a["rb2"]).then_inc(rw_ld, 16)
            load_weights(ihz_at, split_s, {})
            sp.wait_ge(r_ix, 2)
            ps = sp.value_load(choice[0:1, 0:1], min_val=0, max_val=EXPERTS - 1)
            pt = sp.value_load(choice[0:1, 8:9], min_val=0, max_val=EXPERTS - 1)
            pick = {"s": ps, "t": pt}
            sp.dma_start(vsp[:], a["vsp"][bass.ds(ps, 1), :, :].rearrange("a p n -> (a p) n")).then_inc(eb_ld, 16)
            sp.dma_start(vtp[:], a["vtp"][bass.ds(pt, 1), :, :].rearrange("a p n -> (a p) n")).then_inc(eb_ld, 16)
            sp.wait_ge(t_ev, t_read("P"))
            sp.dma_start(rowb[:], a["svrow"][bass.ds(ps, 1), :].to_broadcast([P, D])).then_inc(row_ld, 16)
            tv_at = CHUNKS.index((UNIT["tv"], 0))
            load_weights(split_s, tv_at, pick)
            sp.wait_ge(t_ev, t_read("sv"))
            sp.dma_start(rowb[:], a["tvrow"][bass.ds(pt, 1), :].to_broadcast([P, D])).then_inc(row_ld, 16)
            cv_at = CHUNKS.index((UNIT["cv"], 0))
            load_weights(tv_at, cv_at, pick)
            sp.wait_ge(t_ev, t_read("tv"))
            sp.dma_start(rowb[:], a["rowv"][ROW["cv"]:ROW["cv"] + 1, :].to_broadcast([P, D])).then_inc(row_ld, 16)
            co_at = CHUNKS.index((UNIT["up0"], 0))
            load_weights(cv_at, co_at, pick)
            sp.wait_ge(t_ev, t_read("cv"))
            sp.dma_start(rowb[:], a["rowv"][ROW["cout"]:ROW["cout"] + 1, :].to_broadcast([P, D])).then_inc(row_ld, 16)
            load_weights(co_at, co_at + 4, pick)
            sp.wait_ge(y_st, 1)
            sp.dma_start(rowb[:], a["rowv"][ROW["m2"]:ROW["m2"] + 1, :].to_broadcast([P, D])).then_inc(row_ld, 16)
            load_weights(co_at + 4, len(CHUNKS), pick)
            for j in range(NT):
                sp.wait_ge(t_ev, T_TILES["down"][0] + j + 1 + 2)
                sp.dma_start(out[j * P:(j + 1) * P, :], rows(7)[:, j, :]).then_inc(o_st, 16)
            sp.wait_ge(o_st, 16 * NT)

        @block.gpsimd
        def _(pool):
            for j in range(NT):
                pool.dma_start(rows(1)[:, j, :], a["x"][j * P:(j + 1) * P, :]).then_inc(x_ld, 16)
            pool.memset(ident[:], 0.0).then_inc(pool_c, 1)
            pool.memset(blockdiag[:], 0.0).then_inc(pool_c, 1)
            pool.memset(tri, 1.0).then_inc(pool_c, 1)
            pool.iota(node_id[:], pattern=[[1, N]], base=0, channel_multiplier=0,
                      allow_small_or_imprecise_dtypes=True).then_inc(pool_c, 1)
            pool.wait_ge(pool_c, 4)
            pool.affine_select(out=ident[:], in_=ident[:], compare_op=ALU.not_equal, fill=1.0, base=0,
                               pattern=[[-1, 128]], channel_multiplier=1).then_inc(pool_c, 1)
            pool.affine_select(out=blockdiag[:], in_=blockdiag[:], compare_op=ALU.not_equal, fill=1.0, base=0,
                               pattern=[[-1, NT], [0, P]], channel_multiplier=1).then_inc(pool_c, 1)
            for o in range(2):
                pool.affine_select(out=tri[:, o, :], in_=tri[:, o, :], compare_op=ALU.is_ge, fill=0.0,
                                   base=-1 - o, pattern=[[1, NG]], channel_multiplier=-1).then_inc(pool_c, 1)

            def split_weights(first, last):
                for n in range(first, last):
                    i, k = CHUNKS[n]
                    scale = UNITS[i][6]
                    if k == 0 and i >= 4:
                        was = UNITS[i - 4][7]
                        if was in F_TILES:
                            pool.wait_ge(f_mm, F_TILES[was][1])
                        elif was in T_TILES:
                            pool.wait_ge(t_mm, T_TILES[was][1])
                    pool.wait_ge(w_ld[n % 4], 16 * (n // 4 + 1))
                    pool.tensor_scalar(stage[:, n % 4, :], stage[:, n % 4, :], scale, 1.0,
                                       ALU.mult, ALU.mult).then_inc(w_sc, 1)
                    pool.wait_ge(w_sc, n + 1)
                    pool.tensor_copy(slots[:, i % 4, 0, k, :], stage[:, n % 4, :]).then_inc(w_hi, 1)
                    pool.wait_ge(w_hi, n + 1)
                    pool.tensor_tensor(slots[:, i % 4, 1, k, :], stage[:, n % 4, :], slots[:, i % 4, 0, k, :],
                                       ALU.subtract).then_inc(w_split, 1)

            split_weights(0, FIRST_AFTER_EDGES)
            for s in range(2):
                pool.wait_ge(p_st[s], 16 * NT // 2)
            pool.wait_ge(in_ld, 64)
            with pool.Fori(0, NG // 2) as i:
                for s in range(2):
                    pool.wait_ge(e_sum, (2 * i + s) * GE)
                    pool.tensor_copy(idx_ring[:, s, :], srcs[:, bass.ds((2 * i + s) * GE, GE)]).then_inc(g_ix, 1)
                    pool.wait_ge(ea_hi, 2 * i + s + 1)
                    pool.wait_ge(g_ix, 2 * i + s + 1)
                    pool.tensor_tensor(eal[:, s, :], eas[:, s, :], eah[:, s, :], ALU.subtract).then_inc(ea_lo, 1)
                    for q in range(GE):
                        pool.indirect_dma_start(
                            gath[:, s * GE + q, :], None, proj_d,
                            bass.IndirectOffsetOnAxis(ap=idx_ring[:, s, q:q + 1], axis=0)).then_inc(g_ld[s * GE + q], 16)
            pool.wait_ge(e_lo, ET + 2)
            pool.memset(mask_s, 0.0).then_inc(pool_c, 1)
            pool.memset(mask_t, 0.0).then_inc(pool_c, 1)
            pool.wait_ge(pool_c, 10)
            pool.affine_select(out=mask_s, in_=mask_s, compare_op=ALU.is_ge, fill=MASKED, base=0,
                               pattern=[[-P, 2], [1, PB]], channel_multiplier=-1).then_inc(pool_c, 1)
            pool.affine_select(out=mask_t, in_=mask_t, compare_op=ALU.is_ge, fill=MASKED, base=0,
                               pattern=[[P, 2], [-1, PB]], channel_multiplier=1).then_inc(pool_c, 1)
            split_weights(FIRST_AFTER_EDGES, len(CHUNKS))

        @block.tensor
        def _(pe):
            def f_gemm(name, units, start_waits):
                for s, v in start_waits:
                    pe.wait_ge(s, v)
                for u in units:
                    pe.wait_ge(w_split, SPLIT_AT[u[0]])
                g0 = F_TILES[name][0]
                with pe.Fori(0, KD) as i:
                    for c, (n0, w) in enumerate(CH):
                        pe.wait_ge(f_act, g0 + i * NC + c + 1)
                        todo = [(u, xp, s, r, k) for u, xp in units for k in range(KD)
                                for s, r in ((0, 0), (0, 1), (1, 0))]
                        for m, (u, xp, s, r, k) in enumerate(todo):
                            mm = pe.matmul(bank[c][:, 0:w], slots[:, SLOT[u], s, k, bass.ds(i * 128, 128)],
                                           split(xp)[:, r, k, n0:n0 + w], start=(m == 0), stop=(m == len(todo) - 1))
                        mm.then_inc(f_mm, 1)

            def f_transpose(name, src, start_waits):
                for s, v in start_waits:
                    pe.wait_ge(s, v)
                g0 = F_TILES[name][0]
                for k in range(KD):
                    for c, (n0, w) in enumerate(CH):
                        pe.wait_ge(f_act, g0 + k * NC + c + 1)
                        for q in range(w // P):
                            mm = pe.transpose(bank[c][:, q * P:(q + 1) * P],
                                              rows(src)[:, n0 // P + q, k * 128:(k + 1) * 128], ident[0:P, 0:P])
                        mm.then_inc(f_mm, 1)

            def t_gemm(name, pairs, start_waits):
                for s, v in start_waits:
                    pe.wait_ge(s, v)
                t0 = T_TILES[name][0]
                with pe.Fori(0, NT // 2) as i:
                    for b in range(2):
                        pe.wait_ge(t_ev, t0 + 2 * i + b + 1)
                        todo = [(x, u, k, s, r) for x, u in pairs for k in range(KD)
                                for s, r in ((0, 0), (0, 1), (1, 0))]
                        for m, (x, u, k, s, r) in enumerate(todo):
                            mm = pe.matmul(bank[3 + b][0:P, :], x(s, k, bass.ds((2 * i + b) * P, P)),
                                           slots[:, SLOT[u], r, k, :], start=(m == 0), stop=(m == len(todo) - 1))
                        mm.then_inc(t_mm, 1)

            def of(p):
                return lambda s, k, n: split(p)[:, s, k, n]

            pe.wait_ge(pool_c, 8)
            pe.wait_ge(win_s, 1)
            pe.matmul(bank[7][0:NG, 0:1], tri[:, 0, :], gw[:, 20:21], start=True, stop=True)
            pe.matmul(bank[7][0:NG, 1:2], tri[:, 1, :], gw[:, 20:21], start=True, stop=True).then_inc(win_s, 1)

            f_transpose("hT", 6, [(ln_out, 1)])
            pe.wait_ge(w_split, SPLIT_AT["w1a"])
            t_gemm("P", [(of(3), "w1a")], [(f_lo, f_split("hT"))])

            pe.wait_ge(w_split, SPLIT_AT["w1b"])
            pe.wait_ge(f_act, f_read("hT"))
            pe.wait_ge(dve_c, 1)
            pe.wait_ge(win_io, 32)

            def group(n0, s):
                pe.wait_ge(ea_lo, n0 + 1 + 2)
                for q in range(GE):
                    pe.wait_ge(e_sum, n0 * GE + q - 1 + GE)
                    for m, (x, wt) in enumerate(((eah, 0), (eah, 1), (eal, 0))):
                        mm = pe.matmul(bank[q % 2][0:P, :], x[:, s, q * P:(q + 1) * P],
                                       slots[:, SLOT["w1b"], wt, 0, :], start=(m == 0), stop=(m == 2))
                    mm.then_inc(e_mm, 1)

            def scatter(n0, s):
                first, end, number = (pe.value_load(win[:, bass.ds(n0 * 4 + c, 1)], min_val=lo, max_val=hi)
                                      for c, lo, hi in ((0, 0, NT - 1), (1, 1, NT), (2, 0, NG * NT + NT)))
                with pe.Fori(first, end) as j:
                    pe.wait_ge(e_lo, n0 * GE + GE + 2)
                    pe.wait_ge(s_add, number + j)
                    for q in range(GE):
                        member = onehot[:, s * GE + q, bass.ds(j * P, P)]
                        pe.matmul(bank[2][0:P, :], member, relu[:, s * GE + q, 0, :], start=(q == 0), stop=False)
                        pe.matmul(bank[2][0:P, :], member, relu[:, s * GE + q, 1, :], start=False, stop=(q == GE - 1))
                    for q in range(GE):
                        mm = pe.matmul(bank[5][0:P, 0:1], onehot[:, s * GE + q, bass.ds(j * P, P)], ones16[:],
                                       start=(q == 0), stop=(q == GE - 1))
                    mm.then_inc(s_mm, 1)

            group(0, 0)
            with pe.Fori(0, NG // 2 - 1) as i:
                group(2 * i + 1, 1)
                scatter(2 * i, 0)
                group(2 * i + 2, 0)
                scatter(2 * i + 1, 1)
            group(NG - 1, 1)
            scatter(NG - 2, 0)
            scatter(NG - 1, 1)

            pe.wait_ge(agg_done, 1)
            pe.transpose(bank[7][0:NT, 0:P], cnt[:], ident[0:P, 0:P]).then_inc(c_mt, 1)
            f_transpose("aggT", 5, [])
            pe.wait_ge(f_lo, f_split("aggT"))
            pe.wait_ge(c_s, 1)
            pe.wait_ge(w_split, SPLIT_AT["w2"])
            g0 = F_TILES["M"][0]
            with pe.Fori(0, KD) as i:
                for c, (n0, w) in enumerate(CH):
                    pe.wait_ge(f_act, g0 + i * NC + c + 1)
                    for m, (s, r) in enumerate(((0, 0), (0, 1), (1, 0))):
                        pe.matmul(bank[c][:, 0:w], b2h[:, s, bass.ds(i * 128, 128)], cnth[:, r, n0:n0 + w],
                                  start=(m == 0), stop=False)
                    for k in range(KD):
                        for s, r in ((0, 0), (0, 1), (1, 0)):
                            mm = pe.matmul(bank[c][:, 0:w], slots[:, SLOT["w2"], s, k, bass.ds(i * 128, 128)],
                                           split(4)[:, r, k, n0:n0 + w], start=False, stop=(k == KD - 1 and s == 1))
                    mm.then_inc(f_mm, 1)
            for gate in "rz":
                pe.wait_ge(w_split, SPLIT_AT["hh" + gate])
                f_gemm(gate, [("ih" + gate, 5), ("hh" + gate, 3)], [(f_lo, f_split("M"))])
            pe.wait_ge(w_split, SPLIT_AT["hhn"])
            g0 = F_TILES["n"][0]
            with pe.Fori(0, KD) as i:
                for c, (n0, w) in enumerate(CH):
                    pe.wait_ge(f_act, g0 + i * NC + c + 1)
                    for b, u, xp in ((0, "ihn", 5), (5, "hhn", 3)):
                        for k in range(KD):
                            for s, r in ((0, 0), (0, 1), (1, 0)):
                                mm = pe.matmul(bank[b + c][:, 0:w], slots[:, SLOT[u], s, k, bass.ds(i * 128, 128)],
                                               split(xp)[:, r, k, n0:n0 + w], start=(k == 0 and s == 0 and r == 0),
                                               stop=(k == KD - 1 and s == 1))
                    mm.then_inc(f_mm, 1)
            pe.wait_ge(n_new, KD * NC)
            t0 = T_TILES["x1"][0]
            for j in range(NT):
                pe.wait_ge(t_ev, t0 + j + 1)
                for k in range(KD):
                    mm = pe.transpose(bank[3 + j % 2][0:P, k * 128:(k + 1) * 128], cols(2)[:, k, j * P:(j + 1) * P], ident[:])
                mm.then_inc(t_mm, 1)

            pe.wait_ge(ln_out, 2)
            for k in range(KD):
                for j in range(NT):
                    mm = pe.matmul(bank[7][:, k:k + 1], rows(2)[:, j, k * 128:(k + 1) * 128], ones32[:],
                                   start=(j == 0), stop=(j == NT - 1))
            mm.then_inc(r_mm, 1)
            pe.wait_ge(r_act, 1)
            pe.wait_ge(rw_ld, 48)
            for k in range(KD):
                mm = pe.matmul(bank[7][:, 8:9], rw1[:, k, :], rs[:, k:k + 1], start=(k == 0), stop=(k == KD - 1))
            mm.then_inc(r_mm, 1)
            pe.wait_ge(r_act, 2)
            pe.matmul(bank[7][0:1, 16:24], rs[:, 4:5], rw2[:], start=True, stop=True).then_inc(r_mm, 1)

            f_transpose("xn", 3, [(ln_out, 3)])
            f_transpose("xt", 3, [])

            def qkv(at, x):
                n = at["n"]
                pe.wait_ge(w_split, SPLIT_AT[n + "k" if n == "c" else n + "q"])
                pe.wait_ge(f_lo, f_split({"s": "xn", "t": "cq", "c": "to"}[n]))
                if n != "c":
                    f_gemm(n + "q", [(n + "q", x)], [])
                f_gemm(n + "k", [(n + "k", x)], [])
                pe.wait_ge(w_split, SPLIT_AT[n + "v"])
                t_gemm(n + "v", [(of(x), n + "v")], [])

            def attention(x):
                qh, ql, kk, vv = heads(x["qh"]), heads(x["ql"]), heads(x["k"]), value_cols(x["v"])
                mask_s_flat, mask_t_flat = node_id[:, 0:2 * PB], node_id[:, 2 * PB:4 * PB]
                units, nu = x["units"], len(x["units"])

                def col(pg, h, at, n, k=128):
                    return pg[0:k, bass.ds(h * N + at, n)]

                def val(s_tile, h, n):
                    return vv[:, bass.ds(s_tile * H * 129 + h * 129, n)]

                def maxima(h, e):
                    c, p = units[e]
                    n = x["a0"] + h * nu + e
                    b = bank[(2, 5)[e % 2]]
                    pe.wait_ge(a_mx, n - since(e, nu, 2) + 1 + 2)
                    masked = x["causal"] and c == p
                    if masked:
                        pe.matmul(b[0:P, 0:2 * PB], gain16[0:P, 0:P], mask_t_flat, start=True, stop=False,
                                  skip_group_check=True)
                    for q in range(2):
                        mm = pe.matmul(b[0:P, q * PB:(q + 1) * PB], col(qh, h, c * PB + q * P, P, HD),
                                       col(kk, h, p * PB, PB, HD), start=(q == 0 and not masked), stop=(q == 1),
                                       skip_group_check=True)
                    mm.then_inc(a_mm, 1)

                def scores(h, par, u):
                    c, p = units[u]
                    n = x["u0"] + h * nu + u
                    b = bank[u % 2]
                    pe.wait_ge(s_exp, n - since(u, nu, 2) + 1 + 2)
                    for q in range(2):
                        pe.matmul(b[0:P, q * PB:(q + 1) * PB], eights[:], shift[:, par, c * PB:(c + 1) * PB],
                                  start=(q == 0), stop=False, skip_group_check=True)
                    if x["causal"] and c == p:
                        pe.matmul(b[0:P, 0:2 * PB], gain16[0:P, 0:P], mask_s_flat, start=False, stop=False,
                                  skip_group_check=True)
                    for q in range(2):
                        for part in range(2):
                            mm = pe.matmul(b[0:P, q * PB:(q + 1) * PB], col(kk, h, p * PB + q * P, P),
                                           col((qh, ql)[part], h, c * PB, PB), start=False,
                                           stop=(q == 1 and part == 1), skip_group_check=True)
                    mm.then_inc(s_sc, 1)

                def weigh(h, u):
                    c, p = units[u]
                    n = x["u0"] + h * nu + u
                    if p == 0:
                        pe.wait_ge(o_ev, x["b0"] + NB * h + c - since(c, NB, 2) + 1 + 2)
                    pe.wait_ge(s_plo, n + 1 + 2)
                    last_p = c if x["causal"] else NB - 1
                    for q in range(2):
                        for r in range(2):
                            w = slice(q * PB + r * P, q * PB + (r + 1) * P)
                            fin = p == last_p and q == 1 and r == 1
                            o = bank[3 + c % 2][0:P, :]
                            pe.matmul(o[:, r * 129:r * 129 + 129], probh[0:P, u % 3, w], val(2 * p + q, h, 129),
                                      start=(p == 0 and q == 0 and r == 0), stop=False, skip_group_check=True)
                            mm = pe.matmul(o[:, r * 129:r * 129 + 65], probl[0:P, u % 3, w], val(2 * p + q, h, 65),
                                           start=False, stop=fin, skip_group_check=True)
                    mm.then_inc(s_pv, 1)

                def head(h, par, following):
                    if following:
                        early = x["early"]
                    else:
                        early = [[] for _ in units]
                    pe.wait_ge(m_sh, x["h0"] + h + 1)
                    for u in range(nu):
                        scores(h, par, u)
                        for e in early[u]:
                            maxima(h + 1, e)
                        if u >= 1:
                            weigh(h, u - 1)
                        if following and u == nu - 3:
                            turn(h + 1, 1 - par)
                    weigh(h, nu - 1)

                def turn(h, par):
                    pe.wait_ge(m_all, x["h0"] + h + 1)
                    pe.transpose(bank[6][0:NT, 0:P], mx[:, par, :], ident[0:P, 0:P]).then_inc(m_t, 1)

                for e in range(nu):
                    maxima(0, e)
                turn(0, 0)
                with pe.Fori(0, H // 2 - 1) as i:
                    head(2 * i, 0, True)
                    head(2 * i + 1, 1, True)
                head(H - 2, 0, True)
                head(H - 1, 1, False)

            qkv(ATT[0], 4)
            pe.wait_ge(dup_q, 16 * 4)
            pe.wait_ge(dup_k, 16 * 4)
            pe.wait_ge(v_lo, NT)
            pe.wait_ge(t_ev, t_read("sv"))
            attention(ATT[0])
            f_transpose("soT", 3, [(o_ev, ATT_END[0]["b"] + 2), (s_exp, ATT_END[0]["u"] + 2), (a_mx, ATT_END[0]["u"] + 2)])
            f_gemm("so", [("so", 4)], [(f_lo, f_split("soT")), (w_split, SPLIT_AT["so"])])
            f_gemm("cq", [("cq", 1)], [(f_lo, f_split("so")), (w_split, SPLIT_AT["cq"])])
            qkv(ATT[1], 5)
            pe.wait_ge(dup_q, 16 * 8)
            pe.wait_ge(dup_k, 16 * 8)
            pe.wait_ge(v_lo, 2 * NT)
            pe.wait_ge(pool_c, 12)
            pe.wait_ge(t_ev, t_read("tv"))
            attention(ATT[1])
            f_transpose("toT", 6, [(o_ev, ATT_END[1]["b"] + 2), (s_exp, ATT_END[1]["u"] + 2), (a_mx, ATT_END[1]["u"] + 2)])
            f_gemm("to", [("to", 5)], [(f_lo, f_split("toT")), (w_split, SPLIT_AT["to"])])
            qkv(ATT[2], 4)
            pe.wait_ge(dup_q, 16 * 12)
            pe.wait_ge(dup_k, 16 * 12)
            pe.wait_ge(v_lo, 3 * NT)
            pe.wait_ge(t_ev, t_read("cv"))
            attention(ATT[2])
            f_transpose("coT", 1, [(o_ev, ATT_END[2]["b"] + 2), (s_exp, ATT_END[2]["u"] + 2), (a_mx, ATT_END[2]["u"] + 2)])
            t_gemm("co", [(of(2), "co")], [(f_lo, f_split("coT")), (w_split, SPLIT_AT["co"])])
            f_transpose("h2", 4, [(ln_out, 4)])
            for i in range(4):
                f_gemm(f"up{i}", [(f"up{i}", 6)], [(f_lo, f_split("h2")), (w_split, SPLIT_AT[f"up{i}"])])
            t_gemm("down", [(lambda s, k, n, i=i: wide[s][:, 4 * i + k, n], f"down{i}") for i in range(4)],
                   [(f_lo, f_split("up3")), (w_split, SPLIT_AT["down3"])])

        @block.scalar
        def _(act):
            def f_tile(name, i, c, w, t_dst, hi_dst, func, scale, bias):
                g, lw = F_TILES[name][0] + i * NC + c, LOWS[name][0] + i * NC + c
                act.wait_ge(f_mm, g + 1)
                act.wait_ge(f_lo, lw + 1)
                act.activation(t_dst, bank[c][:, 0:w], func, bias=bias, scale=scale)
                act.activation(hi_dst, bank[c][:, 0:w], func, bias=bias, scale=scale).then_inc(f_act, 1)

            def f_evac(name, dst, scale, bias, func=ACT.Identity):
                with act.Fori(0, KD) as i:
                    for c, (n0, w) in enumerate(CH):
                        f_tile(name, i, c, w, t32[:, c, 0:w], dst(0, i, n0, w), func, scale, bias(i))

            def page_of(p):
                return lambda s, i, n0, w: page[p][:, 0:KD * N].bitcast(F16)[:, bass.ds(i * N + s * KD * N + n0, w)]

            def layer_norm_sd(k):
                act.wait_ge(ln_var, k)
                act.activation(rstd[:], rstd[:], ACT.Sqrt).then_inc(ln_sd, 1)

            def vecs(name):
                return lambda i: vcol(name, i)

            act.wait_ge(ln_var, 1)
            act.activation(bns[:, 0, :], bns[:, 0, :], ACT.Sqrt)
            layer_norm_sd(1)
            for k in range(KD):
                for c, (n0, w) in enumerate(CH):
                    f_tile("hT", k, c, w, cols(2)[:, k, n0:n0 + w], split(3)[:, 0, k, n0:n0 + w], ACT.Identity, 1.0, 0.0)

            def attributes(n0, s):
                act.wait_ge(ea_ld[s], 16 * ((n0 - s) // 2 + 1) if isinstance(n0, int) else n0[1])
                n0 = n0 if isinstance(n0, int) else n0[0]
                act.wait_ge(e_mm, n0 * GE)
                act.activation(eah[:, s, :], eas[:, s, :], ACT.Copy).then_inc(ea_hi, 1)

            def relus(n0, s):
                behind = act.value_load(win[:, bass.ds(n0 * 4 + 3, 1)], min_val=0, max_val=NG * NT + NT)
                act.wait_ge(s_mm, behind)
                for q in range(GE):
                    n = n0 * GE + q
                    act.wait_ge(e_sum, n + 1 + GE)
                    act.activation(relu[:, s * GE + q, 0, :], esum[:, q % 2, :], ACT.Relu).then_inc(e_hi, 1)

            act.wait_ge(win_io, 32)
            attributes(0, 0)
            with act.Fori(0, NG // 2 - 1) as i:
                attributes((2 * i + 1, 16 * (i + 1)), 1)
                relus(2 * i, 0)
                attributes((2 * i + 2, 16 * (i + 2)), 0)
                relus(2 * i + 1, 1)
            attributes(NG - 1, 1)
            relus(NG - 2, 0)
            relus(NG - 1, 1)

            f_evac("aggT", page_of(4), 1.0, lambda i: 0.0)
            f_evac("M", page_of(5), 1.0 / SG, lambda i: 0.0)
            for gate, p, b in (("r", 6, 0), ("z", 7, KD)):
                with act.Fori(0, KD) as i:
                    for c, (n0, w) in enumerate(CH):
                        act.wait_ge(f_mm, F_TILES[gate][0] + i * NC + c + 1)
                        act.activation(page[p][:, bass.ds(i * N + n0, w)], bank[c][:, 0:w], ACT.Sigmoid,
                                       bias=bsum[:, bass.ds(i + b, 1)], scale=1.0 / SG).then_inc(f_act, 1)
            with act.Fori(0, KD) as i:
                for c, (n0, w) in enumerate(CH):
                    act.wait_ge(n_hr, i * NC + c + 1)
                    act.activation(t32[:, c, 0:w], t32[:, c, 0:w], ACT.Tanh, bias=vcol("b_ih", i + 2 * KD),
                                   scale=1.0 / SG).then_inc(f_act, 1)

            act.wait_ge(t_ev, t_read("x1"))
            act.dma_start(x1_d, page[1][0:P, 0:NT * D]).then_inc(sp_io, 16)
            layer_norm_sd(2)
            layer_norm_sd(3)
            act.wait_ge(ln_out, 2)
            act.dma_start(xl_d, page[2][0:P, 0:NT * D]).then_inc(sp_io, 16)
            act.wait_ge(r_mm, 1)
            act.activation(rs[:, 0:KD], bank[7][:, 0:KD], ACT.Copy, scale=1.0 / N).then_inc(r_act, 1)
            act.wait_ge(r_mm, 2)
            act.activation(rs[:, 4:5], bank[7][:, 8:9], ACT.Gelu, bias=vcol("rb1")).then_inc(r_act, 1)

            for name, hi, w_, b_ in (("xn", 4, "ns_w", "ns_b"), ("xt", 5, "nt_w", "nt_b")):
                for k in range(KD):
                    for c, (n0, w) in enumerate(CH):
                        f_tile(name, k, c, w, t32[:, c, 0:w] if name == "xn" else cols(6)[:, k, n0:n0 + w],
                               split(hi)[:, 0, k, n0:n0 + w], ACT.Identity, vcol(w_, k), vcol(b_, k))
            act.wait_ge(f_act, f_read("xt"))
            act.dma_start(xt_d, page[6][:, 0:KD * N]).then_inc(sp_io, 16)

            def duplicate_q(n, src, x):
                for part, dst in enumerate((x["qh"], x["ql"])):
                    for r in range(2):
                        for half in range(2):
                            act.dma_start(
                                page[dst][64 * half:64 * half + 64, 0:KD * N].bitcast(F16).rearrange(
                                    "p (k a n) -> p k a n", k=KD, a=2)[:, :, r, :],
                                split(src)[64 * r:64 * r + 64, part, :, :]).then_inc(dup_q, 16)

            def stack_k(src, x):
                for part in range(2):
                    for r in range(2):
                        act.dma_start(
                            page[x["k"]][64 * part:64 * part + 64, 0:KD * N].bitcast(F16).rearrange(
                                "p (k a n) -> p k a n", k=KD, a=2)[:, :, r, :],
                            split(src)[64 * r:64 * r + 64, part, :, :]).then_inc(dup_k, 16)

            def value_highs(x, a):
                t0 = T_TILES[x["n"] + "v"][0]
                with act.Fori(0, NT // 2) as i:
                    for b in range(2):
                        act.wait_ge(t_ev, t0 + 2 * i + b + 1 + 2)
                        act.activation(
                            value_cols(x["v"])[:, bass.ds((2 * i + b) * H * 129, H * 129)].rearrange(
                                "p (h c) -> p h c", h=H)[:, :, 0:HD],
                            rowst[0:P, b, :].rearrange("p (h c) -> p h c", h=H), ACT.Copy).then_inc(v_hi, 1)

            def exponentials(x):
                nu = len(x["units"])

                def head(h):
                    for u in range(nu):
                        n = x["u0"] + h * nu + u
                        act.wait_ge(s_sc, n + 1)
                        act.wait_ge(s_plo, n - since(u, nu, 2) + 1 + 2)
                        act.activation(prob32[0:P, u % 2, :], bank[u % 2][0:P, 0:2 * PB], ACT.Exp, scale=QK_SCALE)
                        act.wait_ge(s_pv, n - since(u, nu, 3) + 1 + 3)
                        act.activation(probh[0:P, u % 3, :], bank[u % 2][0:P, 0:2 * PB], ACT.Exp,
                                       scale=QK_SCALE).then_inc(s_exp, 1)

                with act.Fori(0, H) as h:
                    head(h)

            x = ATT[0]
            act.wait_ge(eb_ld, 32)
            f_evac("sq", page_of(7), 1.0 / SF, lambda i: vsp[:, bass.ds(i, 1)])
            act.wait_ge(f_lo, f_split("sq"))
            act.wait_ge(f_act, f_read("sq"))
            act.wait_ge(sp_io, 48)
            duplicate_q("s", 7, x)
            f_evac("sk", page_of(3), 1.0 / SF, lambda i: vsp[:, bass.ds(i + KD, 1)])
            act.wait_ge(f_lo, f_split("sk"))
            act.wait_ge(f_act, f_read("sk"))
            stack_k(3, x)
            act.wait_ge(dup_q, 16 * 8)
            value_highs(x, 0)
            exponentials(x)
            f_evac("soT", page_of(4), 1.0, lambda i: 0.0)
            f_evac("so", page_of(1), 1.0 / SF, lambda i: vsp[:, bass.ds(i + 2 * KD, 1)])
            f_evac("cq", page_of(2), 1.0 / SF, vecs("cq_b"))
            x = ATT[1]
            f_evac("tq", page_of(1), 1.0 / SF, lambda i: vtp[:, bass.ds(i, 1)])
            act.wait_ge(f_lo, f_split("tq"))
            act.wait_ge(f_act, f_read("tq"))
            duplicate_q("t", 1, x)
            f_evac("tk", page_of(6), 1.0 / SF, lambda i: vtp[:, bass.ds(i + KD, 1)])
            act.wait_ge(f_lo, f_split("tk"))
            act.wait_ge(f_act, f_read("tk"))
            stack_k(6, x)
            act.wait_ge(dup_q, 16 * 16)
            value_highs(x, 1)
            exponentials(x)
            act.wait_ge(f_mm, F_TILES["toT"][0] + 1)
            act.dma_start(page[3][:, 0:KD * N], xt_d).then_inc(back, 16)
            f_evac("toT", page_of(5), 1.0, lambda i: 0.0)
            with act.Fori(0, KD) as i:
                for c, (n0, w) in enumerate(CH):
                    act.wait_ge(to_sum, i * NC + c + 1)
                    act.activation(page_of(4)(0, i, n0, w), t32[:, c, 0:w], ACT.Identity,
                                   bias=vtp[:, bass.ds(i + 2 * KD, 1)]).then_inc(f_act, 1)
            x = ATT[2]
            act.wait_ge(f_mm, F_TILES["to"][1])
            duplicate_q("c", 2, x)
            f_evac("ck", page_of(1), 1.0 / SF, vecs("ck_b"))
            act.wait_ge(f_lo, f_split("ck"))
            act.wait_ge(f_act, f_read("ck"))
            stack_k(1, x)
            value_highs(x, 2)
            exponentials(x)
            act.wait_ge(f_mm, F_TILES["coT"][0] + 1)
            act.dma_start(page[7][0:P, 0:NT * D], xl_d).then_inc(back, 16)
            act.dma_start(page[3][0:P, 0:NT * D], x1_d).then_inc(back, 16)
            f_evac("coT", page_of(2), 1.0, lambda i: 0.0)
            layer_norm_sd(4)
            for k in range(KD):
                for c, (n0, w) in enumerate(CH):
                    f_tile("h2", k, c, w, t32[:, c, 0:w], split(6)[:, 0, k, n0:n0 + w], ACT.Identity,
                           vcol("nm_w", k), vcol("nm_b", k))
            act.wait_ge(xs_done, 1)
            for m in range(4):
                f_evac(f"up{m}", lambda s, i, n0, w: hidden(s, m, i, n0, w), 1.0 / SF,
                       lambda i: vcol("m1_b", i + 4 * m), ACT.Gelu)

        @block.vector
        def _(dve):
            class Chain:
                start, k = 0, 0

            chain = Chain()

            def link(ins):
                chain.k += 1
                ins.then_inc(link_s, 1)
                dve.wait_ge(link_s, chain.start + chain.k)

            def layer_norm(k, src, dst):
                for j in range(NT):
                    last = dve.bn_stats(stats[:, j, :], rows(src)[:, j, :])
                link(last)
                for j in range(NT):
                    last = dve.bn_aggr(mv[:, j, :], stats[:, j, :])
                link(last)
                dve.tensor_scalar(rstd[:], mv[:, :, 1], EPS, None, ALU.add).then_inc(ln_var, 1)
                dve.wait_ge(ln_sd, k)
                link(dve.reciprocal(rstd[:], rstd[:]))
                for j in range(NT):
                    last = dve.tensor_scalar(rows(dst)[:, j, :], rows(src)[:, j, :], mv[:, j, 0:1], rstd[:, j:j + 1],
                                             ALU.subtract, ALU.mult)
                last.then_inc(ln_out, 1)
                dve.wait_ge(ln_out, k)

            def low(name, i, c, w, t_src, hi_src, lo_dst):
                dve.wait_ge(f_act, F_TILES[name][0] + i * NC + c + 1 + NC)
                dve.tensor_tensor(lo_dst, t_src, hi_src, ALU.subtract).then_inc(f_lo, 1)

            def page_of(p):
                return lambda s, i, n0, w: page[p][:, 0:KD * N].bitcast(F16)[:, bass.ds(i * N + s * KD * N + n0, w)]

            def f_lows(name, dst):
                with dve.Fori(0, KD) as i:
                    for c, (n0, w) in enumerate(CH):
                        low(name, i, c, w, t32[:, c, 0:w], dst(0, i, n0, w), dst(1, i, n0, w))

            dve.memset(eights[:], 1.0 / QK_SCALE)
            dve.memset(ones16[:], 1.0)
            dve.memset(ones32[:], 1.0)
            dve.memset(rows(5), 0.0)
            dve.memset(lg[:], -3e38)
            link(dve.memset(cnt[:], 0.0))
            dve.wait_ge(pool_c, 8)
            dve.tensor_scalar(gain16[:], ident[:], MASK_GAIN, None, ALU.mult).then_inc(dve_c, 1)

            dve.wait_ge(in_ld, 64)
            dve.tensor_copy(dstf, dsts)
            link(dve.tensor_copy(grp_f, grp_i))
            dve.tensor_reduce(gw[:, 0:1], grp_f, AX.X, ALU.min)
            link(dve.tensor_reduce(gw[:, 1:2], grp_f, AX.X, ALU.max))
            edges_of_tiles = node_id[0:NG, P:N:P]
            for q in range(2):
                last = dve.tensor_scalar(gw[:, 2 + 9 * q:11 + 9 * q], edges_of_tiles, gw[:, q:q + 1], None, ALU.is_le)
            link(last)
            for q in range(2):
                last = dve.tensor_reduce(gw[:, 21 + q:22 + q], gw[:, 2 + 9 * q:11 + 9 * q], AX.X, ALU.add)
            link(last)
            link(dve.tensor_scalar(gw[:, 23:24], gw[:, 22:23], 1.0, None, ALU.add))
            dve.tensor_tensor(gw[:, 20:21], gw[:, 23:24], gw[:, 21:22], ALU.subtract).then_inc(win_s, 1)
            dve.wait_ge(win_s, 2)
            dve.tensor_copy(gwi[:, 0:1], gw[:, 21:22])
            dve.tensor_copy(gwi[:, 1:2], gw[:, 23:24])
            link(dve.tensor_scalar(gw[:, 24:26], bank[7][0:NG, 0:2], float(NT), None, ALU.add))
            link(dve.tensor_tensor(gw[:, 24:25], gw[:, 24:25], gw[:, 21:22], ALU.subtract))
            dve.tensor_copy(gwi[:, 2:4], gw[:, 24:26]).then_inc(win_s, 1)

            dve.tensor_tensor(bsum[:, 0:8], vec[:, VEC["b_ih"][0]:VEC["b_ih"][0] + 8],
                              vec[:, VEC["b_hh"][0]:VEC["b_hh"][0] + 8], ALU.add)
            dve.tensor_scalar(bsum[:, 8:12], vec[:, VEC["b_hh"][0] + 8:VEC["b_hh"][0] + 12], SG, None, ALU.mult)

            v0 = VEC["gamma"][0]
            dve.tensor_scalar(bns[:, 0, :], vec[:, v0 + 12:v0 + 16], EPS, None, ALU.add)

            dve.wait_ge(x_ld, 16 * NT)
            layer_norm(1, 1, 6)
            for k in range(KD):
                for c, (n0, w) in enumerate(CH):
                    low("hT", k, c, w, cols(2)[:, k, n0:n0 + w], split(3)[:, 0, k, n0:n0 + w],
                        split(3)[:, 1, k, n0:n0 + w])
            dve.wait_ge(row_ld, 16)
            t0 = T_TILES["P"][0]
            with dve.Fori(0, NT // 2) as i:
                for b in range(2):
                    dve.wait_ge(t_mm, t0 + 2 * i + b + 1)
                    dve.wait_ge(p_st[b], 16 * i)
                    dve.scalar_tensor_tensor(out=rowst[0:P, b, :], in0=bank[3 + b][0:P, :], scalar=1.0 / SG,
                                             in1=rowb[:], op0=ALU.mult, op1=ALU.add).then_inc(t_ev, 1)

            def tiles(n0, s, gath_done):
                behind = dve.value_load(win[:, bass.ds(n0 * 4 + 3, 1)], min_val=0, max_val=NG * NT + NT)
                dve.wait_ge(s_mm, behind)

                def relu_low(q):
                    dve.wait_ge(e_hi, n0 * GE + q + 1 + 2)
                    dve.scalar_tensor_tensor(out=relu[:, s * GE + q, 1, :], in0=esum[:, q % 2, :], scalar=0.0,
                                             in1=relu[:, s * GE + q, 0, :], op0=ALU.max,
                                             op1=ALU.subtract).then_inc(e_lo, 1)

                for q in range(GE):
                    n = n0 * GE + q
                    dve.wait_ge(e_mm, n + 1 + GE)
                    dve.wait_ge(g_ld[s * GE + q], gath_done)
                    dve.wait_ge(e_lo, n + 1)
                    dve.scalar_tensor_tensor(out=esum[:, q % 2, :], in0=bank[q % 2][0:P, :], scalar=1.0 / SG,
                                             in1=gath[:, s * GE + q, :], op0=ALU.mult, op1=ALU.add).then_inc(e_sum, 1)
                    dve.tensor_scalar(onehot[:, s * GE + q, :], node_id[:], dstf[:, bass.ds(n, 1)], None, ALU.is_equal)
                    if q >= 1:
                        relu_low(q - 1)
                relu_low(GE - 1)

            def windows(n0):
                first, end, number = (dve.value_load(win[:, bass.ds(n0 * 4 + c, 1)], min_val=lo, max_val=hi)
                                      for c, lo, hi in ((0, 0, NT - 1), (1, 1, NT), (2, 0, NG * NT + NT)))
                with dve.Fori(first, end) as j:
                    dve.wait_ge(s_mm, number + j + 1)
                    dve.wait_ge(s_add, number + j)
                    dve.tensor_tensor(page[5][0:P, bass.ds(j * D, D)], page[5][0:P, bass.ds(j * D, D)],
                                      bank[2][0:P, :], ALU.add)
                    dve.tensor_tensor(cnt[:, bass.ds(j, 1)], cnt[:, bass.ds(j, 1)], bank[5][0:P, 0:1],
                                      ALU.add).then_inc(s_add, 1)

            dve.wait_ge(win_io, 32)
            tiles(0, 0, 16)
            with dve.Fori(0, NG // 2 - 1) as i:
                tiles(2 * i + 1, 1, 16 * (i + 1))
                windows(2 * i)
                tiles(2 * i + 2, 0, 16 * (i + 2))
                windows(2 * i + 1)
            tiles(NG - 1, 1, 16 * (NG // 2))
            windows(NG - 2)
            windows(NG - 1)
            link(dve.memset(rden[:], 0.0))
            dve.memset(olo[:], 0.0).then_inc(agg_done, 1)

            f_lows("aggT", page_of(4))
            dve.wait_ge(c_mt, 1)
            dve.wait_ge(b2_ld, 16)
            link(dve.tensor_tensor(cntb.rearrange("p (a b) -> p a b", a=NT),
                                   bank[7][0:NT, 0:P].unsqueeze(1).to_broadcast([NT, NT, P]), blockdiag[:], ALU.mult))
            link(dve.tensor_scalar(b2f, b2f, SG, None, ALU.mult))
            dve.tensor_copy(cnth[:, 0, :], cntb)
            link(dve.tensor_copy(b2h[:, 0, :], b2f))
            link(dve.tensor_tensor(cnth[:, 1, :], cntb, cnth[:, 0, :], ALU.subtract))
            dve.tensor_tensor(b2h[:, 1, :], b2f, b2h[:, 0, :], ALU.subtract).then_inc(c_s, 1)
            f_lows("M", page_of(5))
            link(dve.reciprocal(bns[:, 0, :], bns[:, 0, :]))
            link(dve.tensor_tensor(bns[:, 0, :], bns[:, 0, :], vec[:, v0:v0 + 4], ALU.mult))
            link(dve.tensor_tensor(bns[:, 1, :], bns[:, 0, :], vec[:, v0 + 8:v0 + 12], ALU.mult))
            link(dve.tensor_tensor(bns[:, 1, :], vec[:, v0 + 4:v0 + 8], bns[:, 1, :], ALU.subtract))

            def new_front(i, c, n0, w):
                dve.wait_ge(f_mm, F_TILES["n"][0] + i * NC + c + 1)
                r = page[6][:, bass.ds(i * N + n0, w)]
                link(dve.scalar_tensor_tensor(out=t32[:, c, 0:w], in0=bank[5 + c][:, 0:w],
                                              scalar=bsum[:, bass.ds(i + 8, 1)], in1=r, op0=ALU.add, op1=ALU.mult))
                dve.tensor_tensor(t32[:, c, 0:w], t32[:, c, 0:w], bank[c][:, 0:w], ALU.add).then_inc(n_hr, 1)

            def new_back(i, c, n0, w):
                h, d, z = (page[p][:, bass.ds(i * N + n0, w)] for p in (2, 6, 7))
                dve.wait_ge(f_act, F_TILES["n"][0] + i * NC + c + 1 + NC)
                link(dve.tensor_tensor(d, h, t32[:, c, 0:w], ALU.subtract))
                link(dve.tensor_tensor(d, d, z, ALU.mult))
                link(dve.tensor_tensor(d, d, t32[:, c, 0:w], ALU.add))
                link(dve.tensor_scalar(d, d, bns[:, 0, bass.ds(i, 1)], bns[:, 1, bass.ds(i, 1)], ALU.mult, ALU.add))
                dve.tensor_tensor(h, h, d, ALU.add).then_inc(n_new, 1)

            base = chain.start + chain.k
            links = 5 * NC
            dve.wait_ge(f_act, f_read("z"))
            with dve.Fori(0, KD) as i:
                chain.start, chain.k = base + i * links, 0
                for c, (n0, w) in enumerate(CH):
                    new_front(i, c, n0, w)
                    if c:
                        new_back(i, c - 1, *CH[c - 1])
                new_back(i, NC - 1, *CH[NC - 1])
                assert chain.k == links
            chain.start, chain.k = base + KD * links, 0

            t0 = T_TILES["x1"][0]
            for j in range(NT):
                dve.wait_ge(t_mm, t0 + j + 1)
                dve.tensor_tensor(rows(1)[:, j, :], rows(1)[:, j, :], bank[3 + j % 2][0:P, :], ALU.add).then_inc(t_ev, 1)
            dve.wait_ge(t_ev, t_read("x1"))
            layer_norm(2, 1, 2)
            layer_norm(3, 2, 3)
            dve.wait_ge(r_mm, 3)
            link(dve.tensor_tensor(lg[:, 0:8], bank[7][0:1, 16:24], rb2[:], ALU.add))
            dve.tensor_copy(lg[:, 8:12], lg[:, 0:4])
            link(dve.tensor_copy(lg[:, 16:20], lg[:, 4:8]))
            dve.max(lg[:, 24:32], lg[:, 8:16])
            link(dve.max(lg[:, 32:40], lg[:, 16:24]))
            dve.max_index(choice[:, 0:8], lg[:, 24:32], lg[:, 8:16]).then_inc(r_ix, 1)
            dve.max_index(choice[:, 8:16], lg[:, 32:40], lg[:, 16:24]).then_inc(r_ix, 1)

            for name, p in (("xn", 4), ("xt", 5)):
                for k in range(KD):
                    for c, (n0, w) in enumerate(CH):
                        low(name, k, c, w, t32[:, c, 0:w] if name == "xn" else cols(6)[:, k, n0:n0 + w],
                            split(p)[:, 0, k, n0:n0 + w], split(p)[:, 1, k, n0:n0 + w])

            def value_rows(x, a):
                t0 = T_TILES[x["n"] + "v"][0]
                dve.wait_ge(row_ld, 16 * (a + 2))
                if a < 2:
                    dve.wait_ge(dup_q, 16 * 8 * (a + 1))
                dve.memset(values(x["v"])[:, :, :, HD:HD + 1], 1.0)
                with dve.Fori(0, NT // 2) as i:
                    dve.wait_ge(v_lo, a * NT + 2 * i)
                    for b in range(2):
                        dve.wait_ge(t_mm, t0 + 2 * i + b + 1)
                        dve.scalar_tensor_tensor(out=rowst[0:P, b, :], in0=bank[3 + b][0:P, :], scalar=1.0 / SF,
                                                 in1=rowb[:], op0=ALU.mult, op1=ALU.add).then_inc(t_ev, 1)
                    for b in range(2):
                        v = value_cols(x["v"])[:, bass.ds((2 * i + b) * H * 129, H * 129)].rearrange(
                            "p (h c) -> p h c", h=H)
                        dve.wait_ge(v_hi, a * NT + 2 * i + b + 1)
                        dve.wait_ge(t_ev, t0 + 2 * i + b + 1 + 2)
                        dve.tensor_tensor(v[:, :, HD + 1:2 * HD + 1], rowst[0:P, b, :].rearrange("p (h c) -> p h c", h=H),
                                          v[:, :, 0:HD], ALU.subtract).then_inc(v_lo, 1)

            def attention(x):
                units, nu = x["units"], len(x["units"])
                ends = {u: c for u, (c, p) in enumerate(units) if p == (c if x["causal"] else NB - 1)}

                def prob_low(h, u):
                    n = x["u0"] + h * nu + u
                    dve.wait_ge(s_exp, n + 1 + 2)
                    dve.tensor_tensor(probl[0:P, u % 3, :], prob32[0:P, u % 2, :], probh[0:P, u % 3, :],
                                      ALU.subtract).then_inc(s_plo, 1)

                def maxima(h, par, e):
                    c, p = units[e]
                    n = x["a0"] + h * nu + e
                    dve.wait_ge(a_mm, n + 1)
                    b = bank[(2, 5)[e % 2]]
                    dve.tensor_reduce(mxs[:, par, 2 * c:2 * c + 2, p],
                                      b[0:P, 0:2 * PB].rearrange("p (a n) -> p a n", a=2), AX.X,
                                      ALU.max).then_inc(a_mx, 1)

                def all_maxima(h, par):
                    dve.wait_ge(a_mx, x["a0"] + h * nu + nu + 2)
                    dve.tensor_reduce(mx[:, par, :], mxs[:, par, :, :], AX.X, ALU.max).then_inc(m_all, 1)

                def shifts(h, par):
                    dve.wait_ge(m_t, x["h0"] + h + 1)
                    dve.scalar_tensor_tensor(
                        out=shift[:, par, :].rearrange("p (a b) -> p a b", a=NT),
                        in0=bank[6][0:NT, 0:P].unsqueeze(1).to_broadcast([NT, NT, P]), scalar=-QK_SCALE,
                        in1=blockdiag[:], op0=ALU.mult, op1=ALU.mult).then_inc(m_sh, 1)

                def output(h, u):
                    c = ends[u]
                    n = x["u0"] + h * nu + u
                    dve.wait_ge(s_pv, n + 1 + 3)
                    o = bank[3 + c % 2][0:P, 0:258].rearrange("p (a n) -> p a n", a=2)
                    dve.wait_ge(o_ev, x["b0"] + NB * h + c + 2)
                    dve.reciprocal(rden[:], o[:, :, HD])
                    link(dve.tensor_copy(olo[:], o[:, :, HD + 1:2 * HD + 1]))
                    link(dve.tensor_tensor(osum[:], o[:, :, 0:HD], olo[:], ALU.add))
                    dst = page[x["o"]][0:P, bass.ds(2 * c * D + h * HD, D + HD)]
                    for r in range(2):
                        last = dve.tensor_scalar(dst[:, r * D:r * D + HD], osum[:, r, :], rden[:, r:r + 1], None, ALU.mult)
                    last.then_inc(o_ev, 1)

                def head(h, par, following):
                    for u in range(nu):
                        prob_low(h, u)
                        if following:
                            for e in x["early"][u]:
                                maxima(h + 1, 1 - par, e)
                            if u == nu - 5:
                                all_maxima(h + 1, 1 - par)
                        if u - 2 in ends:
                            output(h, u - 2)
                        if following and u == nu - 2:
                            shifts(h + 1, 1 - par)
                    for u in (nu - 2, nu - 1):
                        if u in ends:
                            output(h, u)

                link(dve.memset(mxs[:], -3e38))
                for e in range(nu):
                    maxima(0, 0, e)
                all_maxima(0, 0)
                shifts(0, 0)
                base = chain.start + chain.k
                with dve.Fori(0, H // 2 - 1) as i:
                    chain.start, chain.k = base + i * 4 * NB, 0
                    head(2 * i, 0, True)
                    head(2 * i + 1, 1, True)
                    assert chain.k == 4 * NB
                chain.start, chain.k = base + (H // 2 - 1) * 4 * NB, 0
                head(H - 2, 0, True)
                head(H - 1, 1, False)

            f_lows("sq", page_of(7))
            f_lows("sk", page_of(3))
            value_rows(ATT[0], 0)
            dve.wait_ge(dup_k, 16 * 4)
            attention(ATT[0])
            f_lows("soT", page_of(4))
            f_lows("so", page_of(1))
            f_lows("cq", page_of(2))
            f_lows("tq", page_of(1))
            f_lows("tk", page_of(6))
            value_rows(ATT[1], 1)
            dve.wait_ge(dup_k, 16 * 8)
            attention(ATT[1])
            f_lows("toT", page_of(5))
            dve.wait_ge(back, 16)
            g0, l0 = F_TILES["to"][0], LOWS["to"][0]
            with dve.Fori(0, KD) as i:
                for c, (n0, w) in enumerate(CH):
                    dve.wait_ge(f_mm, g0 + i * NC + c + 1)
                    dve.wait_ge(f_lo, l0 + i * NC + c + 1)
                    dve.scalar_tensor_tensor(out=t32[:, c, 0:w], in0=bank[c][:, 0:w], scalar=1.0 / SF,
                                             in1=page[3][:, bass.ds(i * N + n0, w)], op0=ALU.mult,
                                             op1=ALU.add).then_inc(to_sum, 1)
                for c, (n0, w) in enumerate(CH):
                    dve.wait_ge(f_act, g0 + i * NC + c + 1 + NC)
                    dve.scalar_tensor_tensor(out=page_of(4)(1, i, n0, w), in0=t32[:, c, 0:w],
                                             scalar=vtp[:, bass.ds(i + 2 * KD, 1)], in1=page_of(4)(0, i, n0, w),
                                             op0=ALU.add, op1=ALU.subtract).then_inc(f_lo, 1)
            f_lows("ck", page_of(1))
            value_rows(ATT[2], 2)
            dve.wait_ge(dup_k, 16 * 12)
            attention(ATT[2])
            f_lows("coT", page_of(2))
            dve.wait_ge(back, 48)
            dve.wait_ge(row_ld, 16 * 5)
            for j in range(NT):
                last = dve.tensor_tensor(rows(7)[:, j, :], rows(7)[:, j, :], rowb[:], ALU.add)
            last.then_inc(y_st, 1)
            dve.wait_ge(y_st, 1)
            t0 = T_TILES["co"][0]
            with dve.Fori(0, NT // 2) as i:
                for b in range(2):
                    dve.wait_ge(t_mm, t0 + 2 * i + b + 1)
                    y = page[7][0:P, bass.ds((2 * i + b) * D, D)]
                    dve.scalar_tensor_tensor(out=y, in0=bank[3 + b][0:P, :], scalar=1.0 / SF, in1=y, op0=ALU.mult,
                                             op1=ALU.add).then_inc(t_ev, 1)
            dve.wait_ge(t_ev, t_read("co"))
            layer_norm(4, 7, 4)
            dve.wait_ge(row_ld, 16 * 6)
            link(dve.tensor_tensor(page[7][0:P, 0:NT * D], page[7][0:P, 0:NT * D], page[3][0:P, 0:NT * D], ALU.add))
            for k in range(KD):
                for c, (n0, w) in enumerate(CH):
                    low("h2", k, c, w, t32[:, c, 0:w], split(6)[:, 0, k, n0:n0 + w], split(6)[:, 1, k, n0:n0 + w])
            for j in range(NT):
                last = dve.tensor_tensor(rows(7)[:, j, :], rows(7)[:, j, :], rowb[:], ALU.add)
            last.then_inc(xs_done, 1)
            dve.wait_ge(xs_done, 1)
            for m in range(4):
                f_lows(f"up{m}", lambda s, i, n0, w: hidden(s, m, i, n0, w))
            t0 = T_TILES["down"][0]
            with dve.Fori(0, NT // 2) as i:
                for b in range(2):
                    dve.wait_ge(t_mm, t0 + 2 * i + b + 1)
                    y = page[7][0:P, bass.ds((2 * i + b) * D, D)]
                    dve.scalar_tensor_tensor(out=y, in0=bank[3 + b][0:P, :], scalar=1.0 / SF, in1=y, op0=ALU.mult,
                                             op1=ALU.add).then_inc(t_ev, 1)


def kernel(**inputs):
    import concourse.bacc as bacc
    from concourse.bass_utils import run_bass_kernel_spmd

    v = {k: np.asarray(x) for k, x in inputs.items()}
    g = {k[7:]: x for k, x in v.items() if k.startswith("L0_gnn_")}
    f = {k[7:]: x for k, x in v.items() if k.startswith("L0_ffn_")}

    def fm(x):
        return x.reshape(-1, 128).T

    def fm4(x):
        return x.reshape(x.shape[0], -1, 128).transpose(0, 2, 1)

    cb = f["cross_in_b"]
    parts = {"b_ih": g["b_ih"], "b_hh": g["b_hh"], "gamma": g["gamma"], "beta": g["beta"], "mean": g["run_mean"],
             "var": g["run_var"], "ns_w": f["norm_s_w"], "ns_b": f["norm_s_b"], "nt_w": f["norm_t_w"],
             "nt_b": f["norm_t_b"], "cq_b": cb[0:D], "ck_b": cb[D:2 * D], "nm_w": f["norm_mlp_w"],
             "nm_b": f["norm_mlp_b"], "m1_b": f["mlp_b1"], "rb1": f["router_b1"]}
    arrays = {
        "x": v["x"],
        "src_pt": v["src"].reshape(ET, P).T,
        "dst_pt": v["dst"].reshape(ET, P).T,
        "dst_g": v["dst"].reshape(NG, GW),
        "eaT": v["edge_attr_128"].T,
        "w1T": g["W1"].T, "w2T": g["W2"].T, "wihT": g["W_ih"].T, "whhT": g["W_hh"].T,
        "spinT": f["sp_in_w"].transpose(0, 2, 1), "spoutT": f["sp_out_w"].transpose(0, 2, 1),
        "tqT": f["tq_w"].transpose(0, 2, 1), "tkT": f["tk_w"].transpose(0, 2, 1),
        "tvT": f["tv_w"].transpose(0, 2, 1), "tpT": f["tp_w"].transpose(0, 2, 1),
        "cinT": f["cross_in_w"].T, "coutT": f["cross_out_w"].T, "m1T": f["mlp_w1"].T, "m2T": f["mlp_w2"].T,
        "rw1T": f["router_w1"].T, "rw2T": f["router_w2"].T, "rb2": f["router_b2"].reshape(1, -1),
        "vec": np.concatenate([fm(parts[name]) for name in VEC], axis=1),
        "rowv": np.stack([g["b1"], g["b2"], cb[2 * D:3 * D], f["cross_out_b"], f["mlp_b2"]]),
        "vsp": np.concatenate([fm4(f["sp_in_b"][:, 0:2 * D]), fm4(f["sp_out_b"])], axis=2),
        "vtp": np.concatenate([fm4(f["tq_b"]), fm4(f["tk_b"]), fm4(f["tp_b"])], axis=2),
        "svrow": f["sp_in_b"][:, 2 * D:3 * D], "tvrow": f["tv_b"],
    }
    arrays = {k: np.ascontiguousarray(x) for k, x in arrays.items()}
    nc = bacc.Bacc("TRN2", target_bir_lowering=False, num_devices=1)
    a = {k: nc.dram_tensor("in_" + k, x.shape, mybir.dt.from_np(x.dtype), kind="ExternalInput").ap()
         for k, x in arrays.items()}
    out = nc.dram_tensor("out", (N, D), F32, kind="ExternalOutput").ap()
    nc.disable_value_cache = True
    program(nc, a, out)
    r = run_bass_kernel_spmd(nc, [{"in_" + k: x for k, x in arrays.items()}], core_ids=[0])
    return r.results[0]["out"]
```

```python
from contextlib import ExitStack

import numpy as np
import concourse.bass as bass
from concourse import mybir

F32 = mybir.dt.float32
F16 = mybir.dt.float16
I32 = mybir.dt.int32
U32 = mybir.dt.uint32
ALU = mybir.AluOpType
ACT = mybir.ActivationFunctionType
AX = mybir.AxisListType

N = 1250
E = 20000
D = 512
ED = 128
P = 125
NT = N // P
ET = E // P
GE = 4
NG = ET // GE
GW = GE * P
KD = D // 128
H = 8
HD = D // H
FF = 4 * D
CH = [(0, 500), (500, 500), (1000, 250)]
PB = 2 * P
NC = len(CH)
SG = 64.0
SF = 16.0
EPS = 1e-5
QK_SCALE = HD ** -0.5
MASKED = -60000.0
MASK_GAIN = 2048.0
PAGE = 5160
EXPERTS = 4

VEC = {}
for _name, _n in [("b_ih", 12), ("b_hh", 12), ("gamma", 4), ("beta", 4), ("mean", 4), ("var", 4),
                  ("ns_w", 4), ("ns_b", 4), ("nt_w", 4), ("nt_b", 4), ("cq_b", 4), ("ck_b", 4),
                  ("nm_w", 4), ("nm_b", 4), ("m1_b", 16), ("rb1", 1)]:
    VEC[_name] = (sum(n for _, n in VEC.values()), _n)
NV = sum(n for _, n in VEC.values())
ROW = {"b1": 0, "b2": 1, "cv": 2, "cout": 3, "m2": 4}


def program(nc, a, out):
    ctx = ExitStack()
    with ctx:
        def sb(name, shape, dt):
            return ctx.enter_context(nc.sbuf_tensor(name, shape, dt))

        def sem(name):
            return ctx.enter_context(nc.semaphore(name))

        bank = [ctx.enter_context(nc.psum_tensor(f"bank{i}", [128, 512], F32)) for i in range(8)]

        pages = sb("pages", [128, 7 * PAGE], F32)
        page = [None] + [pages[:, i * PAGE:(i + 1) * PAGE] for i in range(7)]
        wide = [pages[:, 2 * s * PAGE:2 * s * PAGE + 8 * N].bitcast(F16).rearrange("p (k n) -> p k n", k=FF // 128)
                for s in range(2)]
        slots = sb("slots", [128, 4, 2, KD, D], F16)
        stage = sb("stage", [128, 4, D], F32)
        scratch = sb("scratch", [128, 2560], F32)
        t32 = scratch[:, 0:1536].rearrange("p (c n) -> p c n", c=NC)
        rowst = scratch[:, 1536:2560].rearrange("p (c n) -> p c n", c=2)
        prob32 = scratch[:, 0:1000].rearrange("p (c n) -> p c n", c=2)
        probh = scratch[:, 1000:1750].bitcast(F16).rearrange("p (c n) -> p c n", c=3)
        probl = scratch[:, 1750:2500].bitcast(F16).rearrange("p (c n) -> p c n", c=3)
        eah = scratch[:, 0:500].bitcast(F16).rearrange("p (c n) -> p c n", c=2)
        eal = scratch[:, 500:1000].bitcast(F16).rearrange("p (c n) -> p c n", c=2)
        ident = sb("ident", [128, 128], F32)
        gain16 = sb("gain16", [128, 128], F16)
        ones32 = sb("ones32", [P, 1], F32)
        ones16 = sb("ones16", [P, 1], F16)
        blockdiag = sb("blockdiag", [NT, NT, P], F16)
        turns = sb("turns", [128, 1250], F32)
        srcs = turns[0:P, 512:512 + ET].bitcast(I32)
        dstf = turns[0:P, 672:672 + ET]
        win = turns[0:1, 832:832 + 4 * NG].bitcast(I32)     
        rw1 = turns[:, 0:512].rearrange("p (k n) -> p k n", k=KD)
        rden, onorm = turns[:, 0:500], turns[:, 512:1012]
        node_id = sb("node_id", [P, N], F16)
        idx_ring = sb("idx_ring", [P, 2, GE], I32)
        cnt = sb("cnt", [P, NT], F32)
        vec = sb("vec", [128, NV], F32)
        vsp = sb("vsp", [128, 12], F32)
        vtp = sb("vtp", [128, 12], F32)
        rowb = sb("rowb", [P, D], F32)
        stats = sb("stats", [P, NT, 6], F32)
        mv = sb("mv", [P, NT, 2], F32)
        rstd = sb("rstd", [P, NT], F32)
        bsum = sb("bsum", [128, 12], F32)
        bns = sb("bns", [128, 2, KD], F32)
        mxs = sb("mxs", [P, 2, NT, NC], F32)
        mx = sb("mx", [P, 2, NT], F32)
        rs = sb("rs", [128, 8], F32)
        rw2 = sb("rw2", [128, 2 * EXPERTS], F32)
        rb2 = sb("rb2", [1, 2 * EXPERTS], F32)
        lg = sb("lg", [1, 40], F32)
        choice = sb("choice", [1, 16], U32)

        def vcol(name, i=0, n=1):
            at = VEC[name][0] + i
            return vec[:, bass.ds(at, n)]

        def rows(p):
            return page[p][0:P, 0:NT * D].rearrange("p (t d) -> p t d", t=NT)

        def cols(p):
            return page[p][:, 0:KD * N].rearrange("p (k n) -> p k n", k=KD)

        def split(p):
            return page[p][:, 0:KD * N].bitcast(F16).rearrange("p (s k n) -> p s k n", s=2, k=KD)

        def value_highs_of(x):
            return page[x["va"]][0:P, 0:NT * H * HD].bitcast(F16)

        def value_lows_of(x):
            return page[x["vb"]][0:P, 0:NT * H * HD // 2].bitcast(F16)

        def hidden(s, m, i, n0, w):
            return pages[:, 2 * s * PAGE:2 * s * PAGE + 8 * N].bitcast(F16)[:, bass.ds((4 * m + i) * N + n0, w)]

        gath = page[6][0:P, 0:8 * D].rearrange("p (s d) -> p s d", s=8)
        eas = page[6][:, 8 * D:8 * D + 1000].rearrange("p (s n) -> p s n", s=2)
        relu = page[7][0:P, 0:8 * D].bitcast(F16).rearrange("p (s l d) -> p s l d", s=8, l=2)
        esum = page[7][0:P, 8 * D:10 * D].rearrange("p (s d) -> p s d", s=2)
        onehot = page[4][0:P, 0:5000].bitcast(F16).rearrange("p (s n) -> p s n", s=8)
        cntb = page[6][0:NT, 0:N]
        cnth = page[6][0:NT, N:2 * N].bitcast(F16).rearrange("p (l n) -> p l n", l=2)
        b2f = page[6][0:NT, 2 * N:2 * N + D]
        b2h = page[6][0:NT, 2 * N + D:2 * N + 2 * D].bitcast(F16).rearrange("p (l n) -> p l n", l=2)
        mask_s = node_id[:, 0:P]
        mask_t = node_id[:, P:2 * P]
        grp_i = page[7][0:NG, 0:GW].bitcast(I32)
        grp_f = page[7][0:NG, GW:2 * GW]
        gw = page[7][0:NG, 1000:1032]
        gwi = page[7][0:NG, 1040:1044].bitcast(I32)
        tri = page[7][0:NG, 1100:1100 + 2 * NG].rearrange("p (a n) -> p a n", a=2)
        dsts = page[7][0:P, 1200:1200 + ET].bitcast(I32)

        proj_d = nc.dram_tensor("proj_d", (N, D), F32, kind="Internal").ap()
        x1_d = nc.dram_tensor("x1_d", (P, NT * D), F32, kind="Internal").ap()
        xl_d = nc.dram_tensor("xl_d", (P, NT * D), F32, kind="Internal").ap()
        xt_d = nc.dram_tensor("xt_d", (128, KD * N), F32, kind="Internal").ap()
        win_d = nc.dram_tensor("win_d", (NG, 4), I32, kind="Internal").ap()

        in_ld = sem("in_ld")
        x_ld = sem("x_ld")
        pool_c = sem("pool_c")
        dve_c = sem("dve_c")
        link_s = sem("link_s")
        ln_var = sem("ln_var")
        ln_sd = sem("ln_sd")
        ln_out = sem("ln_out")
        f_mm = sem("f_mm")
        f_act = sem("f_act")
        f_lo = sem("f_lo")
        t_mm = sem("t_mm")
        t_ev = sem("t_ev")
        v_hi = sem("v_hi")
        v_lo = sem("v_lo")
        p_st = [sem(f"p_st{i}") for i in range(2)]
        w_ld = [sem(f"w_ld{i}") for i in range(4)]
        w_sc = sem("w_sc")
        w_hi = sem("w_hi")
        w_split = sem("w_split")
        win_s = sem("win_s")
        win_io = sem("win_io")
        ea_ld = [sem(f"ea_ld{i}") for i in range(2)]
        ea_hi = sem("ea_hi")
        ea_lo = sem("ea_lo")
        g_ix = sem("g_ix")
        g_ld = [sem(f"g_ld{i}") for i in range(8)]
        e_mm = sem("e_mm")
        e_sum = sem("e_sum")
        e_hi = sem("e_hi")
        e_lo = sem("e_lo")
        s_mm = sem("s_mm")
        s_add = sem("s_add")
        agg_done = sem("agg_done")
        c_s = sem("c_s")
        c_mt = sem("c_mt")
        n_hr = sem("n_hr")
        n_new = sem("n_new")
        rw_ld = sem("rw_ld")
        b2_ld = sem("b2_ld")
        r_mm = sem("r_mm")
        r_act = sem("r_act")
        r_ix = sem("r_ix")
        sp_io = sem("sp_io")
        to_sum = sem("to_sum")
        xs_done = sem("xs_done")
        back = sem("back")
        back_x1 = sem("back_x1")
        eb_ld = sem("eb_ld")
        row_ld = sem("row_ld")
        big_ld = [sem(f"big_ld{i}") for i in range(2)]
        small_ld = [sem(f"small_ld{i}") for i in range(2)]
        eight = sem("eight")
        v_one = sem("v_one")
        a_mm = sem("a_mm")
        a_mx = sem("a_mx")
        m_all = sem("m_all")
        m_t = sem("m_t")
        m_sh = sem("m_sh")
        s_sc = sem("s_sc")
        s_exp = sem("s_exp")
        s_plo = sem("s_plo")
        s_pv = sem("s_pv")
        o_ev = sem("o_ev")
        o_st = sem("o_st")
        y_st = sem("y_st")

        F_TILES, T_TILES, LOWS = {}, {}, {}
        g = l = t = 0
        for name, kind, tiles, low in [
                ("hT", "F", KD * NC, 1), ("P", "T", NT, 0), ("aggT", "F", KD * NC, 1), ("M", "F", KD * NC, 1),
                ("r", "F", KD * NC, 0), ("z", "F", KD * NC, 0), ("n", "F", KD * NC, 0), ("x1", "T", NT, 0),
                ("xn", "F", KD * NC, 1), ("xt", "F", KD * NC, 1),
                ("sq", "F", KD * NC, 1), ("sk", "F", KD * NC, 1), ("sv", "T", NT, 0),
                ("so", "F", KD * NC, 1), ("cq", "F", KD * NC, 1),
                ("tq", "F", KD * NC, 1), ("tk", "F", KD * NC, 1), ("tv", "T", NT, 0),
                ("to", "F", KD * NC, 1),
                ("ck", "F", KD * NC, 1), ("cv", "T", NT, 0),
                ("co", "T", NT, 0), ("h2", "F", KD * NC, 1),
                ("up0", "F", KD * NC, 1), ("up1", "F", KD * NC, 1), ("up2", "F", KD * NC, 1),
                ("up3", "F", KD * NC, 1), ("down", "T", NT, 0)]:
            if kind == "F":
                F_TILES[name] = (g, g + tiles)
                LOWS[name] = (l, l + tiles * low)
                g, l = g + tiles, l + tiles * low
            else:
                T_TILES[name] = (t, t + tiles)
                t += tiles

        def since(v, units, ring):
            return ring if v >= ring else v + units - max(w for w in range(units) if w % ring == v)

        def f_read(name):
            return F_TILES[name][1] + NC

        def f_split(name):
            return LOWS[name][1] + NC

        def t_read(name):
            return T_TILES[name][1] + 2

        UNITS = [("w1a", "w1T", None, 0, 0, KD, SG, "P"), ("w1b", "w1T", None, D, 0, 1, SG, "aggT"),
                 ("w2", "w2T", None, 0, 0, KD, SG, "M")]
        for i, stg in enumerate(("r", "z", "n")):
            UNITS += [("ih" + stg, "wihT", None, 0, i * D, KD, SG, stg),
                      ("hh" + stg, "whhT", None, 0, i * D, KD, SG, stg)]
        UNITS += [("sq", "spinT", "s", 0, 0, KD, SF, "sq"), ("sk", "spinT", "s", 0, D, KD, SF, "sk"),
                  ("sv", "spinT", "s", 0, 2 * D, KD, SF, "sv"), ("so", "spoutT", "s", 0, 0, KD, SF, "so"),
                  ("cq", "cinT", None, 0, 0, KD, SF, "cq"),
                  ("tq", "tqT", "t", 0, 0, KD, SF, "tq"), ("tk", "tkT", "t", 0, 0, KD, SF, "tk"),
                  ("tv", "tvT", "t", 0, 0, KD, SF, "tv"), ("to", "tpT", "t", 0, 0, KD, SF, "to"),
                  ("ck", "cinT", None, 0, D, KD, SF, "ck"), ("cv", "cinT", None, 0, 2 * D, KD, SF, "cv"),
                  ("co", "coutT", None, 0, 0, KD, SF, "co")]
        UNITS += [(f"up{i}", "m1T", None, 0, i * D, KD, SF, f"up{i}") for i in range(4)]
        UNITS += [(f"down{i}", "m2T", None, i * D, 0, KD, SF, "down") for i in range(4)]
        UNIT = {u[0]: i for i, u in enumerate(UNITS)}
        SLOT = {u[0]: i % 4 for i, u in enumerate(UNITS)}
        CHUNKS = [(i, k) for i, u in enumerate(UNITS) for k in range(u[5])]
        SPLIT_AT = {}
        for n, (i, k) in enumerate(CHUNKS):
            SPLIT_AT[UNITS[i][0]] = n + 1
        FIRST_AFTER_EDGES = CHUNKS.index((2, 0))

        ATT = [dict(n="s", q=7, k=3, ring=2, va=6, vb=1, o=4, causal=False),
               dict(n="t", q=1, k=6, ring=4, va=7, vb=3, o=5, causal=True),
               dict(n="c", q=2, k=1, ring=6, va=7, vb=3, o=4, causal=False)]

        def score_units(causal):
            units = []
            for c, (n0, w) in enumerate(CH):
                before = n0 // P if causal else NT
                if w == 2 * PB:
                    units += [(c, [(s, 0, w, 0, False)]) for s in range(before)]
                    if causal:
                        units += [(c, [(before, 0, w, 0, True)]),
                                  (c, [(before + 1, P, 3 * P, 0, True), (before + 3, 3 * P, P, 3 * P, True)]),
                                  (c, [(before + 2, 2 * P, 2 * P, 0, True)])]
                else:
                    units += [(c, [(s, 0, w, 0, False), (s + 1, 0, w, w, False)]) for s in range(0, before, 2)]
                    if causal:
                        units += [(c, [(before, 0, w, 0, True), (before + 1, P, P, w, True)])]
            return units

        def maximum_units(causal):
            if causal:
                return [[(t, k0, min(w, (t + 1) * P - k0), 0, (t + 1) * P - k0 <= w)]
                        for t in range(NT) for k0, w in CH if k0 < (t + 1) * P]
            return ([[(t, k0, w, 0, False)] for t in range(NT) for k0, w in CH[0:2]]
                    + [[(t + r, CH[2][0], PB, r * PB, False) for r in range(2)] for t in range(0, NT, 2)])

        u0 = b0 = a0 = h0 = 0
        for at in ATT:
            at["units"], at["maxima"] = score_units(at["causal"]), maximum_units(at["causal"])
            at["u0"], at["b0"], at["a0"], at["h0"] = u0, b0, a0, h0
            nu, nm = len(at["units"]), len(at["maxima"])
            at["ends"] = {max(u for u in range(nu) if at["units"][u][0] == c): c for c in range(NC)}
            first, last = 4, nu - 5
            at["early"] = [list(range(nm * (u - first) // (last + 1 - first), nm * (u + 1 - first) // (last + 1 - first)))
                           if first <= u <= last else [] for u in range(nu)]
            u0, b0, a0, h0 = u0 + nu * H, b0 + NC * H, a0 + nm * H, h0 + H
        ATT_END = [dict(u=x["u0"] + len(x["units"]) * H, a=x["a0"] + len(x["maxima"]) * H, b=x["b0"] + NC * H)
                   for x in ATT]
        S_BANKS, M_BANKS, O_BANKS = (0, 1, 7), (2, 5), (3, 4)

        def operands(x, par):
            return [page[x["ring"]][:, 0:KD * N].bitcast(F16)[:, (4 * par + j) * N:(4 * par + j + 1) * N]
                    for j in range(4)]

        block = ctx.enter_context(nc.Block())

        @block.sync
        def _(sp):
            for s, v in ((f_act, NC), (f_lo, NC), (t_ev, 2), (ea_lo, 2), (e_mm, GE), (e_sum, GE), (e_hi, 2),
                         (e_lo, 2), (a_mx, 2), (s_mm, NT), (s_add, NT), (s_exp, 3), (s_plo, 2), (s_pv, 3), (o_ev, 2)):
                sp.sem_inc(s, v)
            sp.dma_start(vec[:], a["vec"]).then_inc(in_ld, 16)
            sp.dma_start(srcs, a["src_pt"]).then_inc(in_ld, 16)
            sp.dma_start(dsts, a["dst_pt"]).then_inc(in_ld, 16)
            sp.dma_start(grp_i, a["dst_g"]).then_inc(in_ld, 16)
            sp.dma_start(rowb[:], a["rowv"][0:1, :].to_broadcast([P, D])).then_inc(row_ld, 16)

            def load_weights(first, last, pick):
                for n in range(first, last):
                    i, k = CHUNKS[n]
                    _, name, expert, r0, c0, _, _, _ = UNITS[i]
                    if n >= 4:
                        sp.wait_ge(w_split, n - 3)
                    src = a[name]
                    if expert:
                        src = src[bass.ds(pick[expert], 1), r0 + 128 * k:r0 + 128 * k + 128, c0:c0 + D]
                        src = src.rearrange("a p n -> (a p) n")
                    else:
                        src = src[r0 + 128 * k:r0 + 128 * k + 128, c0:c0 + D]
                    sp.dma_start(stage[:, n % 4, :], src).then_inc(w_ld[n % 4], 16)

            load_weights(0, FIRST_AFTER_EDGES, {})
            sp.wait_ge(win_s, 3)
            sp.dma_start(win_d, gwi).then_inc(win_io, 16)
            sp.wait_ge(win_io, 16)
            sp.dma_start(win, win_d.rearrange("(o g) c -> o (g c)", o=1)).then_inc(win_io, 16)
            for j in range(NT):
                sp.wait_ge(t_ev, T_TILES["P"][0] + j + 1 + 2)
                sp.dma_start(proj_d[j * P:(j + 1) * P, :], rowst[0:P, j % 2, :]).then_inc(p_st[j % 2], 16)
            sp.wait_ge(f_mm, F_TILES["hT"][1])
            with sp.Fori(0, NG // 2) as i:
                for s in range(2):
                    sp.wait_ge(ea_lo, 2 * i + s + 1)
                    sp.dma_start(eas[:, s, :], a["eaT"][:, bass.ds((2 * i + s) * GW, GW)]).then_inc(ea_ld[s], 16)
            split_s = CHUNKS.index((UNIT["sq"], 0))
            ihz_at = CHUNKS.index((UNIT["ihz"], 0))
            load_weights(FIRST_AFTER_EDGES, ihz_at, {})
            sp.wait_ge(agg_done, 1)
            sp.wait_ge(f_mm, F_TILES["aggT"][1])
            sp.dma_start(b2f, a["rowv"][ROW["b2"]:ROW["b2"] + 1, :].to_broadcast([NT, D])).then_inc(b2_ld, 16)
            sp.dma_start(rw1, a["rw1T"].rearrange("(k p) n -> p k n", p=128)).then_inc(rw_ld, 16)
            sp.dma_start(rw2[:], a["rw2T"]).then_inc(rw_ld, 16)
            sp.dma_start(rb2[:], a["rb2"]).then_inc(rw_ld, 16)
            load_weights(ihz_at, split_s, {})
            sp.wait_ge(r_ix, 2)
            ps = sp.value_load(choice[0:1, 0:1], min_val=0, max_val=EXPERTS - 1)
            pt = sp.value_load(choice[0:1, 8:9], min_val=0, max_val=EXPERTS - 1)
            pick = {"s": ps, "t": pt}
            sp.dma_start(vsp[:], a["vsp"][bass.ds(ps, 1), :, :].rearrange("a p n -> (a p) n")).then_inc(eb_ld, 16)
            sp.dma_start(vtp[:], a["vtp"][bass.ds(pt, 1), :, :].rearrange("a p n -> (a p) n")).then_inc(eb_ld, 16)
            sp.wait_ge(t_ev, t_read("P"))
            sp.dma_start(rowb[:], a["svrow"][bass.ds(ps, 1), :].to_broadcast([P, D])).then_inc(row_ld, 16)
            tv_at = CHUNKS.index((UNIT["tv"], 0))
            load_weights(split_s, tv_at, pick)
            sp.wait_ge(t_ev, t_read("sv"))
            sp.dma_start(rowb[:], a["tvrow"][bass.ds(pt, 1), :].to_broadcast([P, D])).then_inc(row_ld, 16)
            cv_at = CHUNKS.index((UNIT["cv"], 0))
            load_weights(tv_at, cv_at, pick)
            sp.wait_ge(t_ev, t_read("tv"))
            sp.dma_start(rowb[:], a["rowv"][ROW["cv"]:ROW["cv"] + 1, :].to_broadcast([P, D])).then_inc(row_ld, 16)
            co_at = CHUNKS.index((UNIT["up0"], 0))
            load_weights(cv_at, co_at, pick)
            sp.wait_ge(t_ev, t_read("cv"))
            sp.dma_start(rowb[:], a["rowv"][ROW["cout"]:ROW["cout"] + 1, :].to_broadcast([P, D])).then_inc(row_ld, 16)
            load_weights(co_at, co_at + 4, pick)
            sp.wait_ge(y_st, 1)
            sp.dma_start(rowb[:], a["rowv"][ROW["m2"]:ROW["m2"] + 1, :].to_broadcast([P, D])).then_inc(row_ld, 16)
            load_weights(co_at + 4, len(CHUNKS), pick)
            for j in range(NT):
                sp.wait_ge(t_ev, T_TILES["down"][0] + j + 1 + 2)
                sp.dma_start(out[j * P:(j + 1) * P, :], rows(5)[:, j, :]).then_inc(o_st, 16)
            sp.wait_ge(o_st, 16 * NT)

        @block.gpsimd
        def _(pool):
            for j in range(NT):
                pool.dma_start(rows(1)[:, j, :], a["x"][j * P:(j + 1) * P, :]).then_inc(x_ld, 16)
            pool.memset(ident[:], 0.0).then_inc(pool_c, 1)
            pool.memset(blockdiag[:], 0.0).then_inc(pool_c, 1)
            pool.memset(tri, 1.0).then_inc(pool_c, 1)
            pool.iota(node_id[:], pattern=[[1, N]], base=0, channel_multiplier=0,
                      allow_small_or_imprecise_dtypes=True).then_inc(pool_c, 1)
            pool.wait_ge(pool_c, 4)
            pool.affine_select(out=ident[:], in_=ident[:], compare_op=ALU.not_equal, fill=1.0, base=0,
                               pattern=[[-1, 128]], channel_multiplier=1).then_inc(pool_c, 1)
            pool.affine_select(out=blockdiag[:], in_=blockdiag[:], compare_op=ALU.not_equal, fill=1.0, base=0,
                               pattern=[[-1, NT], [0, P]], channel_multiplier=1).then_inc(pool_c, 1)
            for o in range(2):
                pool.affine_select(out=tri[:, o, :], in_=tri[:, o, :], compare_op=ALU.is_ge, fill=0.0,
                                   base=-1 - o, pattern=[[1, NG]], channel_multiplier=-1).then_inc(pool_c, 1)

            def split_weights(first, last):
                for n in range(first, last):
                    i, k = CHUNKS[n]
                    scale = UNITS[i][6]
                    if k == 0 and i >= 4:
                        was = UNITS[i - 4][7]
                        if was in F_TILES:
                            pool.wait_ge(f_mm, F_TILES[was][1])
                        elif was in T_TILES:
                            pool.wait_ge(t_mm, T_TILES[was][1])
                    pool.wait_ge(w_ld[n % 4], 16 * (n // 4 + 1))
                    pool.tensor_scalar(stage[:, n % 4, :], stage[:, n % 4, :], scale, 1.0,
                                       ALU.mult, ALU.mult).then_inc(w_sc, 1)
                    pool.wait_ge(w_sc, n + 1)
                    pool.tensor_copy(slots[:, i % 4, 0, k, :], stage[:, n % 4, :]).then_inc(w_hi, 1)
                    pool.wait_ge(w_hi, n + 1)
                    pool.tensor_tensor(slots[:, i % 4, 1, k, :], stage[:, n % 4, :], slots[:, i % 4, 0, k, :],
                                       ALU.subtract).then_inc(w_split, 1)

            split_weights(0, FIRST_AFTER_EDGES)
            for s in range(2):
                pool.wait_ge(p_st[s], 16 * NT // 2)
            pool.wait_ge(in_ld, 64)
            with pool.Fori(0, NG // 2) as i:
                for s in range(2):
                    pool.wait_ge(e_sum, (2 * i + s) * GE)
                    pool.tensor_copy(idx_ring[:, s, :], srcs[:, bass.ds((2 * i + s) * GE, GE)]).then_inc(g_ix, 1)
                    pool.wait_ge(ea_hi, 2 * i + s + 1)
                    pool.wait_ge(g_ix, 2 * i + s + 1)
                    pool.tensor_tensor(eal[:, s, :], eas[:, s, :], eah[:, s, :], ALU.subtract).then_inc(ea_lo, 1)
                    for q in range(GE):
                        pool.indirect_dma_start(
                            gath[:, s * GE + q, :], None, proj_d,
                            bass.IndirectOffsetOnAxis(ap=idx_ring[:, s, q:q + 1], axis=0)).then_inc(g_ld[s * GE + q], 16)
            pool.wait_ge(e_lo, ET + 2)
            pool.memset(mask_s, 0.0).then_inc(pool_c, 1)
            pool.memset(mask_t, 0.0).then_inc(pool_c, 1)
            pool.wait_ge(pool_c, 10)
            pool.affine_select(out=mask_s, in_=mask_s, compare_op=ALU.is_ge, fill=MASKED, base=0,
                               pattern=[[1, P]], channel_multiplier=-1).then_inc(pool_c, 1)
            pool.affine_select(out=mask_t, in_=mask_t, compare_op=ALU.is_ge, fill=MASKED, base=0,
                               pattern=[[-1, P]], channel_multiplier=1).then_inc(pool_c, 1)
            split_weights(FIRST_AFTER_EDGES, len(CHUNKS))

        @block.tensor
        def _(pe):
            def f_gemm(name, units, start_waits):
                for s, v in start_waits:
                    pe.wait_ge(s, v)
                for u in units:
                    pe.wait_ge(w_split, SPLIT_AT[u[0]])
                g0 = F_TILES[name][0]
                with pe.Fori(0, KD) as i:
                    for c, (n0, w) in enumerate(CH):
                        pe.wait_ge(f_act, g0 + i * NC + c + 1)
                        todo = [(u, xp, s, r, k) for u, xp in units for k in range(KD)
                                for s, r in ((0, 0), (0, 1), (1, 0))]
                        for m, (u, xp, s, r, k) in enumerate(todo):
                            mm = pe.matmul(bank[c][:, 0:w], slots[:, SLOT[u], s, k, bass.ds(i * 128, 128)],
                                           split(xp)[:, r, k, n0:n0 + w], start=(m == 0), stop=(m == len(todo) - 1))
                        mm.then_inc(f_mm, 1)

            def f_transpose(name, src, start_waits):
                for s, v in start_waits:
                    pe.wait_ge(s, v)
                g0 = F_TILES[name][0]
                for k in range(KD):
                    for c, (n0, w) in enumerate(CH):
                        pe.wait_ge(f_act, g0 + k * NC + c + 1)
                        for q in range(w // P):
                            mm = pe.transpose(bank[c][:, q * P:(q + 1) * P],
                                              rows(src)[:, n0 // P + q, k * 128:(k + 1) * 128], ident[0:P, 0:P])
                        mm.then_inc(f_mm, 1)

            def t_gemm(name, pairs, start_waits):
                for s, v in start_waits:
                    pe.wait_ge(s, v)
                t0 = T_TILES[name][0]
                with pe.Fori(0, NT // 2) as i:
                    for b in range(2):
                        pe.wait_ge(t_ev, t0 + 2 * i + b + 1)
                        todo = [(x, u, k, s, r) for x, u in pairs for k in range(KD)
                                for s, r in ((0, 0), (0, 1), (1, 0))]
                        for m, (x, u, k, s, r) in enumerate(todo):
                            mm = pe.matmul(bank[3 + b][0:P, :], x(s, k, bass.ds((2 * i + b) * P, P)),
                                           slots[:, SLOT[u], r, k, :], start=(m == 0), stop=(m == len(todo) - 1))
                        mm.then_inc(t_mm, 1)

            def of(p):
                return lambda s, k, n: split(p)[:, s, k, n]

            pe.wait_ge(pool_c, 8)
            pe.wait_ge(win_s, 1)
            pe.matmul(bank[7][0:NG, 0:1], tri[:, 0, :], gw[:, 20:21], start=True, stop=True)
            pe.matmul(bank[7][0:NG, 1:2], tri[:, 1, :], gw[:, 20:21], start=True, stop=True).then_inc(win_s, 1)

            f_transpose("hT", 6, [(ln_out, 1)])
            pe.wait_ge(w_split, SPLIT_AT["w1a"])
            t_gemm("P", [(of(3), "w1a")], [(f_lo, f_split("hT"))])

            pe.wait_ge(w_split, SPLIT_AT["w1b"])
            pe.wait_ge(f_act, f_read("hT"))
            pe.wait_ge(dve_c, 1)
            pe.wait_ge(win_io, 32)

            def group(n0, s):
                pe.wait_ge(ea_lo, n0 + 1 + 2)
                for q in range(GE):
                    pe.wait_ge(e_sum, n0 * GE + q - 1 + GE)
                    for m, (x, wt) in enumerate(((eah, 0), (eah, 1), (eal, 0))):
                        mm = pe.matmul(bank[q % 2][0:P, :], x[:, s, q * P:(q + 1) * P],
                                       slots[:, SLOT["w1b"], wt, 0, :], start=(m == 0), stop=(m == 2))
                    mm.then_inc(e_mm, 1)

            def scatter(n0, s):
                first, end, number = (pe.value_load(win[:, bass.ds(n0 * 4 + c, 1)], min_val=lo, max_val=hi)
                                      for c, lo, hi in ((0, 0, NT - 1), (1, 1, NT), (2, 0, NG * NT + NT)))
                with pe.Fori(first, end) as j:
                    pe.wait_ge(e_lo, n0 * GE + GE + 2)
                    pe.wait_ge(s_add, number + j)
                    for q in range(GE):
                        member = onehot[:, s * GE + q, bass.ds(j * P, P)]
                        pe.matmul(bank[2][0:P, :], member, relu[:, s * GE + q, 0, :], start=(q == 0), stop=False)
                        pe.matmul(bank[2][0:P, :], member, relu[:, s * GE + q, 1, :], start=False, stop=(q == GE - 1))
                    for q in range(GE):
                        mm = pe.matmul(bank[5][0:P, 0:1], onehot[:, s * GE + q, bass.ds(j * P, P)], ones16[:],
                                       start=(q == 0), stop=(q == GE - 1))
                    mm.then_inc(s_mm, 1)

            group(0, 0)
            with pe.Fori(0, NG // 2 - 1) as i:
                group(2 * i + 1, 1)
                scatter(2 * i, 0)
                group(2 * i + 2, 0)
                scatter(2 * i + 1, 1)
            group(NG - 1, 1)
            scatter(NG - 2, 0)
            scatter(NG - 1, 1)

            pe.wait_ge(agg_done, 1)
            pe.transpose(bank[7][0:NT, 0:P], cnt[:], ident[0:P, 0:P]).then_inc(c_mt, 1)
            f_transpose("aggT", 5, [])
            pe.wait_ge(f_lo, f_split("aggT"))
            pe.wait_ge(c_s, 1)
            pe.wait_ge(w_split, SPLIT_AT["w2"])
            g0 = F_TILES["M"][0]
            with pe.Fori(0, KD) as i:
                for c, (n0, w) in enumerate(CH):
                    pe.wait_ge(f_act, g0 + i * NC + c + 1)
                    for m, (s, r) in enumerate(((0, 0), (0, 1), (1, 0))):
                        pe.matmul(bank[c][:, 0:w], b2h[:, s, bass.ds(i * 128, 128)], cnth[:, r, n0:n0 + w],
                                  start=(m == 0), stop=False)
                    for k in range(KD):
                        for s, r in ((0, 0), (0, 1), (1, 0)):
                            mm = pe.matmul(bank[c][:, 0:w], slots[:, SLOT["w2"], s, k, bass.ds(i * 128, 128)],
                                           split(4)[:, r, k, n0:n0 + w], start=False, stop=(k == KD - 1 and s == 1))
                    mm.then_inc(f_mm, 1)
            for gate in "rz":
                pe.wait_ge(w_split, SPLIT_AT["hh" + gate])
                f_gemm(gate, [("ih" + gate, 5), ("hh" + gate, 3)], [(f_lo, f_split("M"))])
            pe.wait_ge(w_split, SPLIT_AT["hhn"])
            g0 = F_TILES["n"][0]
            with pe.Fori(0, KD) as i:
                for c, (n0, w) in enumerate(CH):
                    pe.wait_ge(f_act, g0 + i * NC + c + 1)
                    for b, u, xp in ((0, "ihn", 5), (5, "hhn", 3)):
                        for k in range(KD):
                            for s, r in ((0, 0), (0, 1), (1, 0)):
                                mm = pe.matmul(bank[b + c][:, 0:w], slots[:, SLOT[u], s, k, bass.ds(i * 128, 128)],
                                               split(xp)[:, r, k, n0:n0 + w], start=(k == 0 and s == 0 and r == 0),
                                               stop=(k == KD - 1 and s == 1))
                    mm.then_inc(f_mm, 1)
            pe.wait_ge(n_new, KD * NC)
            t0 = T_TILES["x1"][0]
            for j in range(NT):
                pe.wait_ge(t_ev, t0 + j + 1)
                for k in range(KD):
                    mm = pe.transpose(bank[3 + j % 2][0:P, k * 128:(k + 1) * 128], cols(2)[:, k, j * P:(j + 1) * P], ident[:])
                mm.then_inc(t_mm, 1)

            pe.wait_ge(ln_out, 2)
            for k in range(KD):
                for j in range(NT):
                    mm = pe.matmul(bank[7][:, k:k + 1], rows(2)[:, j, k * 128:(k + 1) * 128], ones32[:],
                                   start=(j == 0), stop=(j == NT - 1))
            mm.then_inc(r_mm, 1)
            pe.wait_ge(r_act, 1)
            pe.wait_ge(rw_ld, 48)
            for k in range(KD):
                mm = pe.matmul(bank[7][:, 8:9], rw1[:, k, :], rs[:, k:k + 1], start=(k == 0), stop=(k == KD - 1))
            mm.then_inc(r_mm, 1)
            pe.wait_ge(r_act, 2)
            pe.matmul(bank[7][0:1, 16:24], rs[:, 4:5], rw2[:], start=True, stop=True).then_inc(r_mm, 1)

            f_transpose("xn", 3, [(ln_out, 3)])
            f_transpose("xt", 3, [])

            def qkv(at, x):
                n = at["n"]
                pe.wait_ge(w_split, SPLIT_AT[n + "k" if n == "c" else n + "q"])
                pe.wait_ge(f_lo, f_split({"s": "xn", "t": "cq", "c": "to"}[n]))
                if n != "c":
                    f_gemm(n + "q", [(n + "q", x)], [])
                f_gemm(n + "k", [(n + "k", x)], [])
                pe.wait_ge(w_split, SPLIT_AT[n + "v"])
                t_gemm(n + "v", [(of(x), n + "v")], [])

            def attention(a, x):
                v_high, v_low = value_highs_of(x), value_lows_of(x)
                units, nu, nm = x["units"], len(x["units"]), len(x["maxima"])
                firsts = {min(u for u in range(nu) if units[u][0] == c) for c in range(NC)}

                def maxima(h, par, e):
                    k_both, _, q_high, _ = operands(x, par)
                    n = x["a0"] + h * nm + e
                    b = bank[M_BANKS[(par * nm + e) % 2]]
                    pe.wait_ge(a_mx, n - 2 + 1 + 2)
                    todo = []
                    for t, k0, w, at, diagonal in x["maxima"][e]:
                        todo.append((b[0:P, at:at + w], q_high[0:HD, t * P:(t + 1) * P], k_both[0:HD, k0:k0 + w]))
                        if diagonal:
                            todo.append((b[0:P, at + w - P:at + w], gain16[0:P, 0:P], mask_t))
                    for m, (o, l, r) in enumerate(todo):
                        mm = pe.matmul(o, l, r, start=(m == 0), stop=(m == len(todo) - 1), skip_group_check=True)
                    mm.then_inc(a_mm, 1)

                def scores(h, par, u):
                    k_both, k_high, q_high, q_low = operands(x, par)
                    (c, pieces), v = units[u], par * nu + u
                    n = x["u0"] + h * nu + u
                    b = bank[S_BANKS[v % 3]]
                    pe.wait_ge(s_exp, n - since(v, 2 * nu, 3) + 1 + 3)
                    todo = []
                    for s, n0, w, at, diagonal in pieces:
                        t0 = CH[c][0] + n0
                        todo.append((b[0:P, at:at + w], k_both[:, s * P:(s + 1) * P], q_high[:, t0:t0 + w]))
                        todo.append((b[0:P, at:at + w], k_high[0:HD + NT, s * P:(s + 1) * P], q_low[0:HD + NT, t0:t0 + w]))
                        if diagonal:
                            todo.append((b[0:P, at:at + P], gain16[0:P, 0:P], mask_s))
                    for m, (o, l, r) in enumerate(todo):
                        mm = pe.matmul(o, l, r, start=(m == 0), stop=(m == len(todo) - 1), skip_group_check=True)
                    mm.then_inc(s_sc, 1)

                def weigh(h, par, u):
                    (c, pieces), v = units[u], par * nu + u
                    n = x["u0"] + h * nu + u
                    o = bank[O_BANKS[(par * NC + c) % 2]]
                    if u in firsts:
                        pe.wait_ge(o_ev, x["b0"] + NC * h + c - 2 + 1 + 2)
                    pe.wait_ge(s_plo, n + 1 + 2)
                    todo = []
                    for s, n0, w, at, _ in pieces:
                        ones = v_high[:, bass.ds(s * H * 128 + h * 128, 128)]
                        lows = v_low[:, bass.ds(s * H * HD + h * HD, HD)]
                        todo.append((o[:, n0:n0 + w], ones, probh[0:P, v % 3, at:at + w]))
                        todo.append((o[:, n0:n0 + w], ones, probl[0:P, v % 3, at:at + w]))
                        todo.append((o[0:HD, n0:n0 + w], lows, probh[0:P, v % 3, at:at + w]))
                    for m, (o_, l, r) in enumerate(todo):
                        mm = pe.matmul(o_, l, r, start=(u in firsts and m == 0),
                                       stop=(u in x["ends"] and m == len(todo) - 1), skip_group_check=True)
                    mm.then_inc(s_pv, 1)

                def big_loaded(i, par):
                    pe.wait_ge(big_ld[par], 64 * (4 * a + 1) + 64 * i)

                def small_loaded(i, par):
                    pe.wait_ge(small_ld[par], 32 * (4 * a + 1) + 32 * i)
                    pe.wait_ge(m_sh, x["h0"] + 2 * i + par + 1)

                def turn(h, par):
                    pe.wait_ge(m_all, x["h0"] + h + 1)
                    pe.transpose(bank[6][0:NT, 0:P], mx[:, par, :], ident[0:P, 0:P]).then_inc(m_t, 1)

                def head(i, par, following):
                    h, i_next = 2 * i + par, i + par
                    for u in range(nu):
                        if u + 2 < nu:
                            scores(h, par, u + 2)
                        elif following:
                            if u + 2 == nu:
                                small_loaded(i_next, 1 - par)
                            scores(h + 1, 1 - par, u + 2 - nu)
                        if following:
                            for e in x["early"][u]:
                                if e == 0:
                                    big_loaded(i_next, 1 - par)
                                maxima(h + 1, 1 - par, e)
                        weigh(h, par, u)
                        if following and u == nu - 4:
                            turn(h + 1, 1 - par)

                big_loaded(0, 0)
                for e in range(nm):
                    maxima(0, 0, e)
                turn(0, 0)
                pe.wait_ge(v_lo, (a + 1) * NT)
                pe.wait_ge(v_one, a + 1)
                pe.wait_ge(eight, a + 1)
                small_loaded(0, 0)
                for u in range(2):
                    scores(0, 0, u)
                with pe.Fori(0, H // 2 - 1) as i:
                    head(i, 0, True)
                    head(i, 1, True)
                head(H // 2 - 1, 0, True)
                head(H // 2 - 1, 1, False)

            def attention_over(k):
                return [(o_ev, ATT_END[k]["b"] + 2), (s_exp, ATT_END[k]["u"] + 3), (a_mx, ATT_END[k]["a"] + 2)]

            qkv(ATT[0], 4)
            pe.wait_ge(t_ev, t_read("sv"))
            attention(0, ATT[0])
            f_gemm("so", [("so", 4)], attention_over(0) + [(w_split, SPLIT_AT["so"])])
            f_gemm("cq", [("cq", 1)], [(f_lo, f_split("so")), (w_split, SPLIT_AT["cq"])])
            qkv(ATT[1], 5)
            pe.wait_ge(pool_c, 12)
            pe.wait_ge(t_ev, t_read("tv"))
            attention(1, ATT[1])
            f_gemm("to", [("to", 5)], attention_over(1) + [(w_split, SPLIT_AT["to"])])
            qkv(ATT[2], 4)
            pe.wait_ge(t_ev, t_read("cv"))
            attention(2, ATT[2])
            t_gemm("co", [(of(4), "co")], attention_over(2) + [(w_split, SPLIT_AT["co"])])
            f_transpose("h2", 3, [(ln_out, 4)])
            for i in range(4):
                f_gemm(f"up{i}", [(f"up{i}", 6)], [(f_lo, f_split("h2")), (w_split, SPLIT_AT[f"up{i}"])])
            t_gemm("down", [(lambda s, k, n, i=i: wide[s][:, 4 * i + k, n], f"down{i}") for i in range(4)],
                   [(f_lo, f_split("up3")), (w_split, SPLIT_AT["down3"])])

        @block.scalar
        def _(act):
            def f_tile(name, i, c, w, t_dst, hi_dst, func, scale, bias):
                g, lw = F_TILES[name][0] + i * NC + c, LOWS[name][0] + i * NC + c
                act.wait_ge(f_mm, g + 1)
                act.wait_ge(f_lo, lw + 1)
                act.activation(t_dst, bank[c][:, 0:w], func, bias=bias, scale=scale)
                act.activation(hi_dst, bank[c][:, 0:w], func, bias=bias, scale=scale).then_inc(f_act, 1)

            def f_evac(name, dst, scale, bias, func=ACT.Identity):
                with act.Fori(0, KD) as i:
                    for c, (n0, w) in enumerate(CH):
                        f_tile(name, i, c, w, t32[:, c, 0:w], dst(0, i, n0, w), func, scale, bias(i))

            def page_of(p):
                return lambda s, i, n0, w: page[p][:, 0:KD * N].bitcast(F16)[:, bass.ds(i * N + s * KD * N + n0, w)]

            def layer_norm_sd(k):
                act.wait_ge(ln_var, k)
                act.activation(rstd[:], rstd[:], ACT.Sqrt).then_inc(ln_sd, 1)

            def vecs(name):
                return lambda i: vcol(name, i)

            act.wait_ge(ln_var, 1)
            act.activation(bns[:, 0, :], bns[:, 0, :], ACT.Sqrt)
            layer_norm_sd(1)
            for k in range(KD):
                for c, (n0, w) in enumerate(CH):
                    f_tile("hT", k, c, w, cols(2)[:, k, n0:n0 + w], split(3)[:, 0, k, n0:n0 + w], ACT.Identity, 1.0, 0.0)

            def attributes(n0, s):
                act.wait_ge(ea_ld[s], 16 * ((n0 - s) // 2 + 1) if isinstance(n0, int) else n0[1])
                n0 = n0 if isinstance(n0, int) else n0[0]
                act.wait_ge(e_mm, n0 * GE)
                act.activation(eah[:, s, :], eas[:, s, :], ACT.Copy).then_inc(ea_hi, 1)

            def relus(n0, s):
                behind = act.value_load(win[:, bass.ds(n0 * 4 + 3, 1)], min_val=0, max_val=NG * NT + NT)
                act.wait_ge(s_mm, behind)
                for q in range(GE):
                    n = n0 * GE + q
                    act.wait_ge(e_sum, n + 1 + GE)
                    act.activation(relu[:, s * GE + q, 0, :], esum[:, q % 2, :], ACT.Relu).then_inc(e_hi, 1)

            act.wait_ge(win_io, 32)
            attributes(0, 0)
            with act.Fori(0, NG // 2 - 1) as i:
                attributes((2 * i + 1, 16 * (i + 1)), 1)
                relus(2 * i, 0)
                attributes((2 * i + 2, 16 * (i + 2)), 0)
                relus(2 * i + 1, 1)
            attributes(NG - 1, 1)
            relus(NG - 2, 0)
            relus(NG - 1, 1)

            f_evac("aggT", page_of(4), 1.0, lambda i: 0.0)
            f_evac("M", page_of(5), 1.0 / SG, lambda i: 0.0)
            for gate, p, b in (("r", 6, 0), ("z", 7, KD)):
                with act.Fori(0, KD) as i:
                    for c, (n0, w) in enumerate(CH):
                        act.wait_ge(f_mm, F_TILES[gate][0] + i * NC + c + 1)
                        act.activation(page[p][:, bass.ds(i * N + n0, w)], bank[c][:, 0:w], ACT.Sigmoid,
                                       bias=bsum[:, bass.ds(i + b, 1)], scale=1.0 / SG).then_inc(f_act, 1)
            with act.Fori(0, KD) as i:
                for c, (n0, w) in enumerate(CH):
                    act.wait_ge(n_hr, i * NC + c + 1)
                    act.activation(t32[:, c, 0:w], t32[:, c, 0:w], ACT.Tanh, bias=vcol("b_ih", i + 2 * KD),
                                   scale=1.0 / SG).then_inc(f_act, 1)

            act.wait_ge(t_ev, t_read("x1"))
            act.dma_start(x1_d, page[1][0:P, 0:NT * D]).then_inc(sp_io, 16)
            layer_norm_sd(2)
            layer_norm_sd(3)
            act.wait_ge(ln_out, 2)
            act.dma_start(xl_d, page[2][0:P, 0:NT * D]).then_inc(sp_io, 16)
            act.wait_ge(r_mm, 1)
            act.activation(rs[:, 0:KD], bank[7][:, 0:KD], ACT.Copy, scale=1.0 / N).then_inc(r_act, 1)
            act.wait_ge(r_mm, 2)
            act.activation(rs[:, 4:5], bank[7][:, 8:9], ACT.Gelu, bias=vcol("rb1")).then_inc(r_act, 1)

            for name, hi, w_, b_ in (("xn", 4, "ns_w", "ns_b"), ("xt", 5, "nt_w", "nt_b")):
                for k in range(KD):
                    for c, (n0, w) in enumerate(CH):
                        f_tile(name, k, c, w, t32[:, c, 0:w] if name == "xn" else cols(6)[:, k, n0:n0 + w],
                               split(hi)[:, 0, k, n0:n0 + w], ACT.Identity, vcol(w_, k), vcol(b_, k))
            act.wait_ge(f_act, f_read("xt"))
            act.dma_start(xt_d, page[6][:, 0:KD * N]).then_inc(sp_io, 16)

            def load_operands(x, i, par):
                k_both, k_high, q_high, q_low = operands(x, par)

                def part(src, hi_lo):
                    return page[src][64 * par:64 * par + 64, 0:KD * N].bitcast(F16)[:, bass.ds(i * N + hi_lo * KD * N, N)]

                for dst, src in ((k_both[0:64, :], part(x["k"], 0)), (k_both[64:128, :], part(x["k"], 1)),
                                 (q_high[0:64, :], part(x["q"], 0)), (q_high[64:128, :], part(x["q"], 0))):
                    act.dma_start(dst, src).then_inc(big_ld[par], 16)
                for dst, src in ((k_high[0:64, :], part(x["k"], 0)), (q_low[0:64, :], part(x["q"], 1))):
                    act.dma_start(dst, src).then_inc(small_ld[par], 16)

            def value_highs(x, a):
                t0 = T_TILES[x["n"] + "v"][0]
                with act.Fori(0, NT // 2) as i:
                    for b in range(2):
                        act.wait_ge(t_ev, t0 + 2 * i + b + 1 + 2)
                        act.activation(
                            value_highs_of(x)[:, bass.ds((2 * i + b) * H * 128, H * 128)].rearrange(
                                "p (h c) -> p h c", h=H)[:, :, 0:HD],
                            rowst[0:P, b, :].rearrange("p (h c) -> p h c", h=H), ACT.Copy).then_inc(v_hi, 1)

            def exponentials(x):
                nu = len(x["units"])

                def head(i, par, following):
                    for u in range(nu):
                        v = par * nu + u
                        n = x["u0"] + (2 * i + par) * nu + u
                        w = sum(piece[2] for piece in x["units"][u][1])
                        b = bank[S_BANKS[v % 3]]
                        act.wait_ge(s_sc, n + 1)
                        act.wait_ge(s_plo, n - 2 + 1 + 2)
                        act.activation(prob32[0:P, v % 2, 0:w], b[0:P, 0:w], ACT.Exp, scale=QK_SCALE)
                        act.wait_ge(s_pv, n - since(v, 2 * nu, 3) + 1 + 3)
                        act.activation(probh[0:P, v % 3, 0:w], b[0:P, 0:w], ACT.Exp, scale=QK_SCALE).then_inc(s_exp, 1)
                        if u == 0 and following:
                            load_operands(x, i + par, 1 - par)

                with act.Fori(0, H // 2 - 1) as i:
                    head(i, 0, True)
                    head(i, 1, True)
                head(H // 2 - 1, 0, True)
                head(H // 2 - 1, 1, False)

            def split_written(name):
                act.wait_ge(f_lo, f_split(name))
                act.wait_ge(f_act, f_read(name))

            x = ATT[0]
            act.wait_ge(eb_ld, 32)
            f_evac("sq", page_of(7), 1.0 / SF, lambda i: vsp[:, bass.ds(i, 1)])
            f_evac("sk", page_of(3), 1.0 / SF, lambda i: vsp[:, bass.ds(i + KD, 1)])
            split_written("sk")
            act.wait_ge(sp_io, 48)
            load_operands(x, 0, 0)
            value_highs(x, 0)
            exponentials(x)
            f_evac("so", page_of(1), 1.0 / SF, lambda i: vsp[:, bass.ds(i + 2 * KD, 1)])
            f_evac("cq", page_of(2), 1.0 / SF, vecs("cq_b"))
            x = ATT[1]
            f_evac("tq", page_of(1), 1.0 / SF, lambda i: vtp[:, bass.ds(i, 1)])
            f_evac("tk", page_of(6), 1.0 / SF, lambda i: vtp[:, bass.ds(i + KD, 1)])
            split_written("tk")
            load_operands(x, 0, 0)
            value_highs(x, 1)
            exponentials(x)
            act.wait_ge(small_ld[1], 32 * 8)
            act.dma_start(page[1][:, 0:KD * N], xt_d).then_inc(back, 16)
            with act.Fori(0, KD) as i:
                for c, (n0, w) in enumerate(CH):
                    act.wait_ge(to_sum, i * NC + c + 1)
                    act.activation(page_of(4)(0, i, n0, w), t32[:, c, 0:w], ACT.Identity,
                                   bias=vtp[:, bass.ds(i + 2 * KD, 1)]).then_inc(f_act, 1)
            x = ATT[2]
            act.wait_ge(f_mm, F_TILES["to"][1])
            act.dma_start(page[5][0:P, 0:NT * D], xl_d).then_inc(back, 16)
            f_evac("ck", page_of(1), 1.0 / SF, vecs("ck_b"))
            split_written("ck")
            load_operands(x, 0, 0)
            value_highs(x, 2)
            exponentials(x)
            act.wait_ge(small_ld[1], 32 * 12)
            act.dma_start(page[2][0:P, 0:NT * D], x1_d).then_inc(back_x1, 16)
            layer_norm_sd(4)
            for k in range(KD):
                for c, (n0, w) in enumerate(CH):
                    f_tile("h2", k, c, w, t32[:, c, 0:w], split(6)[:, 0, k, n0:n0 + w], ACT.Identity,
                           vcol("nm_w", k), vcol("nm_b", k))
            act.wait_ge(xs_done, 1)
            for m in range(4):
                f_evac(f"up{m}", lambda s, i, n0, w: hidden(s, m, i, n0, w), 1.0 / SF,
                       lambda i: vcol("m1_b", i + 4 * m), ACT.Gelu)

        @block.vector
        def _(dve):
            class Chain:
                start, k = 0, 0

            chain = Chain()

            def link(ins):
                chain.k += 1
                ins.then_inc(link_s, 1)
                dve.wait_ge(link_s, chain.start + chain.k)

            def layer_norm(k, src, dst):
                for j in range(NT):
                    last = dve.bn_stats(stats[:, j, :], rows(src)[:, j, :])
                link(last)
                for j in range(NT):
                    last = dve.bn_aggr(mv[:, j, :], stats[:, j, :])
                link(last)
                dve.tensor_scalar(rstd[:], mv[:, :, 1], EPS, None, ALU.add).then_inc(ln_var, 1)
                dve.wait_ge(ln_sd, k)
                link(dve.reciprocal(rstd[:], rstd[:]))
                for j in range(NT):
                    last = dve.tensor_scalar(rows(dst)[:, j, :], rows(src)[:, j, :], mv[:, j, 0:1], rstd[:, j:j + 1],
                                             ALU.subtract, ALU.mult)
                last.then_inc(ln_out, 1)
                dve.wait_ge(ln_out, k)

            def low(name, i, c, w, t_src, hi_src, lo_dst):
                dve.wait_ge(f_act, F_TILES[name][0] + i * NC + c + 1 + NC)
                dve.tensor_tensor(lo_dst, t_src, hi_src, ALU.subtract).then_inc(f_lo, 1)

            def page_of(p):
                return lambda s, i, n0, w: page[p][:, 0:KD * N].bitcast(F16)[:, bass.ds(i * N + s * KD * N + n0, w)]

            def f_lows(name, dst):
                with dve.Fori(0, KD) as i:
                    for c, (n0, w) in enumerate(CH):
                        low(name, i, c, w, t32[:, c, 0:w], dst(0, i, n0, w), dst(1, i, n0, w))

            dve.memset(ones16[:], 1.0)
            dve.memset(ones32[:], 1.0)
            dve.memset(rows(5), 0.0)
            dve.memset(lg[:], -3e38)
            link(dve.memset(cnt[:], 0.0))
            dve.wait_ge(pool_c, 8)
            dve.tensor_scalar(gain16[:], ident[:], MASK_GAIN, None, ALU.mult).then_inc(dve_c, 1)

            dve.wait_ge(in_ld, 64)
            dve.tensor_copy(dstf, dsts)
            link(dve.tensor_copy(grp_f, grp_i))
            dve.tensor_reduce(gw[:, 0:1], grp_f, AX.X, ALU.min)
            link(dve.tensor_reduce(gw[:, 1:2], grp_f, AX.X, ALU.max))
            edges_of_tiles = node_id[0:NG, P:N:P]
            for q in range(2):
                last = dve.tensor_scalar(gw[:, 2 + 9 * q:11 + 9 * q], edges_of_tiles, gw[:, q:q + 1], None, ALU.is_le)
            link(last)
            for q in range(2):
                last = dve.tensor_reduce(gw[:, 21 + q:22 + q], gw[:, 2 + 9 * q:11 + 9 * q], AX.X, ALU.add)
            link(last)
            link(dve.tensor_scalar(gw[:, 23:24], gw[:, 22:23], 1.0, None, ALU.add))
            dve.tensor_tensor(gw[:, 20:21], gw[:, 23:24], gw[:, 21:22], ALU.subtract).then_inc(win_s, 1)
            dve.wait_ge(win_s, 2)
            dve.tensor_copy(gwi[:, 0:1], gw[:, 21:22])
            dve.tensor_copy(gwi[:, 1:2], gw[:, 23:24])
            link(dve.tensor_scalar(gw[:, 24:26], bank[7][0:NG, 0:2], float(NT), None, ALU.add))
            link(dve.tensor_tensor(gw[:, 24:25], gw[:, 24:25], gw[:, 21:22], ALU.subtract))
            dve.tensor_copy(gwi[:, 2:4], gw[:, 24:26]).then_inc(win_s, 1)

            dve.tensor_tensor(bsum[:, 0:8], vec[:, VEC["b_ih"][0]:VEC["b_ih"][0] + 8],
                              vec[:, VEC["b_hh"][0]:VEC["b_hh"][0] + 8], ALU.add)
            dve.tensor_scalar(bsum[:, 8:12], vec[:, VEC["b_hh"][0] + 8:VEC["b_hh"][0] + 12], SG, None, ALU.mult)

            v0 = VEC["gamma"][0]
            dve.tensor_scalar(bns[:, 0, :], vec[:, v0 + 12:v0 + 16], EPS, None, ALU.add)

            dve.wait_ge(x_ld, 16 * NT)
            layer_norm(1, 1, 6)
            for k in range(KD):
                for c, (n0, w) in enumerate(CH):
                    low("hT", k, c, w, cols(2)[:, k, n0:n0 + w], split(3)[:, 0, k, n0:n0 + w],
                        split(3)[:, 1, k, n0:n0 + w])
            dve.wait_ge(row_ld, 16)
            t0 = T_TILES["P"][0]
            with dve.Fori(0, NT // 2) as i:
                for b in range(2):
                    dve.wait_ge(t_mm, t0 + 2 * i + b + 1)
                    dve.wait_ge(p_st[b], 16 * i)
                    dve.scalar_tensor_tensor(out=rowst[0:P, b, :], in0=bank[3 + b][0:P, :], scalar=1.0 / SG,
                                             in1=rowb[:], op0=ALU.mult, op1=ALU.add).then_inc(t_ev, 1)

            def tiles(n0, s, gath_done):
                behind = dve.value_load(win[:, bass.ds(n0 * 4 + 3, 1)], min_val=0, max_val=NG * NT + NT)
                dve.wait_ge(s_mm, behind)

                def relu_low(q):
                    dve.wait_ge(e_hi, n0 * GE + q + 1 + 2)
                    dve.scalar_tensor_tensor(out=relu[:, s * GE + q, 1, :], in0=esum[:, q % 2, :], scalar=0.0,
                                             in1=relu[:, s * GE + q, 0, :], op0=ALU.max,
                                             op1=ALU.subtract).then_inc(e_lo, 1)

                for q in range(GE):
                    n = n0 * GE + q
                    dve.wait_ge(e_mm, n + 1 + GE)
                    dve.wait_ge(g_ld[s * GE + q], gath_done)
                    dve.wait_ge(e_lo, n + 1)
                    dve.scalar_tensor_tensor(out=esum[:, q % 2, :], in0=bank[q % 2][0:P, :], scalar=1.0 / SG,
                                             in1=gath[:, s * GE + q, :], op0=ALU.mult, op1=ALU.add).then_inc(e_sum, 1)
                    dve.tensor_scalar(onehot[:, s * GE + q, :], node_id[:], dstf[:, bass.ds(n, 1)], None, ALU.is_equal)
                    if q >= 1:
                        relu_low(q - 1)
                relu_low(GE - 1)

            def windows(n0):
                first, end, number = (dve.value_load(win[:, bass.ds(n0 * 4 + c, 1)], min_val=lo, max_val=hi)
                                      for c, lo, hi in ((0, 0, NT - 1), (1, 1, NT), (2, 0, NG * NT + NT)))
                with dve.Fori(first, end) as j:
                    dve.wait_ge(s_mm, number + j + 1)
                    dve.wait_ge(s_add, number + j)
                    dve.tensor_tensor(page[5][0:P, bass.ds(j * D, D)], page[5][0:P, bass.ds(j * D, D)],
                                      bank[2][0:P, :], ALU.add)
                    dve.tensor_tensor(cnt[:, bass.ds(j, 1)], cnt[:, bass.ds(j, 1)], bank[5][0:P, 0:1],
                                      ALU.add).then_inc(s_add, 1)

            dve.wait_ge(win_io, 32)
            tiles(0, 0, 16)
            with dve.Fori(0, NG // 2 - 1) as i:
                tiles(2 * i + 1, 1, 16 * (i + 1))
                windows(2 * i)
                tiles(2 * i + 2, 0, 16 * (i + 2))
                windows(2 * i + 1)
            tiles(NG - 1, 1, 16 * (NG // 2))
            windows(NG - 2)
            windows(NG - 1)
            dve.memset(stats[:], 0.0).then_inc(agg_done, 1)

            f_lows("aggT", page_of(4))
            dve.wait_ge(c_mt, 1)
            dve.wait_ge(b2_ld, 16)
            link(dve.tensor_tensor(cntb.rearrange("p (a b) -> p a b", a=NT),
                                   bank[7][0:NT, 0:P].unsqueeze(1).to_broadcast([NT, NT, P]), blockdiag[:], ALU.mult))
            link(dve.tensor_scalar(b2f, b2f, SG, None, ALU.mult))
            dve.tensor_copy(cnth[:, 0, :], cntb)
            link(dve.tensor_copy(b2h[:, 0, :], b2f))
            link(dve.tensor_tensor(cnth[:, 1, :], cntb, cnth[:, 0, :], ALU.subtract))
            dve.tensor_tensor(b2h[:, 1, :], b2f, b2h[:, 0, :], ALU.subtract).then_inc(c_s, 1)
            f_lows("M", page_of(5))
            link(dve.reciprocal(bns[:, 0, :], bns[:, 0, :]))
            link(dve.tensor_tensor(bns[:, 0, :], bns[:, 0, :], vec[:, v0:v0 + 4], ALU.mult))
            link(dve.tensor_tensor(bns[:, 1, :], bns[:, 0, :], vec[:, v0 + 8:v0 + 12], ALU.mult))
            link(dve.tensor_tensor(bns[:, 1, :], vec[:, v0 + 4:v0 + 8], bns[:, 1, :], ALU.subtract))

            def new_front(i, c, n0, w):
                dve.wait_ge(f_mm, F_TILES["n"][0] + i * NC + c + 1)
                r = page[6][:, bass.ds(i * N + n0, w)]
                link(dve.scalar_tensor_tensor(out=t32[:, c, 0:w], in0=bank[5 + c][:, 0:w],
                                              scalar=bsum[:, bass.ds(i + 8, 1)], in1=r, op0=ALU.add, op1=ALU.mult))
                dve.tensor_tensor(t32[:, c, 0:w], t32[:, c, 0:w], bank[c][:, 0:w], ALU.add).then_inc(n_hr, 1)

            def new_back(i, c, n0, w):
                h, d, z = (page[p][:, bass.ds(i * N + n0, w)] for p in (2, 6, 7))
                dve.wait_ge(f_act, F_TILES["n"][0] + i * NC + c + 1 + NC)
                link(dve.tensor_tensor(d, h, t32[:, c, 0:w], ALU.subtract))
                link(dve.tensor_tensor(d, d, z, ALU.mult))
                link(dve.tensor_tensor(d, d, t32[:, c, 0:w], ALU.add))
                link(dve.tensor_scalar(d, d, bns[:, 0, bass.ds(i, 1)], bns[:, 1, bass.ds(i, 1)], ALU.mult, ALU.add))
                dve.tensor_tensor(h, h, d, ALU.add).then_inc(n_new, 1)

            base = chain.start + chain.k
            links = 5 * NC
            dve.wait_ge(f_act, f_read("z"))
            with dve.Fori(0, KD) as i:
                chain.start, chain.k = base + i * links, 0
                for c, (n0, w) in enumerate(CH):
                    new_front(i, c, n0, w)
                    if c:
                        new_back(i, c - 1, *CH[c - 1])
                new_back(i, NC - 1, *CH[NC - 1])
                assert chain.k == links
            chain.start, chain.k = base + KD * links, 0

            t0 = T_TILES["x1"][0]
            for j in range(NT):
                dve.wait_ge(t_mm, t0 + j + 1)
                dve.tensor_tensor(rows(1)[:, j, :], rows(1)[:, j, :], bank[3 + j % 2][0:P, :], ALU.add).then_inc(t_ev, 1)
            dve.wait_ge(t_ev, t_read("x1"))
            layer_norm(2, 1, 2)
            layer_norm(3, 2, 3)
            dve.wait_ge(r_mm, 3)
            link(dve.tensor_tensor(lg[:, 0:8], bank[7][0:1, 16:24], rb2[:], ALU.add))
            dve.tensor_copy(lg[:, 8:12], lg[:, 0:4])
            link(dve.tensor_copy(lg[:, 16:20], lg[:, 4:8]))
            dve.max(lg[:, 24:32], lg[:, 8:16])
            link(dve.max(lg[:, 32:40], lg[:, 16:24]))
            dve.max_index(choice[:, 0:8], lg[:, 24:32], lg[:, 8:16]).then_inc(r_ix, 1)
            dve.max_index(choice[:, 8:16], lg[:, 32:40], lg[:, 16:24]).then_inc(r_ix, 1)

            for name, p in (("xn", 4), ("xt", 5)):
                for k in range(KD):
                    for c, (n0, w) in enumerate(CH):
                        low(name, k, c, w, t32[:, c, 0:w] if name == "xn" else cols(6)[:, k, n0:n0 + w],
                            split(p)[:, 0, k, n0:n0 + w], split(p)[:, 1, k, n0:n0 + w])

            def value_rows(x, a):
                t0 = T_TILES[x["n"] + "v"][0]
                dve.wait_ge(row_ld, 16 * (a + 2))
                dve.memset(value_highs_of(x).rearrange("p (s c) -> p s c", c=128)[:, :, HD:128], 1.0).then_inc(v_one, 1)
                for par in range(2):
                    last = dve.memset(operands(x, par)[1][HD:HD + NT, :], 1.0 / QK_SCALE)
                last.then_inc(eight, 1)
                with dve.Fori(0, NT // 2) as i:
                    dve.wait_ge(v_lo, a * NT + 2 * i)
                    for b in range(2):
                        dve.wait_ge(t_mm, t0 + 2 * i + b + 1)
                        dve.scalar_tensor_tensor(out=rowst[0:P, b, :], in0=bank[3 + b][0:P, :], scalar=1.0 / SF,
                                                 in1=rowb[:], op0=ALU.mult, op1=ALU.add).then_inc(t_ev, 1)
                    for b in range(2):
                        v = value_highs_of(x)[:, bass.ds((2 * i + b) * H * 128, H * 128)].rearrange(
                            "p (h c) -> p h c", h=H)
                        dve.wait_ge(v_hi, a * NT + 2 * i + b + 1)
                        dve.wait_ge(t_ev, t0 + 2 * i + b + 1 + 2)
                        dve.tensor_tensor(value_lows_of(x)[:, bass.ds((2 * i + b) * H * HD, H * HD)].rearrange(
                            "p (h c) -> p h c", h=H), rowst[0:P, b, :].rearrange("p (h c) -> p h c", h=H),
                            v[:, :, 0:HD], ALU.subtract).then_inc(v_lo, 1)

            def attention(x):
                units, nu, nm = x["units"], len(x["units"]), len(x["maxima"])

                def prob_low(h, par, u):
                    n, v = x["u0"] + h * nu + u, par * nu + u
                    w = sum(piece[2] for piece in units[u][1])
                    dve.wait_ge(s_exp, n + 1 + 3)
                    dve.tensor_tensor(probl[0:P, v % 3, 0:w], prob32[0:P, v % 2, 0:w], probh[0:P, v % 3, 0:w],
                                      ALU.subtract).then_inc(s_plo, 1)

                def maxima(h, par, e):
                    pieces = x["maxima"][e]
                    t, k0, w, _, _ = pieces[0]
                    b = bank[M_BANKS[(par * nm + e) % 2]]
                    dve.wait_ge(a_mm, x["a0"] + h * nm + e + 1)
                    dve.tensor_reduce(mxs[:, par, t:t + len(pieces), k0 // 500],
                                      b[0:P, 0:len(pieces) * w].rearrange("p (a n) -> p a n", a=len(pieces)), AX.X,
                                      ALU.max).then_inc(a_mx, 1)

                def all_maxima(h, par):
                    dve.wait_ge(a_mx, x["a0"] + h * nm + nm + 2)
                    dve.tensor_reduce(mx[:, par, :], mxs[:, par, :, :], AX.X, ALU.max).then_inc(m_all, 1)

                def shifts(h, par):
                    dve.wait_ge(m_t, x["h0"] + h + 1)
                    dve.scalar_tensor_tensor(
                        out=operands(x, par)[3][HD:HD + NT, :].rearrange("p (a b) -> p a b", a=NT),
                        in0=bank[6][0:NT, 0:P].unsqueeze(1).to_broadcast([NT, NT, P]), scalar=-QK_SCALE,
                        in1=blockdiag[:], op0=ALU.mult, op1=ALU.mult).then_inc(m_sh, 1)

                def output(i, par, u):
                    c = x["ends"][u]
                    n0, w = CH[c]
                    at = slice(64 * par, 64 * par + 64)
                    o = bank[O_BANKS[(par * NC + c) % 2]]
                    dst = page[x["o"]][at, 0:KD * N].bitcast(F16)
                    hi, lo = (dst[:, bass.ds(i * N + (p * KD * N + n0), w)] for p in range(2))
                    dve.wait_ge(s_pv, x["u0"] + (2 * i + par) * nu + u + 1 + 3)
                    link(dve.reciprocal(rden[at, 0:w], o[64:128, 0:w]))
                    link(dve.tensor_tensor(onorm[at, 0:w], o[0:64, 0:w], rden[at, 0:w], ALU.mult))
                    link(dve.tensor_copy(hi, onorm[at, 0:w]))
                    dve.tensor_tensor(lo, onorm[at, 0:w], hi, ALU.subtract).then_inc(o_ev, 1)
                    dve.wait_ge(o_ev, x["b0"] + NC * (2 * i + par) + c + 1 + 2)

                def head(i, par, following):
                    h = 2 * i + par
                    for u in range(nu):
                        if u + 1 < nu:
                            prob_low(h, par, u + 1)
                        elif following:
                            prob_low(h + 1, 1 - par, 0)
                        if following:
                            for e in x["early"][u]:
                                maxima(h + 1, 1 - par, e)
                            if u == nu - 5:
                                all_maxima(h + 1, 1 - par)
                        if u in x["ends"]:
                            output(i, par, u)
                        if following and u == nu - 4:
                            shifts(h + 1, 1 - par)

                link(dve.memset(mxs[:], -3e38))
                for e in range(nm):
                    maxima(0, 0, e)
                all_maxima(0, 0)
                shifts(0, 0)
                prob_low(0, 0, 0)
                base = chain.start + chain.k
                links = 2 * 3 * NC
                with dve.Fori(0, H // 2 - 1) as i:
                    chain.start, chain.k = base + i * links, 0
                    head(i, 0, True)
                    head(i, 1, True)
                    assert chain.k == links
                chain.start, chain.k = base + (H // 2 - 1) * links, 0
                head(H // 2 - 1, 0, True)
                head(H // 2 - 1, 1, False)

            f_lows("sq", page_of(7))
            f_lows("sk", page_of(3))
            dve.wait_ge(sp_io, 48)
            value_rows(ATT[0], 0)
            attention(ATT[0])
            f_lows("so", page_of(1))
            f_lows("cq", page_of(2))
            f_lows("tq", page_of(1))
            f_lows("tk", page_of(6))
            value_rows(ATT[1], 1)
            attention(ATT[1])
            dve.wait_ge(back, 16)
            g0, l0 = F_TILES["to"][0], LOWS["to"][0]
            with dve.Fori(0, KD) as i:
                for c, (n0, w) in enumerate(CH):
                    dve.wait_ge(f_mm, g0 + i * NC + c + 1)
                    dve.wait_ge(f_lo, l0 + i * NC + c + 1)
                    dve.scalar_tensor_tensor(out=t32[:, c, 0:w], in0=bank[c][:, 0:w], scalar=1.0 / SF,
                                             in1=page[1][:, bass.ds(i * N + n0, w)], op0=ALU.mult,
                                             op1=ALU.add).then_inc(to_sum, 1)
                for c, (n0, w) in enumerate(CH):
                    dve.wait_ge(f_act, g0 + i * NC + c + 1 + NC)
                    dve.scalar_tensor_tensor(out=page_of(4)(1, i, n0, w), in0=t32[:, c, 0:w],
                                             scalar=vtp[:, bass.ds(i + 2 * KD, 1)], in1=page_of(4)(0, i, n0, w),
                                             op0=ALU.add, op1=ALU.subtract).then_inc(f_lo, 1)
            f_lows("ck", page_of(1))
            value_rows(ATT[2], 2)
            attention(ATT[2])
            dve.wait_ge(back, 32)
            dve.wait_ge(row_ld, 16 * 5)
            for j in range(NT):
                last = dve.tensor_tensor(rows(5)[:, j, :], rows(5)[:, j, :], rowb[:], ALU.add)
            last.then_inc(y_st, 1)
            dve.wait_ge(y_st, 1)
            t0 = T_TILES["co"][0]
            with dve.Fori(0, NT // 2) as i:
                for b in range(2):
                    dve.wait_ge(t_mm, t0 + 2 * i + b + 1)
                    y = page[5][0:P, bass.ds((2 * i + b) * D, D)]
                    dve.scalar_tensor_tensor(out=y, in0=bank[3 + b][0:P, :], scalar=1.0 / SF, in1=y, op0=ALU.mult,
                                             op1=ALU.add).then_inc(t_ev, 1)
            dve.wait_ge(t_ev, t_read("co"))
            layer_norm(4, 5, 3)
            dve.wait_ge(row_ld, 16 * 6)
            dve.wait_ge(back_x1, 16)
            link(dve.tensor_tensor(page[5][0:P, 0:NT * D], page[5][0:P, 0:NT * D], page[2][0:P, 0:NT * D], ALU.add))
            for k in range(KD):
                for c, (n0, w) in enumerate(CH):
                    low("h2", k, c, w, t32[:, c, 0:w], split(6)[:, 0, k, n0:n0 + w], split(6)[:, 1, k, n0:n0 + w])
            for j in range(NT):
                last = dve.tensor_tensor(rows(5)[:, j, :], rows(5)[:, j, :], rowb[:], ALU.add)
            last.then_inc(xs_done, 1)
            dve.wait_ge(xs_done, 1)
            for m in range(4):
                f_lows(f"up{m}", lambda s, i, n0, w: hidden(s, m, i, n0, w))
            t0 = T_TILES["down"][0]
            with dve.Fori(0, NT // 2) as i:
                for b in range(2):
                    dve.wait_ge(t_mm, t0 + 2 * i + b + 1)
                    y = page[5][0:P, bass.ds((2 * i + b) * D, D)]
                    dve.scalar_tensor_tensor(out=y, in0=bank[3 + b][0:P, :], scalar=1.0 / SF, in1=y, op0=ALU.mult,
                                             op1=ALU.add).then_inc(t_ev, 1)


def kernel(**inputs):
    import concourse.bacc as bacc
    from concourse.bass_utils import run_bass_kernel_spmd

    v = {k: np.asarray(x) for k, x in inputs.items()}
    g = {k[7:]: x for k, x in v.items() if k.startswith("L0_gnn_")}
    f = {k[7:]: x for k, x in v.items() if k.startswith("L0_ffn_")}

    def fm(x):
        return x.reshape(-1, 128).T

    def fm4(x):
        return x.reshape(x.shape[0], -1, 128).transpose(0, 2, 1)

    cb = f["cross_in_b"]
    parts = {"b_ih": g["b_ih"], "b_hh": g["b_hh"], "gamma": g["gamma"], "beta": g["beta"], "mean": g["run_mean"],
             "var": g["run_var"], "ns_w": f["norm_s_w"], "ns_b": f["norm_s_b"], "nt_w": f["norm_t_w"],
             "nt_b": f["norm_t_b"], "cq_b": cb[0:D], "ck_b": cb[D:2 * D], "nm_w": f["norm_mlp_w"],
             "nm_b": f["norm_mlp_b"], "m1_b": f["mlp_b1"], "rb1": f["router_b1"]}
    arrays = {
        "x": v["x"],
        "src_pt": v["src"].reshape(ET, P).T,
        "dst_pt": v["dst"].reshape(ET, P).T,
        "dst_g": v["dst"].reshape(NG, GW),
        "eaT": v["edge_attr_128"].T,
        "w1T": g["W1"].T, "w2T": g["W2"].T, "wihT": g["W_ih"].T, "whhT": g["W_hh"].T,
        "spinT": f["sp_in_w"].transpose(0, 2, 1), "spoutT": f["sp_out_w"].transpose(0, 2, 1),
        "tqT": f["tq_w"].transpose(0, 2, 1), "tkT": f["tk_w"].transpose(0, 2, 1),
        "tvT": f["tv_w"].transpose(0, 2, 1), "tpT": f["tp_w"].transpose(0, 2, 1),
        "cinT": f["cross_in_w"].T, "coutT": f["cross_out_w"].T, "m1T": f["mlp_w1"].T, "m2T": f["mlp_w2"].T,
        "rw1T": f["router_w1"].T, "rw2T": f["router_w2"].T, "rb2": f["router_b2"].reshape(1, -1),
        "vec": np.concatenate([fm(parts[name]) for name in VEC], axis=1),
        "rowv": np.stack([g["b1"], g["b2"], cb[2 * D:3 * D], f["cross_out_b"], f["mlp_b2"]]),
        "vsp": np.concatenate([fm4(f["sp_in_b"][:, 0:2 * D]), fm4(f["sp_out_b"])], axis=2),
        "vtp": np.concatenate([fm4(f["tq_b"]), fm4(f["tk_b"]), fm4(f["tp_b"])], axis=2),
        "svrow": f["sp_in_b"][:, 2 * D:3 * D], "tvrow": f["tv_b"],
    }
    arrays = {k: np.ascontiguousarray(x) for k, x in arrays.items()}
    nc = bacc.Bacc("TRN2", target_bir_lowering=False, num_devices=1)
    a = {k: nc.dram_tensor("in_" + k, x.shape, mybir.dt.from_np(x.dtype), kind="ExternalInput").ap()
         for k, x in arrays.items()}
    out = nc.dram_tensor("out", (N, D), F32, kind="ExternalOutput").ap()
    nc.disable_value_cache = True
    program(nc, a, out)
    r = run_bass_kernel_spmd(nc, [{"in_" + k: x for k, x in arrays.items()}], core_ids=[0])
    return r.results[0]["out"]
```

```python
from contextlib import ExitStack

import numpy as np
import concourse.bass as bass
from concourse import mybir

F32 = mybir.dt.float32
F16 = mybir.dt.float16
I32 = mybir.dt.int32
U32 = mybir.dt.uint32
ALU = mybir.AluOpType
ACT = mybir.ActivationFunctionType
AX = mybir.AxisListType

N = 1250
E = 20000
D = 512
ED = 128
P = 125
NT = N // P
ET = E // P
GE = 4
NG = ET // GE
GW = GE * P
KD = D // 128
H = 8
HD = D // H
FF = 4 * D
CH = [(0, 500), (500, 500), (1000, 250)]
PB = 2 * P
NC = len(CH)
SG = 64.0
SF = 16.0
EPS = 1e-5
QK_SCALE = HD ** -0.5
MASKED = -60000.0
MASK_GAIN = 2048.0
R32, R16 = 3, 5
AHEAD = 3
PAGE = 5160
EXPERTS = 4

VEC = {}
for _name, _n in [("b_ih", 12), ("b_hh", 12), ("gamma", 4), ("beta", 4), ("mean", 4), ("var", 4),
                  ("ns_w", 4), ("ns_b", 4), ("nt_w", 4), ("nt_b", 4), ("cq_b", 4), ("ck_b", 4),
                  ("nm_w", 4), ("nm_b", 4), ("m1_b", 16), ("rb1", 1)]:
    VEC[_name] = (sum(n for _, n in VEC.values()), _n)
NV = sum(n for _, n in VEC.values())
ROW = {"b1": 0, "b2": 1, "cv": 2, "cout": 3, "m2": 4}


def program(nc, a, out):
    ctx = ExitStack()
    with ctx:
        def sb(name, shape, dt):
            return ctx.enter_context(nc.sbuf_tensor(name, shape, dt))

        def sem(name):
            return ctx.enter_context(nc.semaphore(name))

        bank = [ctx.enter_context(nc.psum_tensor(f"bank{i}", [128, 512], F32)) for i in range(8)]

        pages = sb("pages", [128, 7 * PAGE], F32)
        page = [None] + [pages[:, i * PAGE:(i + 1) * PAGE] for i in range(7)]
        wide = [pages[:, 2 * s * PAGE:2 * s * PAGE + 8 * N].bitcast(F16).rearrange("p (k n) -> p k n", k=FF // 128)
                for s in range(2)]
        slots = sb("slots", [128, 4, 2, KD, D], F16)
        stage = sb("stage", [128, 4, D], F32)
        scratch = sb("scratch", [128, 2560], F32)
        t32 = scratch[:, 0:1536].rearrange("p (c n) -> p c n", c=NC)
        rowst = scratch[:, 1536:2560].rearrange("p (c n) -> p c n", c=2)
        eah = scratch[:, 0:500].bitcast(F16).rearrange("p (c n) -> p c n", c=2)
        eal = scratch[:, 500:1000].bitcast(F16).rearrange("p (c n) -> p c n", c=2)
        ident = sb("ident", [128, 128], F32)
        gain16 = sb("gain16", [128, 128], F16)
        ones32 = sb("ones32", [P, 1], F32)
        ones16 = sb("ones16", [P, 1], F16)
        blockdiag = sb("blockdiag", [NT, NT, P], F16)
        turns = sb("turns", [128, 1250], F32)
        srcs = turns[0:P, 512:512 + ET].bitcast(I32)
        dstf = turns[0:P, 672:672 + ET]
        win = turns[0:1, 832:832 + 4 * NG].bitcast(I32)     
        rw1 = turns[:, 0:512].rearrange("p (k n) -> p k n", k=KD)
        oraw = turns[0:HD + 1, 0:1000].rearrange("p (c n) -> p c n", c=2)
        node_id = sb("node_id", [P, N], F16)
        idx_ring = sb("idx_ring", [P, 2, GE], I32)
        cnt = sb("cnt", [P, NT], F32)
        vec = sb("vec", [128, NV], F32)
        vsp = sb("vsp", [128, 12], F32)
        vtp = sb("vtp", [128, 12], F32)
        rowb = sb("rowb", [P, D], F32)
        stats = sb("stats", [P, NT, 6], F32)
        mv = sb("mv", [P, NT, 2], F32)
        rstd = sb("rstd", [P, NT], F32)
        bsum = sb("bsum", [128, 12], F32)
        bns = sb("bns", [128, 2, KD], F32)
        mxs = sb("mxs", [P, 2, NT, NC], F32)
        mx = sb("mx", [P, 2, NT], F32)
        rinv = sb("rinv", [P, 4], F32)
        onorm = sb("onorm", [128, 500], F32)
        rs = sb("rs", [128, 8], F32)
        rw2 = sb("rw2", [128, 2 * EXPERTS], F32)
        rb2 = sb("rb2", [1, 2 * EXPERTS], F32)
        lg = sb("lg", [1, 40], F32)
        choice = sb("choice", [1, 16], U32)

        def vcol(name, i=0, n=1):
            at = VEC[name][0] + i
            return vec[:, bass.ds(at, n)]

        def rows(p):
            return page[p][0:P, 0:NT * D].rearrange("p (t d) -> p t d", t=NT)

        def cols(p):
            return page[p][:, 0:KD * N].rearrange("p (k n) -> p k n", k=KD)

        def split(p):
            return page[p][:, 0:KD * N].bitcast(F16).rearrange("p (s k n) -> p s k n", s=2, k=KD)

        def exps32(x, v, w):
            at = v % R32 * 500
            return page[x["p"]][0:P, at:at + w]

        def exps16(x, v, w, part):
            at = R32 * 500 + (2 * (v % R16) + part) * 250
            return page[x["p"]][0:P, at:at + 250].bitcast(F16)[:, 0:w]

        def values(x):
            return page[x["v"]][0:P, 0:NT * H * 129 // 2].bitcast(F16)

        def hidden(s, m, i, n0, w):
            return pages[:, 2 * s * PAGE:2 * s * PAGE + 8 * N].bitcast(F16)[:, bass.ds((4 * m + i) * N + n0, w)]

        gath = page[6][0:P, 0:8 * D].rearrange("p (s d) -> p s d", s=8)
        eas = page[6][:, 8 * D:8 * D + 1000].rearrange("p (s n) -> p s n", s=2)
        relu = page[7][0:P, 0:8 * D].bitcast(F16).rearrange("p (s l d) -> p s l d", s=8, l=2)
        esum = page[7][0:P, 8 * D:10 * D].rearrange("p (s d) -> p s d", s=2)
        onehot = page[4][0:P, 0:5000].bitcast(F16).rearrange("p (s n) -> p s n", s=8)
        cntb = page[6][0:NT, 0:N]
        cnth = page[6][0:NT, N:2 * N].bitcast(F16).rearrange("p (l n) -> p l n", l=2)
        b2f = page[6][0:NT, 2 * N:2 * N + D]
        b2h = page[6][0:NT, 2 * N + D:2 * N + 2 * D].bitcast(F16).rearrange("p (l n) -> p l n", l=2)
        mask_s = node_id[:, 0:P]
        mask_t = node_id[:, P:2 * P]
        grp_i = page[7][0:NG, 0:GW].bitcast(I32)
        grp_f = page[7][0:NG, GW:2 * GW]
        gw = page[7][0:NG, 1000:1032]
        gwi = page[7][0:NG, 1040:1044].bitcast(I32)
        tri = page[7][0:NG, 1100:1100 + 2 * NG].rearrange("p (a n) -> p a n", a=2)
        dsts = page[7][0:P, 1200:1200 + ET].bitcast(I32)

        proj_d = nc.dram_tensor("proj_d", (N, D), F32, kind="Internal").ap()
        x1_d = nc.dram_tensor("x1_d", (P, NT * D), F32, kind="Internal").ap()
        xl_d = nc.dram_tensor("xl_d", (P, NT * D), F32, kind="Internal").ap()
        xt_d = nc.dram_tensor("xt_d", (128, KD * N), F32, kind="Internal").ap()
        win_d = nc.dram_tensor("win_d", (NG, 4), I32, kind="Internal").ap()

        in_ld = sem("in_ld")
        x_ld = sem("x_ld")
        pool_c = sem("pool_c")
        dve_c = sem("dve_c")
        link_s = sem("link_s")
        ln_var = sem("ln_var")
        ln_sd = sem("ln_sd")
        ln_out = sem("ln_out")
        ln_tile = sem("ln_tile")
        f_mm = sem("f_mm")
        f_act = sem("f_act")
        f_lo = sem("f_lo")
        t_mm = sem("t_mm")
        t_ev = sem("t_ev")
        v_hi = sem("v_hi")
        v_lo = sem("v_lo")
        p_st = [sem(f"p_st{i}") for i in range(2)]
        w_ld = [sem(f"w_ld{i}") for i in range(4)]
        w_sc = sem("w_sc")
        w_hi = sem("w_hi")
        w_split = sem("w_split")
        win_s = sem("win_s")
        win_io = sem("win_io")
        ea_ld = [sem(f"ea_ld{i}") for i in range(2)]
        ea_hi = sem("ea_hi")
        ea_lo = sem("ea_lo")
        g_ix = sem("g_ix")
        g_ld = [sem(f"g_ld{i}") for i in range(8)]
        e_mm = sem("e_mm")
        e_sum = sem("e_sum")
        e_hi = sem("e_hi")
        e_lo = sem("e_lo")
        s_mm = sem("s_mm")
        s_add = sem("s_add")
        agg_done = sem("agg_done")
        c_s = sem("c_s")
        c_mt = sem("c_mt")
        n_hr = sem("n_hr")
        n_new = sem("n_new")
        rw_ld = sem("rw_ld")
        b2_ld = sem("b2_ld")
        r_mm = sem("r_mm")
        r_act = sem("r_act")
        r_ix = sem("r_ix")
        sp_io = sem("sp_io")
        to_sum = sem("to_sum")
        xs_done = sem("xs_done")
        back = sem("back")
        back_x1 = sem("back_x1")
        eb_ld = sem("eb_ld")
        row_ld = sem("row_ld")
        big_ld = [sem(f"big_ld{i}") for i in range(2)]
        small_ld = [sem(f"small_ld{i}") for i in range(2)]
        eight = sem("eight")
        a_mm = sem("a_mm")
        a_mx = sem("a_mx")
        m_all = sem("m_all")
        m_t = sem("m_t")
        m_sh = sem("m_sh")
        s_sc = sem("s_sc")
        s_exp = sem("s_exp")
        s_plo = sem("s_plo")
        s_pv = sem("s_pv")
        o_raw = sem("o_raw")
        o_den = sem("o_den")
        o_rec = sem("o_rec")
        o_bc = sem("o_bc")
        o_norm = sem("o_norm")
        o_hi = sem("o_hi")
        o_ev = sem("o_ev")
        o_st = sem("o_st")
        y_st = sem("y_st")
        co_stats = sem("co_stats")

        F_TILES, T_TILES, LOWS = {}, {}, {}
        g = l = t = 0
        for name, kind, tiles, low in [
                ("hT", "F", KD * NC, 1), ("P", "T", NT, 0), ("aggT", "F", KD * NC, 1), ("M", "F", KD * NC, 1),
                ("r", "F", KD * NC, 0), ("z", "F", KD * NC, 0), ("n", "F", KD * NC, 0), ("x1", "T", NT, 0),
                ("xn", "F", KD * NC, 1), ("xt", "F", KD * NC, 1),
                ("sq", "F", KD * NC, 1), ("sk", "F", KD * NC, 1), ("sv", "T", NT, 0),
                ("so", "F", KD * NC, 1), ("cq", "F", KD * NC, 1),
                ("tq", "F", KD * NC, 1), ("tk", "F", KD * NC, 1), ("tv", "T", NT, 0),
                ("to", "F", KD * NC, 1),
                ("ck", "F", KD * NC, 1), ("cv", "T", NT, 0),
                ("co", "T", NT, 0), ("h2", "F", KD * NC, 1),
                ("up0", "F", KD * NC, 1), ("up1", "F", KD * NC, 1), ("up2", "F", KD * NC, 1),
                ("up3", "F", KD * NC, 1), ("down", "T", NT, 0)]:
            if kind == "F":
                F_TILES[name] = (g, g + tiles)
                LOWS[name] = (l, l + tiles * low)
                g, l = g + tiles, l + tiles * low
            else:
                T_TILES[name] = (t, t + tiles)
                t += tiles

        def since(v, units, ring):
            return ring if v >= ring else v + units - max(w for w in range(units) if w % ring == v)

        def f_read(name):
            return F_TILES[name][1] + NC

        def f_split(name):
            return LOWS[name][1] + NC

        def t_read(name):
            return T_TILES[name][1] + 2

        UNITS = [("w1a", "w1T", None, 0, 0, KD, SG, "P"), ("w1b", "w1T", None, D, 0, 1, SG, "aggT"),
                 ("w2", "w2T", None, 0, 0, KD, SG, "M")]
        for i, stg in enumerate(("r", "z", "n")):
            UNITS += [("ih" + stg, "wihT", None, 0, i * D, KD, SG, stg),
                      ("hh" + stg, "whhT", None, 0, i * D, KD, SG, stg)]
        UNITS += [("sq", "spinT", "s", 0, 0, KD, SF, "sq"), ("sk", "spinT", "s", 0, D, KD, SF, "sk"),
                  ("sv", "spinT", "s", 0, 2 * D, KD, SF, "sv"), ("so", "spoutT", "s", 0, 0, KD, SF, "so"),
                  ("cq", "cinT", None, 0, 0, KD, SF, "cq"),
                  ("tq", "tqT", "t", 0, 0, KD, SF, "tq"), ("tk", "tkT", "t", 0, 0, KD, SF, "tk"),
                  ("tv", "tvT", "t", 0, 0, KD, SF, "tv"), ("to", "tpT", "t", 0, 0, KD, SF, "to"),
                  ("ck", "cinT", None, 0, D, KD, SF, "ck"), ("cv", "cinT", None, 0, 2 * D, KD, SF, "cv"),
                  ("co", "coutT", None, 0, 0, KD, SF, "co")]
        UNITS += [(f"up{i}", "m1T", None, 0, i * D, KD, SF, f"up{i}") for i in range(4)]
        UNITS += [(f"down{i}", "m2T", None, i * D, 0, KD, SF, "down") for i in range(4)]
        UNIT = {u[0]: i for i, u in enumerate(UNITS)}
        SLOT = {u[0]: i % 4 for i, u in enumerate(UNITS)}
        BEFORE = {u[0]: UNITS[i - 4][7] if i >= 4 else None for i, u in enumerate(UNITS)}
        SLOT.update(down0=4, down1=5, down2=SLOT["up0"], down3=SLOT["up1"])
        BEFORE.update(down0="co", down1="co", down2="up0", down3="up1")
        extra = page[7][:, 0:2 * KD * D].bitcast(F16).rearrange("p (u s k n) -> p u s k n", u=2, s=2, k=KD)

        def slot(name):
            i = SLOT[name]
            return slots[:, i] if i < 4 else extra[:, i - 4]

        CHUNKS = [(i, k) for i, u in enumerate(UNITS) for k in range(u[5])]
        SPLIT_AT = {}
        for n, (i, k) in enumerate(CHUNKS):
            SPLIT_AT[UNITS[i][0]] = n + 1
        FIRST_AFTER_EDGES = CHUNKS.index((UNIT["hhr"], 0))

        ATT = [dict(n="s", q=7, k=3, ring=2, v=6, o=4, p=1, causal=False),
               dict(n="t", q=1, k=6, ring=4, v=7, o=5, p=3, causal=True),
               dict(n="c", q=2, k=1, ring=6, v=7, o=4, p=3, causal=False)]

        def score_units(causal):
            units = []
            for c, (n0, w) in enumerate(CH):
                before = n0 // P if causal else NT
                if w == 2 * PB:
                    units += [(c, [(s, 0, w, 0, False)]) for s in range(before)]
                    if causal:
                        units += [(c, [(before, 0, w, 0, True)]),
                                  (c, [(before + 1, P, 3 * P, 0, True), (before + 3, 3 * P, P, 3 * P, True)]),
                                  (c, [(before + 2, 2 * P, 2 * P, 0, True)])]
                else:
                    units += [(c, [(s, 0, w, 0, False), (s + 1, 0, w, w, False)]) for s in range(0, before, 2)]
                    if causal:
                        units += [(c, [(before, 0, w, 0, True), (before + 1, P, P, w, True)])]
            return units

        def maximum_units(causal):
            if causal:
                return [[(t, k0, min(w, (t + 1) * P - k0), 0, (t + 1) * P - k0 <= w)]
                        for t in range(NT) for k0, w in CH if k0 < (t + 1) * P]
            return ([[(t, k0, w, 0, False)] for t in range(NT) for k0, w in CH[0:2]]
                    + [[(t + r, CH[2][0], PB, r * PB, False) for r in range(2)] for t in range(0, NT, 2)])

        u0 = b0 = a0 = h0 = 0
        for at in ATT:
            at["units"], at["maxima"] = score_units(at["causal"]), maximum_units(at["causal"])
            at["u0"], at["b0"], at["a0"], at["h0"] = u0, b0, a0, h0
            nu, nm = len(at["units"]), len(at["maxima"])
            at["first"] = [list(range(nm * (j - 3) // (NT - 3), nm * (j - 2) // (NT - 3))) if j >= 3 else []
                           for j in range(NT)]
            at["ends"] = {max(u for u in range(nu) if at["units"][u][0] == c): c for c in range(NC)}
            first, last = (1 if at["causal"] else 2), nu - 6
            at["early"] = [list(range(nm * (u - first) // (last + 1 - first), nm * (u + 1 - first) // (last + 1 - first)))
                           if first <= u <= last else [] for u in range(nu)]
            u0, b0, a0, h0 = u0 + nu * H, b0 + NC * H, a0 + nm * H, h0 + H
        ATT_END = [dict(u=x["u0"] + len(x["units"]) * H, a=x["a0"] + len(x["maxima"]) * H, b=x["b0"] + NC * H)
                   for x in ATT]
        E_BANKS = (0, 1, 6, 7)
        S_BANKS, M_BANKS, O_BANKS = (0, 1, 7), (2, 5), (3, 4)

        def due(x, u, after, head, before):
            nu = len(x["units"])
            for e, c in sorted(x["ends"].items()):
                if e + after == u:
                    yield head, c
                elif e + after - nu == u and before:
                    yield before, c

        def head_loop(engine, body):
            body((0, 0, 0), None, (1, 0, 1))
            with engine.Fori(0, H // 2 - 1) as i:
                body((2 * i + 1, i, 1), (2 * i, i, 0), (2 * i + 2, i + 1, 0))
                body((2 * i + 2, i + 1, 0), (2 * i + 1, i, 1), (2 * i + 3, i + 1, 1))
            body((H - 1, H // 2 - 1, 1), (H - 2, H // 2 - 1, 0), None)

        def tail(x, steps):
            nu = len(x["units"])
            for u in range(nu, nu + 6):
                for after, step in steps:
                    for hd, c in due(x, u, after, (H - 1, H // 2 - 1, 1), None):
                        step(hd, c)

        def operands(x, par):
            return [page[x["ring"]][:, 0:KD * N].bitcast(F16)[:, (4 * par + j) * N:(4 * par + j + 1) * N]
                    for j in range(4)]

        block = ctx.enter_context(nc.Block())

        def load_x(engine, half):
            t0 = half * NT // 2
            engine.dma_start(rows(1)[:, t0:t0 + NT // 2, :],
                             a["x"][t0 * P:(t0 + NT // 2) * P, :].rearrange("(t p) d -> p t d", p=P)).then_inc(x_ld, 16)

        @block.sync
        def _(sp):
            for s, v in ((f_act, NC), (f_lo, NC), (t_ev, 2), (ea_lo, 2), (e_mm, GE), (e_sum, 2 * GE), (e_hi, 2),
                         (e_lo, 2), (a_mx, 2), (s_mm, NT), (s_add, NT), (v_lo, 1), (p_st[0], 16), (p_st[1], 16),
                         (s_exp, 3), (s_plo, R32), (s_pv, R16), (o_raw, 2), (o_norm, 1), (o_ev, 2)):
                sp.sem_inc(s, v)
            load_x(sp, 1)
            sp.dma_start(vec[:], a["vec"]).then_inc(in_ld, 16)
            sp.dma_start(srcs, a["src_pt"]).then_inc(in_ld, 16)
            sp.dma_start(dsts, a["dst_pt"]).then_inc(in_ld, 16)
            sp.dma_start(grp_i, a["dst_g"]).then_inc(in_ld, 16)
            sp.dma_start(rowb[:], a["rowv"][0:1, :].to_broadcast([P, D])).then_inc(row_ld, 16)

            def load_weights(first, last, pick):
                for n in range(first, last):
                    i, k = CHUNKS[n]
                    _, name, expert, r0, c0, _, _, _ = UNITS[i]
                    if n >= 4:
                        sp.wait_ge(w_split, n - 3)
                    src = a[name]
                    if expert:
                        src = src[bass.ds(pick[expert], 1), r0 + 128 * k:r0 + 128 * k + 128, c0:c0 + D]
                        src = src.rearrange("a p n -> (a p) n")
                    else:
                        src = src[r0 + 128 * k:r0 + 128 * k + 128, c0:c0 + D]
                    sp.dma_start(stage[:, n % 4, :], src).then_inc(w_ld[n % 4], 16)

            def load_operands(x, i, par):
                k_both, k_high, q_high, q_low = operands(x, par)

                def part(src, hi_lo):
                    return page[src][64 * par:64 * par + 64, 0:KD * N].bitcast(F16)[:, bass.ds(i * N + hi_lo * KD * N, N)]

                for dst, src in ((k_both[0:64, :], part(x["k"], 0)), (k_both[64:128, :], part(x["k"], 1)),
                                 (q_high[0:64, :], part(x["q"], 0)), (q_high[64:128, :], part(x["q"], 0))):
                    sp.dma_start(dst, src).then_inc(big_ld[par], 16)
                for dst, src in ((k_high[0:64, :], part(x["k"], 0)), (q_low[0:64, :], part(x["q"], 1))):
                    sp.dma_start(dst, src).then_inc(small_ld[par], 16)

            def attention_operands(a):
                x, nu = ATT[a], len(ATT[a]["units"])
                sp.wait_ge(f_lo, f_split(x["n"] + "k"))
                sp.wait_ge(f_act, f_read(x["n"] + "k"))
                if a == 0:
                    sp.wait_ge(sp_io, 48)
                load_operands(x, 0, 0)

                def head(hd, before, after):
                    if after:
                        sp.wait_ge(s_sc, x["u0"] + hd[0] * nu + 1)
                        load_operands(x, *after[1:])

                head_loop(sp, head)

            load_weights(0, FIRST_AFTER_EDGES, {})
            sp.wait_ge(f_mm, F_TILES["hT"][1])
            with sp.Fori(0, NG // 2) as i:
                for s in range(2):
                    sp.wait_ge(ea_lo, 2 * i + s + 1)
                    sp.dma_start(eas[:, s, :], a["eaT"][:, bass.ds((2 * i + s) * GW, GW)]).then_inc(ea_ld[s], 16)
            split_s = CHUNKS.index((UNIT["sq"], 0))
            ihz_at = CHUNKS.index((UNIT["ihz"], 0))
            load_weights(FIRST_AFTER_EDGES, ihz_at, {})
            sp.wait_ge(agg_done, 1)
            sp.wait_ge(f_mm, F_TILES["aggT"][1])
            sp.dma_start(b2f, a["rowv"][ROW["b2"]:ROW["b2"] + 1, :].to_broadcast([NT, D])).then_inc(b2_ld, 16)
            sp.dma_start(rw1, a["rw1T"].rearrange("(k p) n -> p k n", p=128)).then_inc(rw_ld, 16)
            sp.dma_start(rw2[:], a["rw2T"]).then_inc(rw_ld, 16)
            sp.dma_start(rb2[:], a["rb2"]).then_inc(rw_ld, 16)
            load_weights(ihz_at, split_s, {})
            sp.wait_ge(r_ix, 2)
            ps = sp.value_load(choice[0:1, 0:1], min_val=0, max_val=EXPERTS - 1)
            pt = sp.value_load(choice[0:1, 8:9], min_val=0, max_val=EXPERTS - 1)
            pick = {"s": ps, "t": pt}
            sp.dma_start(vsp[:], a["vsp"][bass.ds(ps, 1), :, :].rearrange("a p n -> (a p) n")).then_inc(eb_ld, 16)
            sp.dma_start(vtp[:], a["vtp"][bass.ds(pt, 1), :, :].rearrange("a p n -> (a p) n")).then_inc(eb_ld, 16)
            sp.wait_ge(t_ev, t_read("P"))
            sp.dma_start(rowb[:], a["svrow"][bass.ds(ps, 1), :].to_broadcast([P, D])).then_inc(row_ld, 16)
            at = {name: CHUNKS.index((UNIT[name], 0)) for name in ("so", "tv", "to", "cv", "co", "up0", "up1")}
            load_weights(split_s, at["so"], pick)
            attention_operands(0)
            load_weights(at["so"], at["tv"], pick)
            sp.wait_ge(t_ev, t_read("sv"))
            sp.dma_start(rowb[:], a["tvrow"][bass.ds(pt, 1), :].to_broadcast([P, D])).then_inc(row_ld, 16)
            load_weights(at["tv"], at["to"], pick)
            attention_operands(1)
            load_weights(at["to"], at["cv"], pick)
            sp.wait_ge(t_ev, t_read("tv"))
            sp.dma_start(rowb[:], a["rowv"][ROW["cv"]:ROW["cv"] + 1, :].to_broadcast([P, D])).then_inc(row_ld, 16)
            load_weights(at["cv"], at["co"], pick)
            attention_operands(2)
            load_weights(at["co"], at["up0"], pick)
            sp.wait_ge(t_ev, t_read("cv"))
            sp.dma_start(rowb[:], a["rowv"][ROW["cout"]:ROW["cout"] + 1, :].to_broadcast([P, D])).then_inc(row_ld, 16)
            load_weights(at["up0"], at["up1"], pick)
            sp.wait_ge(y_st, 1)
            sp.dma_start(rowb[:], a["rowv"][ROW["m2"]:ROW["m2"] + 1, :].to_broadcast([P, D])).then_inc(row_ld, 16)
            load_weights(at["up1"], len(CHUNKS), pick)
            for j in range(NT):
                sp.wait_ge(t_ev, T_TILES["down"][0] + j + 1 + 2)
                sp.dma_start(out[j * P:(j + 1) * P, :], rows(5)[:, j, :]).then_inc(o_st, 16)
            sp.wait_ge(o_st, 16 * NT)

        @block.gpsimd
        def _(pool):
            pool.memset(ident[:], 0.0).then_inc(pool_c, 1)
            pool.memset(blockdiag[:], 0.0).then_inc(pool_c, 1)
            pool.memset(tri, 1.0).then_inc(pool_c, 1)
            pool.iota(node_id[:], pattern=[[1, N]], base=0, channel_multiplier=0,
                      allow_small_or_imprecise_dtypes=True).then_inc(pool_c, 1)
            pool.wait_ge(pool_c, 4)
            pool.affine_select(out=ident[:], in_=ident[:], compare_op=ALU.not_equal, fill=1.0, base=0,
                               pattern=[[-1, 128]], channel_multiplier=1).then_inc(pool_c, 1)
            pool.affine_select(out=blockdiag[:], in_=blockdiag[:], compare_op=ALU.not_equal, fill=1.0, base=0,
                               pattern=[[-1, NT], [0, P]], channel_multiplier=1).then_inc(pool_c, 1)
            for o in range(2):
                pool.affine_select(out=tri[:, o, :], in_=tri[:, o, :], compare_op=ALU.is_ge, fill=0.0,
                                   base=-1 - o, pattern=[[1, NG]], channel_multiplier=-1).then_inc(pool_c, 1)

            def split_weights(first, last):
                for n in range(first, last):
                    i, k = CHUNKS[n]
                    scale = UNITS[i][6]
                    name = UNITS[i][0]
                    if k == 0 and BEFORE[name]:
                        was = BEFORE[name]
                        if was in F_TILES:
                            pool.wait_ge(f_mm, F_TILES[was][1])
                        elif was in T_TILES:
                            pool.wait_ge(t_mm, T_TILES[was][1])
                    pool.wait_ge(w_ld[n % 4], 16 * (n // 4 + 1))
                    pool.tensor_scalar(stage[:, n % 4, :], stage[:, n % 4, :], scale, 1.0,
                                       ALU.mult, ALU.mult).then_inc(w_sc, 1)
                    pool.wait_ge(w_sc, n + 1)
                    pool.tensor_copy(slot(name)[:, 0, k, :], stage[:, n % 4, :]).then_inc(w_hi, 1)
                    pool.wait_ge(w_hi, n + 1)
                    pool.tensor_tensor(slot(name)[:, 1, k, :], stage[:, n % 4, :], slot(name)[:, 0, k, :],
                                       ALU.subtract).then_inc(w_split, 1)

            split_weights(0, FIRST_AFTER_EDGES)
            for s in range(2):
                pool.wait_ge(p_st[s], 16 * NT // 2 + 16)
            pool.wait_ge(in_ld, 64)
            with pool.Fori(0, NG // 2) as i:
                for s in range(2):
                    pool.wait_ge(e_sum, (2 * i + s) * GE + GE)
                    pool.tensor_copy(idx_ring[:, s, :], srcs[:, bass.ds((2 * i + s) * GE, GE)]).then_inc(g_ix, 1)
                    pool.wait_ge(ea_hi, 2 * i + s + 1)
                    pool.wait_ge(g_ix, 2 * i + s + 1)
                    pool.tensor_tensor(eal[:, s, :], eas[:, s, :], eah[:, s, :], ALU.subtract).then_inc(ea_lo, 1)
                    for q in range(GE):
                        pool.indirect_dma_start(
                            gath[:, s * GE + q, :], None, proj_d,
                            bass.IndirectOffsetOnAxis(ap=idx_ring[:, s, q:q + 1], axis=0)).then_inc(g_ld[s * GE + q], 16)
            pool.wait_ge(e_lo, ET + 2)
            pool.memset(mask_s, 0.0).then_inc(pool_c, 1)
            pool.memset(mask_t, 0.0).then_inc(pool_c, 1)
            pool.wait_ge(pool_c, 10)
            pool.affine_select(out=mask_s, in_=mask_s, compare_op=ALU.is_ge, fill=MASKED, base=0,
                               pattern=[[1, P]], channel_multiplier=-1).then_inc(pool_c, 1)
            pool.affine_select(out=mask_t, in_=mask_t, compare_op=ALU.is_ge, fill=MASKED, base=0,
                               pattern=[[-1, P]], channel_multiplier=1).then_inc(pool_c, 1)
            split_weights(FIRST_AFTER_EDGES, len(CHUNKS))

        @block.tensor
        def _(pe):
            def f_gemm(name, units, start_waits):
                for s, v in start_waits:
                    pe.wait_ge(s, v)
                for u in units:
                    pe.wait_ge(w_split, SPLIT_AT[u[0]])
                g0 = F_TILES[name][0]
                with pe.Fori(0, KD) as i:
                    for c, (n0, w) in enumerate(CH):
                        pe.wait_ge(f_act, g0 + i * NC + c + 1)
                        todo = [(u, xp, s, r, k) for u, xp in units for k in range(KD)
                                for s, r in ((0, 0), (0, 1), (1, 0))]
                        for m, (u, xp, s, r, k) in enumerate(todo):
                            mm = pe.matmul(bank[c][:, 0:w], slot(u)[:, s, k, bass.ds(i * 128, 128)],
                                           split(xp)[:, r, k, n0:n0 + w], start=(m == 0), stop=(m == len(todo) - 1))
                        mm.then_inc(f_mm, 1)

            def f_transpose(name, src, start_waits):
                for s, v in start_waits:
                    pe.wait_ge(s, v)
                g0 = F_TILES[name][0]
                for k in range(KD):
                    for c, (n0, w) in enumerate(CH):
                        pe.wait_ge(f_act, g0 + k * NC + c + 1)
                        for q in range(w // P):
                            mm = pe.transpose(bank[c][:, q * P:(q + 1) * P],
                                              rows(src)[:, n0 // P + q, k * 128:(k + 1) * 128], ident[0:P, 0:P])
                        mm.then_inc(f_mm, 1)

            def t_gemm(name, pairs, start_waits):
                for s, v in start_waits:
                    pe.wait_ge(s, v)
                t0 = T_TILES[name][0]
                with pe.Fori(0, NT // 2) as i:
                    for b in range(2):
                        pe.wait_ge(t_ev, t0 + 2 * i + b + 1)
                        todo = [(x, u, k, s, r) for x, u in pairs for k in range(KD)
                                for s, r in ((0, 0), (0, 1), (1, 0))]
                        for m, (x, u, k, s, r) in enumerate(todo):
                            mm = pe.matmul(bank[3 + b][0:P, :], x(s, k, bass.ds((2 * i + b) * P, P)),
                                           slot(u)[:, r, k, :], start=(m == 0), stop=(m == len(todo) - 1))
                        mm.then_inc(t_mm, 1)

            def of(p):
                return lambda s, k, n: split(p)[:, s, k, n]

            pe.wait_ge(pool_c, 8)
            f_transpose("hT", 6, [(ln_out, 1)])
            pe.wait_ge(win_s, 1)
            pe.matmul(bank[7][0:NG, 0:1], tri[:, 0, :], gw[:, 20:21], start=True, stop=True)
            pe.matmul(bank[7][0:NG, 1:2], tri[:, 1, :], gw[:, 20:21], start=True, stop=True).then_inc(win_s, 1)

            pe.wait_ge(w_split, SPLIT_AT["w1a"])
            t_gemm("P", [(of(3), "w1a")], [(f_lo, f_split("hT"))])

            pe.wait_ge(w_split, SPLIT_AT["w1b"])
            pe.wait_ge(f_act, f_read("hT"))
            pe.wait_ge(dve_c, 1)
            pe.wait_ge(win_io, 32)

            def group(n0, s):
                pe.wait_ge(ea_lo, n0 + 1 + 2)
                for q in range(GE):
                    pe.wait_ge(e_sum, n0 * GE + q - GE + 1 + 2 * GE)
                    for m, (x, wt) in enumerate(((eah, 0), (eah, 1), (eal, 0))):
                        mm = pe.matmul(bank[E_BANKS[q]][0:P, :], x[:, s, q * P:(q + 1) * P],
                                       slot("w1b")[:, wt, 0, :], start=(m == 0), stop=(m == 2))
                    mm.then_inc(e_mm, 1)

            def scatter(n0, s):
                first, end, number = (pe.value_load(win[:, bass.ds(n0 * 4 + c, 1)], min_val=lo, max_val=hi)
                                      for c, lo, hi in ((0, 0, NT - 1), (1, 1, NT), (2, 1, NG * NT + NT)))
                with pe.Fori(first, end) as j:
                    pe.wait_ge(e_lo, n0 * GE + GE + 2)
                    pe.wait_ge(s_add, number + j)
                    for q in range(GE):
                        member = onehot[:, s * GE + q, bass.ds(j * P, P)]
                        pe.matmul(bank[2][0:P, :], member, relu[:, s * GE + q, 0, :], start=(q == 0), stop=False)
                        pe.matmul(bank[2][0:P, :], member, relu[:, s * GE + q, 1, :], start=False, stop=(q == GE - 1))
                    for q in range(GE):
                        mm = pe.matmul(bank[5][0:P, 0:1], onehot[:, s * GE + q, bass.ds(j * P, P)], ones16[:],
                                       start=(q == 0), stop=(q == GE - 1))
                    mm.then_inc(s_mm, 1)

            group(0, 0)
            group(1, 1)
            with pe.Fori(0, NG // 2 - 1) as i:
                scatter(2 * i, 0)
                group(2 * i + 2, 0)
                scatter(2 * i + 1, 1)
                group(2 * i + 3, 1)
            scatter(NG - 2, 0)
            scatter(NG - 1, 1)

            pe.wait_ge(agg_done, 1)
            pe.transpose(bank[7][0:NT, 0:P], cnt[:], ident[0:P, 0:P]).then_inc(c_mt, 1)
            f_transpose("aggT", 5, [])
            pe.wait_ge(f_lo, f_split("aggT"))
            pe.wait_ge(c_s, 1)
            pe.wait_ge(w_split, SPLIT_AT["w2"])
            g0 = F_TILES["M"][0]
            with pe.Fori(0, KD) as i:
                for c, (n0, w) in enumerate(CH):
                    pe.wait_ge(f_act, g0 + i * NC + c + 1)
                    for m, (s, r) in enumerate(((0, 0), (0, 1), (1, 0))):
                        pe.matmul(bank[c][:, 0:w], b2h[:, s, bass.ds(i * 128, 128)], cnth[:, r, n0:n0 + w],
                                  start=(m == 0), stop=False)
                    for k in range(KD):
                        for s, r in ((0, 0), (0, 1), (1, 0)):
                            mm = pe.matmul(bank[c][:, 0:w], slot("w2")[:, s, k, bass.ds(i * 128, 128)],
                                           split(4)[:, r, k, n0:n0 + w], start=False, stop=(k == KD - 1 and s == 1))
                    mm.then_inc(f_mm, 1)
            for gate in "rz":
                pe.wait_ge(w_split, SPLIT_AT["hh" + gate])
                f_gemm(gate, [("ih" + gate, 5), ("hh" + gate, 3)], [(f_lo, f_split("M"))])
            pe.wait_ge(w_split, SPLIT_AT["hhn"])
            g0 = F_TILES["n"][0]
            with pe.Fori(0, KD) as i:
                for c, (n0, w) in enumerate(CH):
                    pe.wait_ge(f_act, g0 + i * NC + c + 1)
                    for b, u, xp in ((0, "ihn", 5), (5, "hhn", 3)):
                        for k in range(KD):
                            for s, r in ((0, 0), (0, 1), (1, 0)):
                                mm = pe.matmul(bank[b + c][:, 0:w], slot(u)[:, s, k, bass.ds(i * 128, 128)],
                                               split(xp)[:, r, k, n0:n0 + w], start=(k == 0 and s == 0 and r == 0),
                                               stop=(k == KD - 1 and s == 1))
                    mm.then_inc(f_mm, 1)
            pe.wait_ge(n_new, KD)
            t0 = T_TILES["x1"][0]
            for j in range(NT):
                pe.wait_ge(t_ev, t0 + j + 1)
                for k in range(KD):
                    mm = pe.transpose(bank[3 + j % 2][0:P, k * 128:(k + 1) * 128],
                                      cols(2)[:, k, j * P:(j + 1) * P], ident[:])
                mm.then_inc(t_mm, 1)

            for j in range(NT):
                pe.wait_ge(ln_tile, j + 1)
                for k in range(KD):
                    mm = pe.matmul(bank[7][:, k:k + 1], rows(2)[:, j, k * 128:(k + 1) * 128], ones32[:],
                                   start=(j == 0 and k == 0), stop=(j == NT - 1), skip_group_check=True)
            mm.then_inc(r_mm, 1)
            pe.wait_ge(r_act, 1)
            pe.wait_ge(rw_ld, 48)
            for k in range(KD):
                mm = pe.matmul(bank[7][:, 8:9], rw1[:, k, :], rs[:, k:k + 1], start=(k == 0), stop=(k == KD - 1))
            mm.then_inc(r_mm, 1)
            pe.wait_ge(r_act, 2)
            pe.matmul(bank[7][0:1, 16:24], rs[:, 4:5], rw2[:], start=True, stop=True).then_inc(r_mm, 1)

            f_transpose("xn", 3, [(ln_out, 2)])
            f_transpose("xt", 3, [])

            def queries_keys(at, x):
                n = at["n"]
                pe.wait_ge(w_split, SPLIT_AT[n + "k" if n == "c" else n + "q"])
                pe.wait_ge(f_lo, f_split({"s": "xn", "t": "cq", "c": "to"}[n]))
                if n != "c":
                    f_gemm(n + "q", [(n + "q", x)], [])
                f_gemm(n + "k", [(n + "k", x)], [])
            def attention(a, x, source):
                vals = values(x)
                units, nu, nm = x["units"], len(x["units"]), len(x["maxima"])
                firsts = {min(u for u in range(nu) if units[u][0] == c) for c in range(NC)}

                def maxima(h, par, e):
                    k_both, _, q_high, _ = operands(x, par)
                    n = x["a0"] + h * nm + e
                    b = bank[M_BANKS[(par * nm + e) % 2]]
                    pe.wait_ge(a_mx, n - 2 + 1 + 2)
                    todo = []
                    for t, k0, w, at, diagonal in x["maxima"][e]:
                        todo.append((b[0:P, at:at + w], q_high[0:HD, t * P:(t + 1) * P], k_both[0:HD, k0:k0 + w]))
                        if diagonal:
                            todo.append((b[0:P, at + w - P:at + w], gain16[0:P, 0:P], mask_t))
                    for m, (o, l, r) in enumerate(todo):
                        mm = pe.matmul(o, l, r, start=(m == 0), stop=(m == len(todo) - 1), skip_group_check=True)
                    mm.then_inc(a_mm, 1)

                def scores(h, par, u):
                    k_both, k_high, q_high, q_low = operands(x, par)
                    (c, pieces), v = units[u], par * nu + u
                    n = x["u0"] + h * nu + u
                    b = bank[S_BANKS[v % 3]]
                    pe.wait_ge(s_exp, n - since(v, 2 * nu, 3) + 1 + 3)
                    todo = []
                    for s, n0, w, at, diagonal in pieces:
                        t0 = CH[c][0] + n0
                        todo.append((b[0:P, at:at + w], k_both[:, s * P:(s + 1) * P], q_high[:, t0:t0 + w]))
                        todo.append((b[0:P, at:at + w], k_high[0:HD + NT, s * P:(s + 1) * P],
                                     q_low[0:HD + NT, t0:t0 + w]))
                        if diagonal:
                            todo.append((b[0:P, at:at + P], gain16[0:P, 0:P], mask_s))
                    for m, (o, l, r) in enumerate(todo):
                        mm = pe.matmul(o, l, r, start=(m == 0), stop=(m == len(todo) - 1), skip_group_check=True)
                    mm.then_inc(s_sc, 1)

                def weigh(h, par, u):
                    (c, pieces), v = units[u], par * nu + u
                    n = x["u0"] + h * nu + u
                    o = bank[O_BANKS[(par * NC + c) % 2]]
                    if u in firsts:
                        pe.wait_ge(o_raw, x["b0"] + NC * h + c - 2 + 1 + 2)
                    pe.wait_ge(s_plo, n + 1 + R32)
                    todo = []
                    for s, n0, w, at, _ in pieces:
                        highs = vals[:, bass.ds(s * H * 129 + h * 129, HD + 1)]
                        lows = vals[:, bass.ds(s * H * 129 + h * 129 + HD + 1, HD)]
                        todo.append((o[0:HD + 1, n0:n0 + w], highs, exps16(x, v, 500, 0)[:, at:at + w]))
                        todo.append((o[0:HD + 1, n0:n0 + w], highs, exps16(x, v, 500, 1)[:, at:at + w]))
                        todo.append((o[0:HD, n0:n0 + w], lows, exps16(x, v, 500, 0)[:, at:at + w]))
                    for m, (o_, l, r) in enumerate(todo):
                        mm = pe.matmul(o_, l, r, start=(u in firsts and m == 0),
                                       stop=(u in x["ends"] and m == len(todo) - 1), skip_group_check=True)
                    mm.then_inc(s_pv, 1)

                def big_loaded(i, par):
                    pe.wait_ge(big_ld[par], 64 * (4 * a + 1) + 64 * i)

                def small_loaded(i, par):
                    pe.wait_ge(small_ld[par], 32 * (4 * a + 1) + 32 * i)
                    pe.wait_ge(m_sh, 2 * (x["h0"] + 2 * i + par) + 2)

                def turn(h, par):
                    pe.wait_ge(m_all, x["h0"] + h + 1)
                    pe.transpose(bank[6][0:NT, 0:P], mx[:, par, :], ident[0:P, 0:P]).then_inc(m_t, 1)

                def turn_sums(hd, c):
                    n = x["b0"] + NC * hd[0] + c
                    pe.wait_ge(o_raw, n + 1 + 2)
                    pe.wait_ge(o_norm, n - 1 + 1 + 1)
                    for j in range(CH[c][1] // P):
                        mm = pe.matmul(bank[6][0:P, 504 + j:505 + j],
                                       oraw[HD:HD + 1, (hd[2] * NC + c) % 2, j * P:(j + 1) * P],
                                       ident[HD:HD + 1, HD:HD + 1], start=(j == 0), stop=(j == CH[c][1] // P - 1),
                                       skip_group_check=True)
                    mm.then_inc(o_den, 1)

                def spread(hd, c):
                    pe.wait_ge(o_rec, x["b0"] + NC * hd[0] + c + 1)
                    for j in range(CH[c][1] // P):
                        mm = pe.matmul(bank[6][HD:128, j * P:(j + 1) * P], rinv[:, j:j + 1].to_broadcast([P, HD]),
                                       ident[0:P, 0:P], start=(j == 0), stop=(j == CH[c][1] // P - 1),
                                       skip_group_check=True)
                    mm.then_inc(o_bc, 1)

                def head(hd, before, after):
                    h, _, par = hd
                    for u in range(nu):
                        if u + AHEAD < nu:
                            scores(h, par, u + AHEAD)
                        elif after:
                            if u + AHEAD == nu:
                                small_loaded(*after[1:])
                            scores(after[0], after[2], u + AHEAD - nu)
                        if after:
                            for e in x["early"][u]:
                                if e == 0:
                                    big_loaded(*after[1:])
                                maxima(after[0], after[2], e)
                        weigh(h, par, u)
                        for one in due(x, u, 2, hd, before):
                            spread(*one)
                        for one in due(x, u, 1, hd, before):
                            turn_sums(*one)
                        if after and u == nu - 5:
                            turn(after[0], after[2])

                t0 = T_TILES[x["n"] + "v"][0]
                pe.wait_ge(w_split, SPLIT_AT[x["n"] + "v"])
                for j in range(NT):
                    pe.wait_ge(t_ev, t0 + j + 1)
                    for k in range(KD):
                        for m, (p, r) in enumerate(((0, 0), (0, 1), (1, 0))):
                            mm = pe.matmul(bank[3 + j % 2][0:P, :], split(source)[:, p, k, j * P:(j + 1) * P],
                                           slot(x["n"] + "v")[:, r, k, :], start=(k == 0 and m == 0),
                                           stop=(k == KD - 1 and m == 2))
                    mm.then_inc(t_mm, 1)
                    for e in x["first"][j]:
                        if e == 0:
                            pe.wait_ge(f_act, f_read(x["n"] + "k"))
                            big_loaded(0, 0)
                        maxima(0, 0, e)
                turn(0, 0)
                pe.wait_ge(t_ev, t_read(x["n"] + "v"))
                pe.wait_ge(v_lo, (a + 1) * NT + 1)
                pe.wait_ge(eight, a + 1)
                small_loaded(0, 0)
                for u in range(AHEAD):
                    scores(0, 0, u)
                head_loop(pe, head)
                tail(x, [(2, spread), (1, turn_sums)])

            def attention_over(k):
                return [(o_ev, ATT_END[k]["b"] + 2), (s_exp, ATT_END[k]["u"] + 3), (a_mx, ATT_END[k]["a"] + 2)]

            queries_keys(ATT[0], 4)
            attention(0, ATT[0], 4)
            f_gemm("so", [("so", 4)], attention_over(0) + [(w_split, SPLIT_AT["so"])])
            f_gemm("cq", [("cq", 1)], [(f_lo, f_split("so")), (w_split, SPLIT_AT["cq"])])
            queries_keys(ATT[1], 5)
            pe.wait_ge(pool_c, 12)
            attention(1, ATT[1], 5)
            f_gemm("to", [("to", 5)], attention_over(1) + [(w_split, SPLIT_AT["to"])])
            queries_keys(ATT[2], 4)
            attention(2, ATT[2], 4)
            t_gemm("co", [(of(4), "co")], attention_over(2) + [(w_split, SPLIT_AT["co"])])
            f_transpose("h2", 3, [(ln_out, 3)])
            for i in range(4):
                f_gemm(f"up{i}", [(f"up{i}", 6)], [(f_lo, f_split("h2")), (w_split, SPLIT_AT[f"up{i}"])])
            t_gemm("down", [(lambda s, k, n, i=i: wide[s][:, 4 * i + k, n], f"down{i}") for i in range(4)],
                   [(f_lo, f_split("up3")), (w_split, SPLIT_AT["down3"])])

        @block.scalar
        def _(act):
            def f_tile(name, i, c, w, t_dst, hi_dst, func, scale, bias):
                g, lw = F_TILES[name][0] + i * NC + c, LOWS[name][0] + i * NC + c
                act.wait_ge(f_mm, g + 1)
                act.wait_ge(f_lo, lw + 1)
                act.activation(t_dst, bank[c][:, 0:w], func, bias=bias, scale=scale)
                act.activation(hi_dst, bank[c][:, 0:w], func, bias=bias, scale=scale).then_inc(f_act, 1)

            def f_evac(name, dst, scale, bias, func=ACT.Identity):
                with act.Fori(0, KD) as i:
                    for c, (n0, w) in enumerate(CH):
                        f_tile(name, i, c, w, t32[:, c, 0:w], dst(0, i, n0, w), func, scale, bias(i))

            def page_of(p):
                return lambda s, i, n0, w: page[p][:, 0:KD * N].bitcast(F16)[:, bass.ds(i * N + s * KD * N + n0, w)]

            def layer_norm_sd(k):
                act.wait_ge(ln_var, k)
                act.activation(rstd[:], rstd[:], ACT.Sqrt).then_inc(ln_sd, 1)

            def vecs(name):
                return lambda i: vcol(name, i)

            load_x(act, 0)
            act.wait_ge(ln_var, 1)
            act.activation(bns[:, 0, :], bns[:, 0, :], ACT.Sqrt)
            layer_norm_sd(1)
            for k in range(KD):
                for c, (n0, w) in enumerate(CH):
                    f_tile("hT", k, c, w, cols(2)[:, k, n0:n0 + w], split(3)[:, 0, k, n0:n0 + w], ACT.Identity, 1.0, 0.0)

            act.wait_ge(win_s, 3)
            act.dma_start(win_d, gwi).then_inc(win_io, 16)
            act.wait_ge(win_io, 16)
            act.dma_start(win, win_d.rearrange("(o g) c -> o (g c)", o=1)).then_inc(win_io, 16)
            for j in range(NT):
                act.wait_ge(t_ev, T_TILES["P"][0] + j + 1 + 2)
                act.dma_start(proj_d[j * P:(j + 1) * P, :], rowst[0:P, j % 2, :]).then_inc(p_st[j % 2], 16)
            def attributes(n0, s, loads):
                act.wait_ge(ea_ld[s], 16 * loads)
                act.wait_ge(e_mm, n0 * GE)
                act.activation(eah[:, s, :], eas[:, s, :], ACT.Copy).then_inc(ea_hi, 1)

            def relus(n0, s):
                behind = act.value_load(win[:, bass.ds(n0 * 4 + 3, 1)], min_val=NT, max_val=NG * NT + NT)
                act.wait_ge(s_mm, behind)
                for q in range(GE):
                    n = n0 * GE + q
                    act.wait_ge(e_sum, n + 1 + 2 * GE)
                    act.activation(relu[:, s * GE + q, 0, :], esum[:, q % 2, :], ACT.Relu).then_inc(e_hi, 1)

            act.wait_ge(win_io, 32)
            attributes(0, 0, 1)
            with act.Fori(0, NG // 2 - 1) as i:
                attributes(2 * i + 1, 1, i + 1)
                relus(2 * i, 0)
                attributes(2 * i + 2, 0, i + 2)
                relus(2 * i + 1, 1)
            attributes(NG - 1, 1, NG // 2)
            relus(NG - 2, 0)
            relus(NG - 1, 1)

            f_evac("aggT", page_of(4), 1.0, lambda i: 0.0)
            f_evac("M", page_of(5), 1.0 / SG, lambda i: 0.0)
            for gate, p, b in (("r", 6, 0), ("z", 7, KD)):
                with act.Fori(0, KD) as i:
                    for c, (n0, w) in enumerate(CH):
                        act.wait_ge(f_mm, F_TILES[gate][0] + i * NC + c + 1)
                        act.activation(page[p][:, bass.ds(i * N + n0, w)], bank[c][:, 0:w], ACT.Sigmoid,
                                       bias=bsum[:, bass.ds(i + b, 1)], scale=1.0 / SG).then_inc(f_act, 1)
            with act.Fori(0, KD) as i:
                for c, (n0, w) in enumerate(CH):
                    act.wait_ge(n_hr, i * NC + c + 1)
                    act.activation(page[4][:, bass.ds(i * N + n0, w)], t32[:, c, 0:w], ACT.Tanh,
                                   bias=vcol("b_ih", i + 2 * KD), scale=1.0 / SG).then_inc(f_act, 1)

            act.wait_ge(t_ev, t_read("x1"))
            act.dma_start(x1_d, page[1][0:P, 0:NT * D]).then_inc(sp_io, 16)
            layer_norm_sd(2)
            layer_norm_sd(3)
            act.wait_ge(ln_tile, NT)
            act.dma_start(xl_d, page[2][0:P, 0:NT * D]).then_inc(sp_io, 16)
            act.wait_ge(r_mm, 1)
            act.activation(rs[:, 0:KD], bank[7][:, 0:KD], ACT.Copy, scale=1.0 / N).then_inc(r_act, 1)
            act.wait_ge(r_mm, 2)
            act.activation(rs[:, 4:5], bank[7][:, 8:9], ACT.Gelu, bias=vcol("rb1")).then_inc(r_act, 1)

            for name, hi, w_, b_ in (("xn", 4, "ns_w", "ns_b"), ("xt", 5, "nt_w", "nt_b")):
                for k in range(KD):
                    for c, (n0, w) in enumerate(CH):
                        f_tile(name, k, c, w, t32[:, c, 0:w] if name == "xn" else cols(6)[:, k, n0:n0 + w],
                               split(hi)[:, 0, k, n0:n0 + w], ACT.Identity, vcol(w_, k), vcol(b_, k))
            act.wait_ge(f_act, f_read("xt"))
            act.dma_start(xt_d, page[6][:, 0:KD * N]).then_inc(sp_io, 16)

            def value_highs(x, a):
                t0 = T_TILES[x["n"] + "v"][0]
                with act.Fori(0, NT // 2) as i:
                    for b in range(2):
                        act.wait_ge(t_ev, t0 + 2 * i + b + 1 + 2)
                        act.activation(
                            values(x)[:, bass.ds((2 * i + b) * H * 129, H * 129)].rearrange(
                                "p (h c) -> p h c", h=H)[:, :, 0:HD],
                            rowst[0:P, b, :].rearrange("p (h c) -> p h c", h=H), ACT.Copy).then_inc(v_hi, 1)

            def exponentials(x):
                nu = len(x["units"])

                def exps(h, par, u):
                    n, v = x["u0"] + h * nu + u, par * nu + u
                    w = sum(piece[2] for piece in x["units"][u][1])
                    b = bank[S_BANKS[v % 3]]
                    act.wait_ge(s_sc, n + 1)
                    act.wait_ge(s_plo, n - since(v, 2 * nu, R32) + 1 + R32)
                    act.activation(exps32(x, v, w), b[0:P, 0:w], ACT.Exp, scale=QK_SCALE)
                    act.wait_ge(s_pv, n - since(v, 2 * nu, R16) + 1 + R16)
                    act.activation(exps16(x, v, w, 0), b[0:P, 0:w], ACT.Exp, scale=QK_SCALE).then_inc(s_exp, 1)

                def outputs(hd, c):
                    n, at = x["b0"] + NC * hd[0] + c, (hd[2] * NC + c) % 2
                    u = [e for e in x["ends"] if x["ends"][e] == c][0]
                    act.wait_ge(s_pv, x["u0"] + hd[0] * nu + u + 1 + R16)
                    act.wait_ge(o_norm, n - 2 + 1 + 1)
                    act.activation(oraw[:, at, 0:CH[c][1]], bank[O_BANKS[at]][0:HD + 1, 0:CH[c][1]],
                                   ACT.Copy).then_inc(o_raw, 1)

                def output_high(hd, c):
                    n, (n0, w) = x["b0"] + NC * hd[0] + c, CH[c]
                    at = slice(64 * hd[2], 64 * hd[2] + 64)
                    act.wait_ge(o_norm, n + 1 + 1)
                    act.activation(page[x["o"]][at, 0:KD * N].bitcast(F16)[:, bass.ds(hd[1] * N + n0, w)],
                                   onorm[at, 0:w], ACT.Copy).then_inc(o_hi, 1)

                def head(hd, before, after):
                    for u in range(nu):
                        if u + 2 < nu:
                            exps(hd[0], hd[2], u + 2)
                        elif after:
                            exps(after[0], after[2], u + 2 - nu)
                        for one in due(x, u, 0, hd, before):
                            outputs(*one)
                        for one in due(x, u, 4, hd, before):
                            output_high(*one)

                for u in range(2):
                    exps(0, 0, u)
                head_loop(act, head)
                tail(x, [(4, output_high)])

            x = ATT[0]
            act.wait_ge(eb_ld, 32)
            f_evac("sq", page_of(7), 1.0 / SF, lambda i: vsp[:, bass.ds(i, 1)])
            f_evac("sk", page_of(3), 1.0 / SF, lambda i: vsp[:, bass.ds(i + KD, 1)])
            act.wait_ge(sp_io, 48)
            value_highs(x, 0)
            exponentials(x)
            f_evac("so", page_of(1), 1.0 / SF, lambda i: vsp[:, bass.ds(i + 2 * KD, 1)])
            f_evac("cq", page_of(2), 1.0 / SF, vecs("cq_b"))
            x = ATT[1]
            f_evac("tq", page_of(1), 1.0 / SF, lambda i: vtp[:, bass.ds(i, 1)])
            f_evac("tk", page_of(6), 1.0 / SF, lambda i: vtp[:, bass.ds(i + KD, 1)])
            value_highs(x, 1)
            exponentials(x)
            act.wait_ge(small_ld[1], 32 * 8)
            act.dma_start(page[1][:, 0:KD * N], xt_d).then_inc(back, 16)
            with act.Fori(0, KD) as i:
                for c, (n0, w) in enumerate(CH):
                    act.wait_ge(to_sum, i * NC + c + 1)
                    act.activation(page_of(4)(0, i, n0, w), t32[:, c, 0:w], ACT.Identity,
                                   bias=vtp[:, bass.ds(i + 2 * KD, 1)]).then_inc(f_act, 1)
            x = ATT[2]
            act.wait_ge(f_mm, F_TILES["to"][1])
            act.dma_start(page[5][0:P, 0:NT * D], xl_d).then_inc(back, 16)
            f_evac("ck", page_of(1), 1.0 / SF, vecs("ck_b"))
            value_highs(x, 2)
            exponentials(x)
            act.wait_ge(small_ld[1], 32 * 12)
            act.dma_start(page[2][0:P, 0:NT * D], x1_d).then_inc(back_x1, 16)
            layer_norm_sd(4)
            for k in range(KD):
                for c, (n0, w) in enumerate(CH):
                    f_tile("h2", k, c, w, t32[:, c, 0:w], split(6)[:, 0, k, n0:n0 + w], ACT.Identity,
                           vcol("nm_w", k), vcol("nm_b", k))
            act.wait_ge(xs_done, 1)
            for m in range(4):
                f_evac(f"up{m}", lambda s, i, n0, w: hidden(s, m, i, n0, w), 1.0 / SF,
                       lambda i: vcol("m1_b", i + 4 * m), ACT.Gelu)

        @block.vector
        def _(dve):
            class Chain:
                start, k = 0, 0

            chain = Chain()

            def link(ins):
                chain.k += 1
                ins.then_inc(link_s, 1)
                dve.wait_ge(link_s, chain.start + chain.k)

            def row_stats(j, src):
                return dve.bn_stats(stats[:, j, :], rows(src)[:, j, :])

            def layer_norm(k, src, dst, have_stats=False, tile_out=None):
                if not have_stats:
                    for j in range(NT):
                        last = row_stats(j, src)
                    link(last)
                for j in range(NT):
                    last = dve.bn_aggr(mv[:, j, :], stats[:, j, :])
                link(last)
                dve.tensor_scalar(rstd[:], mv[:, :, 1], EPS, None, ALU.add).then_inc(ln_var, 1)
                dve.wait_ge(ln_sd, k)
                link(dve.reciprocal(rstd[:], rstd[:]))
                for j in range(NT):
                    last = dve.tensor_scalar(rows(dst)[:, j, :], rows(src)[:, j, :], mv[:, j, 0:1], rstd[:, j:j + 1],
                                             ALU.subtract, ALU.mult)
                    if tile_out:
                        last.then_inc(ln_tile, 1)
                        tile_out(j)
                if tile_out:
                    dve.wait_ge(ln_tile, NT)
                else:
                    last.then_inc(ln_out, 1)
                    dve.wait_ge(ln_out, k - 1 if k > 1 else k)

            def low(name, i, c, w, t_src, hi_src, lo_dst):
                dve.wait_ge(f_act, F_TILES[name][0] + i * NC + c + 1 + NC)
                dve.tensor_tensor(lo_dst, t_src, hi_src, ALU.subtract).then_inc(f_lo, 1)

            def page_of(p):
                return lambda s, i, n0, w: page[p][:, 0:KD * N].bitcast(F16)[:, bass.ds(i * N + s * KD * N + n0, w)]

            def f_lows(name, dst):
                with dve.Fori(0, KD) as i:
                    for c, (n0, w) in enumerate(CH):
                        low(name, i, c, w, t32[:, c, 0:w], dst(0, i, n0, w), dst(1, i, n0, w))

            dve.memset(ones16[:], 1.0)
            dve.memset(ones32[:], 1.0)
            dve.memset(rows(5), 0.0)
            dve.memset(lg[:], -3e38)
            link(dve.memset(cnt[:], 0.0))
            dve.wait_ge(pool_c, 8)
            dve.tensor_scalar(gain16[:], ident[:], MASK_GAIN, None, ALU.mult).then_inc(dve_c, 1)

            dve.wait_ge(in_ld, 64)
            dve.tensor_tensor(bsum[:, 0:8], vec[:, VEC["b_ih"][0]:VEC["b_ih"][0] + 8],
                              vec[:, VEC["b_hh"][0]:VEC["b_hh"][0] + 8], ALU.add)
            dve.tensor_scalar(bsum[:, 8:12], vec[:, VEC["b_hh"][0] + 8:VEC["b_hh"][0] + 12], SG, None, ALU.mult)

            v0 = VEC["gamma"][0]
            dve.tensor_scalar(bns[:, 0, :], vec[:, v0 + 12:v0 + 16], EPS, None, ALU.add)

            dve.wait_ge(x_ld, 32)
            layer_norm(1, 1, 6)
            for k in range(KD):
                for c, (n0, w) in enumerate(CH):
                    low("hT", k, c, w, cols(2)[:, k, n0:n0 + w], split(3)[:, 0, k, n0:n0 + w],
                        split(3)[:, 1, k, n0:n0 + w])
            dve.tensor_copy(dstf, dsts)
            link(dve.tensor_copy(grp_f, grp_i))
            dve.tensor_reduce(gw[:, 0:1], grp_f, AX.X, ALU.min)
            link(dve.tensor_reduce(gw[:, 1:2], grp_f, AX.X, ALU.max))
            edges_of_tiles = node_id[0:NG, P:N:P]
            for q in range(2):
                last = dve.tensor_scalar(gw[:, 2 + 9 * q:11 + 9 * q], edges_of_tiles, gw[:, q:q + 1], None, ALU.is_le)
            link(last)
            for q in range(2):
                last = dve.tensor_reduce(gw[:, 21 + q:22 + q], gw[:, 2 + 9 * q:11 + 9 * q], AX.X, ALU.add)
            link(last)
            link(dve.tensor_scalar(gw[:, 23:24], gw[:, 22:23], 1.0, None, ALU.add))
            dve.tensor_tensor(gw[:, 20:21], gw[:, 23:24], gw[:, 21:22], ALU.subtract).then_inc(win_s, 1)
            dve.wait_ge(win_s, 2)
            dve.tensor_copy(gwi[:, 0:1], gw[:, 21:22])
            dve.tensor_copy(gwi[:, 1:2], gw[:, 23:24])
            link(dve.tensor_scalar(gw[:, 24:26], bank[7][0:NG, 0:2], float(NT), None, ALU.add))
            link(dve.tensor_tensor(gw[:, 24:25], gw[:, 24:25], gw[:, 21:22], ALU.subtract))
            dve.tensor_copy(gwi[:, 2:4], gw[:, 24:26]).then_inc(win_s, 1)

            dve.wait_ge(row_ld, 16)
            t0 = T_TILES["P"][0]
            with dve.Fori(0, NT // 2) as i:
                for b in range(2):
                    dve.wait_ge(t_mm, t0 + 2 * i + b + 1)
                    dve.wait_ge(p_st[b], 16 * i + 16)
                    dve.scalar_tensor_tensor(out=rowst[0:P, b, :], in0=bank[3 + b][0:P, :], scalar=1.0 / SG,
                                             in1=rowb[:], op0=ALU.mult, op1=ALU.add).then_inc(t_ev, 1)

            def tiles(n0, s, gath_done):
                def relu_low(q):
                    dve.wait_ge(e_hi, n0 * GE + q + 1 + 2)
                    dve.scalar_tensor_tensor(out=relu[:, s * GE + q, 1, :], in0=esum[:, q % 2, :], scalar=0.0,
                                             in1=relu[:, s * GE + q, 0, :], op0=ALU.max,
                                             op1=ALU.subtract).then_inc(e_lo, 1)

                for q in range(GE):
                    n = n0 * GE + q
                    dve.wait_ge(e_mm, n + 1 + GE)
                    dve.wait_ge(g_ld[s * GE + q], gath_done)
                    dve.wait_ge(e_lo, n + 1)
                    dve.scalar_tensor_tensor(out=esum[:, q % 2, :], in0=bank[E_BANKS[q]][0:P, :], scalar=1.0 / SG,
                                             in1=gath[:, s * GE + q, :], op0=ALU.mult, op1=ALU.add).then_inc(e_sum, 1)
                    dve.tensor_scalar(onehot[:, s * GE + q, :], node_id[:], dstf[:, bass.ds(n, 1)], None, ALU.is_equal)
                    if q >= 1:
                        relu_low(q - 1)
                relu_low(GE - 1)

            def windows(n0):
                first, end, number = (dve.value_load(win[:, bass.ds(n0 * 4 + c, 1)], min_val=lo, max_val=hi)
                                      for c, lo, hi in ((0, 0, NT - 1), (1, 1, NT), (2, 1, NG * NT + NT)))
                with dve.Fori(first, end) as j:
                    dve.wait_ge(s_mm, number + j + 1)
                    dve.wait_ge(s_add, number + j)
                    dve.tensor_tensor(page[5][0:P, bass.ds(j * D, D)], page[5][0:P, bass.ds(j * D, D)],
                                      bank[2][0:P, :], ALU.add)
                    dve.tensor_tensor(cnt[:, bass.ds(j, 1)], cnt[:, bass.ds(j, 1)], bank[5][0:P, 0:1],
                                      ALU.add).then_inc(s_add, 1)

            dve.wait_ge(win_io, 32)
            tiles(0, 0, 16)
            with dve.Fori(0, NG // 2 - 1) as i:
                tiles(2 * i + 1, 1, 16 * (i + 1))
                windows(2 * i)
                tiles(2 * i + 2, 0, 16 * (i + 2))
                windows(2 * i + 1)
            tiles(NG - 1, 1, 16 * (NG // 2))
            windows(NG - 2)
            windows(NG - 1)
            dve.memset(stats[:], 0.0).then_inc(agg_done, 1)

            f_lows("aggT", page_of(4))
            dve.wait_ge(c_mt, 1)
            dve.wait_ge(b2_ld, 16)
            link(dve.tensor_tensor(cntb.rearrange("p (a b) -> p a b", a=NT),
                                   bank[7][0:NT, 0:P].unsqueeze(1).to_broadcast([NT, NT, P]), blockdiag[:], ALU.mult))
            link(dve.tensor_scalar(b2f, b2f, SG, None, ALU.mult))
            dve.tensor_copy(cnth[:, 0, :], cntb)
            link(dve.tensor_copy(b2h[:, 0, :], b2f))
            link(dve.tensor_tensor(cnth[:, 1, :], cntb, cnth[:, 0, :], ALU.subtract))
            dve.tensor_tensor(b2h[:, 1, :], b2f, b2h[:, 0, :], ALU.subtract).then_inc(c_s, 1)
            f_lows("M", page_of(5))
            link(dve.reciprocal(bns[:, 0, :], bns[:, 0, :]))
            link(dve.tensor_tensor(bns[:, 0, :], bns[:, 0, :], vec[:, v0:v0 + 4], ALU.mult))
            link(dve.tensor_tensor(bns[:, 1, :], bns[:, 0, :], vec[:, v0 + 8:v0 + 12], ALU.mult))
            link(dve.tensor_tensor(bns[:, 1, :], vec[:, v0 + 4:v0 + 8], bns[:, 1, :], ALU.subtract))

            def new_front(i, c, n0, w):
                dve.wait_ge(f_mm, F_TILES["n"][0] + i * NC + c + 1)
                r = page[6][:, bass.ds(i * N + n0, w)]
                link(dve.scalar_tensor_tensor(out=t32[:, c, 0:w], in0=bank[5 + c][:, 0:w],
                                              scalar=bsum[:, bass.ds(i + 8, 1)], in1=r, op0=ALU.add, op1=ALU.mult))
                dve.tensor_tensor(t32[:, c, 0:w], t32[:, c, 0:w], bank[c][:, 0:w], ALU.add).then_inc(n_hr, 1)

            def new_back(i):
                n, h, d, z = (page[p][:, bass.ds(i * N, N)] for p in (4, 2, 6, 7))
                dve.wait_ge(f_act, F_TILES["n"][0] + (i + 1) * NC + NC)
                link(dve.tensor_tensor(d, h, n, ALU.subtract))
                link(dve.tensor_tensor(d, d, z, ALU.mult))
                link(dve.tensor_tensor(d, d, n, ALU.add))
                link(dve.tensor_scalar(d, d, bns[:, 0, bass.ds(i, 1)], bns[:, 1, bass.ds(i, 1)], ALU.mult, ALU.add))
                dve.tensor_tensor(h, h, d, ALU.add).then_inc(n_new, 1)

            base = chain.start + chain.k
            links = NC + 4
            dve.wait_ge(f_act, f_read("z"))
            for c, (n0, w) in enumerate(CH):
                new_front(0, c, n0, w)
            base += NC
            with dve.Fori(0, KD - 1) as i:
                chain.start, chain.k = base + i * links, 0
                for c, (n0, w) in enumerate(CH):
                    new_front(i + 1, c, n0, w)
                new_back(i)
                assert chain.k == links
            chain.start, chain.k = base + (KD - 1) * links, 0
            new_back(KD - 1)

            t0 = T_TILES["x1"][0]
            for j in range(NT + 1):
                if j < NT:
                    dve.wait_ge(t_mm, t0 + j + 1)
                    dve.tensor_tensor(rows(1)[:, j, :], rows(1)[:, j, :], bank[3 + j % 2][0:P, :],
                                      ALU.add).then_inc(t_ev, 1)
                if j:
                    dve.wait_ge(t_ev, t0 + j + 2)
                    last = row_stats(j - 1, 1)
            link(last)

            def next_stats(j):
                if j:
                    dve.wait_ge(ln_tile, j)
                    row_stats(j - 1, 2)

            layer_norm(2, 1, 2, True, next_stats)
            link(row_stats(NT - 1, 2))
            layer_norm(3, 2, 3, True)
            dve.wait_ge(r_mm, 3)
            link(dve.tensor_tensor(lg[:, 0:8], bank[7][0:1, 16:24], rb2[:], ALU.add))
            dve.tensor_copy(lg[:, 8:12], lg[:, 0:4])
            link(dve.tensor_copy(lg[:, 16:20], lg[:, 4:8]))
            dve.max(lg[:, 24:32], lg[:, 8:16])
            link(dve.max(lg[:, 32:40], lg[:, 16:24]))
            dve.max_index(choice[:, 0:8], lg[:, 24:32], lg[:, 8:16]).then_inc(r_ix, 1)
            dve.max_index(choice[:, 8:16], lg[:, 32:40], lg[:, 16:24]).then_inc(r_ix, 1)

            for name, p in (("xn", 4), ("xt", 5)):
                for k in range(KD):
                    for c, (n0, w) in enumerate(CH):
                        low(name, k, c, w, t32[:, c, 0:w] if name == "xn" else cols(6)[:, k, n0:n0 + w],
                            split(p)[:, 0, k, n0:n0 + w], split(p)[:, 1, k, n0:n0 + w])

            def values_out(x, a, maxima):
                t0 = T_TILES[x["n"] + "v"][0]
                dve.wait_ge(row_ld, 16 * (a + 2))
                dve.memset(values(x).rearrange("p (s c) -> p s c", c=129)[:, :, HD:HD + 1], 1.0)
                for par in range(2):
                    last = dve.memset(operands(x, par)[1][HD:HD + NT, :], 1.0 / QK_SCALE)
                last.then_inc(eight, 1)
                for j in range(NT):
                    dve.wait_ge(t_mm, t0 + j + 1)
                    dve.wait_ge(v_lo, a * NT + j - 2 + 1 + 1 if j >= 2 else a * NT + 1)
                    dve.scalar_tensor_tensor(out=rowst[0:P, j % 2, :], in0=bank[3 + j % 2][0:P, :], scalar=1.0 / SF,
                                             in1=rowb[:], op0=ALU.mult, op1=ALU.add).then_inc(t_ev, 1)
                    for e in x["first"][j]:
                        maxima(0, 0, e)
                    v = values(x)[:, j * H * 129:(j + 1) * H * 129].rearrange("p (h c) -> p h c", h=H)
                    dve.wait_ge(v_hi, a * NT + j + 1)
                    dve.wait_ge(t_ev, t0 + j + 1 + 2)
                    dve.tensor_tensor(v[:, :, HD + 1:2 * HD + 1], rowst[0:P, j % 2, :].rearrange("p (h c) -> p h c", h=H),
                                      v[:, :, 0:HD], ALU.subtract).then_inc(v_lo, 1)

            def attention(x, a):
                units, nu, nm = x["units"], len(x["units"]), len(x["maxima"])

                def prob_low(h, par, u):
                    n, v = x["u0"] + h * nu + u, par * nu + u
                    w = sum(piece[2] for piece in units[u][1])
                    dve.wait_ge(s_exp, n + 1 + 3)
                    dve.tensor_tensor(exps16(x, v, w, 1), exps32(x, v, w), exps16(x, v, w, 0),
                                      ALU.subtract).then_inc(s_plo, 1)

                def maxima(h, par, e):
                    pieces = x["maxima"][e]
                    t, k0, w, _, _ = pieces[0]
                    b = bank[M_BANKS[(par * nm + e) % 2]]
                    dve.wait_ge(a_mm, x["a0"] + h * nm + e + 1)
                    dve.tensor_reduce(mxs[:, par, t:t + len(pieces), k0 // 500],
                                      b[0:P, 0:len(pieces) * w].rearrange("p (a n) -> p a n", a=len(pieces)), AX.X,
                                      ALU.max).then_inc(a_mx, 1)

                def all_maxima(h, par):
                    dve.wait_ge(a_mx, x["a0"] + h * nm + nm + 2)
                    dve.tensor_reduce(mx[:, par, :], mxs[:, par, :, :], AX.X, ALU.max).then_inc(m_all, 1)

                def shifts(h, par, half):
                    t = slice(half * NT // 2, (half + 1) * NT // 2)
                    dve.wait_ge(m_t, x["h0"] + h + 1)
                    dve.scalar_tensor_tensor(
                        out=operands(x, par)[3][HD:HD + NT, :].rearrange("p (a b) -> p a b", a=NT)[:, t, :],
                        in0=bank[6][0:NT, 0:P].unsqueeze(1).to_broadcast([NT, NT // 2, P]), scalar=-QK_SCALE,
                        in1=blockdiag[:, t, :], op0=ALU.mult, op1=ALU.mult).then_inc(m_sh, 1)

                def invert(hd, c):
                    n = x["b0"] + NC * hd[0] + c
                    dve.wait_ge(o_den, n + 1)
                    dve.reciprocal(rinv[:, 0:CH[c][1] // P], bank[6][0:P, 504:504 + CH[c][1] // P]).then_inc(o_rec, 1)

                def normalise(hd, c):
                    n, w = x["b0"] + NC * hd[0] + c, CH[c][1]
                    at = slice(64 * hd[2], 64 * hd[2] + 64)
                    dve.wait_ge(o_bc, n + 1)
                    dve.wait_ge(o_ev, n - 1 + 1 + 2)
                    dve.tensor_tensor(onorm[at, 0:w], bank[6][HD:128, 0:w], oraw[0:HD, (hd[2] * NC + c) % 2, 0:w],
                                      ALU.mult).then_inc(o_norm, 1)

                def output_low(hd, c):
                    n, (n0, w) = x["b0"] + NC * hd[0] + c, CH[c]
                    at = slice(64 * hd[2], 64 * hd[2] + 64)
                    hi, lo = (page[x["o"]][at, 0:KD * N].bitcast(F16)[:, bass.ds(hd[1] * N + (p * KD * N + n0), w)]
                              for p in range(2))
                    dve.wait_ge(o_hi, n + 1)
                    dve.tensor_tensor(lo, onorm[at, 0:w], hi, ALU.subtract).then_inc(o_ev, 1)

                def head(hd, before, after):
                    h, _, par = hd
                    for u in range(nu):
                        for one in due(x, u, 2, hd, before):
                            invert(*one)
                        if u + 1 < nu:
                            prob_low(h, par, u + 1)
                        elif after:
                            prob_low(after[0], after[2], 0)
                        if after:
                            for e in x["early"][u]:
                                maxima(after[0], after[2], e)
                            if u == nu - 6:
                                all_maxima(after[0], after[2])
                        for one in due(x, u, 5, hd, before):
                            output_low(*one)
                        for one in due(x, u, 3, hd, before):
                            normalise(*one)
                        if after and u in (nu - 5, nu - 4):
                            shifts(after[0], after[2], u - (nu - 5))

                link(dve.memset(mxs[:], -3e38))
                values_out(x, a, maxima)
                all_maxima(0, 0)
                for half in range(2):
                    shifts(0, 0, half)
                prob_low(0, 0, 0)
                head_loop(dve, head)
                tail(x, [(2, invert), (3, normalise), (5, output_low)])

            f_lows("sq", page_of(7))
            f_lows("sk", page_of(3))
            dve.wait_ge(sp_io, 48)
            attention(ATT[0], 0)
            f_lows("so", page_of(1))
            f_lows("cq", page_of(2))
            f_lows("tq", page_of(1))
            f_lows("tk", page_of(6))
            attention(ATT[1], 1)
            dve.wait_ge(back, 16)
            g0, l0 = F_TILES["to"][0], LOWS["to"][0]
            with dve.Fori(0, KD) as i:
                for c, (n0, w) in enumerate(CH):
                    dve.wait_ge(f_mm, g0 + i * NC + c + 1)
                    dve.wait_ge(f_lo, l0 + i * NC + c + 1)
                    dve.scalar_tensor_tensor(out=t32[:, c, 0:w], in0=bank[c][:, 0:w], scalar=1.0 / SF,
                                             in1=page[1][:, bass.ds(i * N + n0, w)], op0=ALU.mult,
                                             op1=ALU.add).then_inc(to_sum, 1)
                for c, (n0, w) in enumerate(CH):
                    dve.wait_ge(f_act, g0 + i * NC + c + 1 + NC)
                    dve.scalar_tensor_tensor(out=page_of(4)(1, i, n0, w), in0=t32[:, c, 0:w],
                                             scalar=vtp[:, bass.ds(i + 2 * KD, 1)], in1=page_of(4)(0, i, n0, w),
                                             op0=ALU.add, op1=ALU.subtract).then_inc(f_lo, 1)
            f_lows("ck", page_of(1))
            attention(ATT[2], 2)
            dve.wait_ge(back, 32)
            dve.wait_ge(row_ld, 16 * 5)
            for j in range(NT):
                last = dve.tensor_tensor(rows(5)[:, j, :], rows(5)[:, j, :], rowb[:], ALU.add)
            last.then_inc(y_st, 1)
            dve.wait_ge(y_st, 1)
            t0 = T_TILES["co"][0]
            with dve.Fori(0, NT // 2) as i:
                for b in range(2):
                    dve.wait_ge(t_mm, t0 + 2 * i + b + 1)
                    y = page[5][0:P, bass.ds((2 * i + b) * D, D)]
                    dve.scalar_tensor_tensor(out=y, in0=bank[3 + b][0:P, :], scalar=1.0 / SF, in1=y, op0=ALU.mult,
                                             op1=ALU.add).then_inc(t_ev, 1)
                for b in range(2):
                    dve.wait_ge(t_ev, t0 + 2 * i + b + 1 + 2)
                    last = dve.bn_stats(stats[:].rearrange("p t s -> p (t s)")[:, bass.ds((2 * i + b) * 6, 6)],
                                        page[5][0:P, bass.ds((2 * i + b) * D, D)])
                last.then_inc(co_stats, 1)
            dve.wait_ge(co_stats, NT // 2)
            layer_norm(4, 5, 3, True)
            dve.wait_ge(row_ld, 16 * 6)
            dve.wait_ge(back_x1, 16)
            link(dve.tensor_tensor(page[5][0:P, 0:NT * D], page[5][0:P, 0:NT * D], page[2][0:P, 0:NT * D], ALU.add))
            for k in range(KD):
                for c, (n0, w) in enumerate(CH):
                    low("h2", k, c, w, t32[:, c, 0:w], split(6)[:, 0, k, n0:n0 + w], split(6)[:, 1, k, n0:n0 + w])
            for j in range(NT):
                last = dve.tensor_tensor(rows(5)[:, j, :], rows(5)[:, j, :], rowb[:], ALU.add)
            last.then_inc(xs_done, 1)
            dve.wait_ge(xs_done, 1)
            for m in range(4):
                f_lows(f"up{m}", lambda s, i, n0, w: hidden(s, m, i, n0, w))
            t0 = T_TILES["down"][0]
            with dve.Fori(0, NT // 2) as i:
                for b in range(2):
                    dve.wait_ge(t_mm, t0 + 2 * i + b + 1)
                    y = page[5][0:P, bass.ds((2 * i + b) * D, D)]
                    dve.scalar_tensor_tensor(out=y, in0=bank[3 + b][0:P, :], scalar=1.0 / SF, in1=y, op0=ALU.mult,
                                             op1=ALU.add).then_inc(t_ev, 1)


def kernel(**inputs):
    import concourse.bacc as bacc
    from concourse.bass_utils import run_bass_kernel_spmd

    v = {k: np.asarray(x) for k, x in inputs.items()}
    g = {k[7:]: x for k, x in v.items() if k.startswith("L0_gnn_")}
    f = {k[7:]: x for k, x in v.items() if k.startswith("L0_ffn_")}

    def fm(x):
        return x.reshape(-1, 128).T

    def fm4(x):
        return x.reshape(x.shape[0], -1, 128).transpose(0, 2, 1)

    cb = f["cross_in_b"]
    parts = {"b_ih": g["b_ih"], "b_hh": g["b_hh"], "gamma": g["gamma"], "beta": g["beta"], "mean": g["run_mean"],
             "var": g["run_var"], "ns_w": f["norm_s_w"], "ns_b": f["norm_s_b"], "nt_w": f["norm_t_w"],
             "nt_b": f["norm_t_b"], "cq_b": cb[0:D], "ck_b": cb[D:2 * D], "nm_w": f["norm_mlp_w"],
             "nm_b": f["norm_mlp_b"], "m1_b": f["mlp_b1"], "rb1": f["router_b1"]}
    arrays = {
        "x": v["x"],
        "src_pt": v["src"].reshape(ET, P).T,
        "dst_pt": v["dst"].reshape(ET, P).T,
        "dst_g": v["dst"].reshape(NG, GW),
        "eaT": v["edge_attr_128"].T,
        "w1T": g["W1"].T, "w2T": g["W2"].T, "wihT": g["W_ih"].T, "whhT": g["W_hh"].T,
        "spinT": f["sp_in_w"].transpose(0, 2, 1), "spoutT": f["sp_out_w"].transpose(0, 2, 1),
        "tqT": f["tq_w"].transpose(0, 2, 1), "tkT": f["tk_w"].transpose(0, 2, 1),
        "tvT": f["tv_w"].transpose(0, 2, 1), "tpT": f["tp_w"].transpose(0, 2, 1),
        "cinT": f["cross_in_w"].T, "coutT": f["cross_out_w"].T, "m1T": f["mlp_w1"].T, "m2T": f["mlp_w2"].T,
        "rw1T": f["router_w1"].T, "rw2T": f["router_w2"].T, "rb2": f["router_b2"].reshape(1, -1),
        "vec": np.concatenate([fm(parts[name]) for name in VEC], axis=1),
        "rowv": np.stack([g["b1"], g["b2"], cb[2 * D:3 * D], f["cross_out_b"], f["mlp_b2"]]),
        "vsp": np.concatenate([fm4(f["sp_in_b"][:, 0:2 * D]), fm4(f["sp_out_b"])], axis=2),
        "vtp": np.concatenate([fm4(f["tq_b"]), fm4(f["tk_b"]), fm4(f["tp_b"])], axis=2),
        "svrow": f["sp_in_b"][:, 2 * D:3 * D], "tvrow": f["tv_b"],
    }
    arrays = {k: np.ascontiguousarray(x) for k, x in arrays.items()}
    nc = bacc.Bacc("TRN2", target_bir_lowering=False, num_devices=1)
    a = {k: nc.dram_tensor("in_" + k, x.shape, mybir.dt.from_np(x.dtype), kind="ExternalInput").ap()
         for k, x in arrays.items()}
    out = nc.dram_tensor("out", (N, D), F32, kind="ExternalOutput").ap()
    nc.disable_value_cache = True
    program(nc, a, out)
    r = run_bass_kernel_spmd(nc, [{"in_" + k: x for k, x in arrays.items()}], core_ids=[0])
    return r.results[0]["out"]
```
